# Optimizing a Trainium2 kernel written in Bass

```python
import numpy as np
import jax
import jax.numpy as jnp

def _softmax(x, axis=-1):
    return jax.nn.softmax(x, axis=axis)

def _gelu(x):
    return jax.nn.gelu(x, approximate=True)

def _silu(x):
    return jax.nn.silu(x)

def _sigmoid(x):
    return jax.nn.sigmoid(x)

def _layernorm(x, axis=-1, eps=1e-05):
    m = jnp.mean(x, axis=axis, keepdims=True)
    v = jnp.var(x, axis=axis, keepdims=True)
    return (x - m) / jnp.sqrt(v + eps)

def _scatter_add(tgt, idx, src, axis=0):
    return tgt.at[idx].add(src)

def _segment_sum(src, seg, n):
    return jax.ops.segment_sum(src, seg, n)
kernel_name = 'mk_lm_tower_d2_tok_ids256_r4_20ade0'

def setup_inputs(seed: int=0):
    np.random.seed(seed)
    _w = jnp.asarray

    def _rec_inputs():
        import jax
        import jax.numpy as jnp
        _rk = jax.random.key(seed)
        x = jax.random.randint(jax.random.fold_in(_rk, 1), (2, 2048), 0, 127998, jnp.int32)
        return x
    x = _rec_inputs()

    def _L0_tok_setup():
        import jax, jax.numpy as jnp
        import numpy as np
        VOCAB = 32000
        HIDDEN = 512
        BATCH, SEQ = (4, 1024)
        key = jax.random.key(seed)
        k_ids, k_tab = jax.random.split(key)
        input_ids = jax.random.randint(k_ids, (BATCH, SEQ), 0, VOCAB, dtype=jnp.int32)
        ple_table = jax.random.normal(k_tab, (VOCAB, HIDDEN), dtype=jnp.float32)
        return {'input_ids': input_ids, 'ple_table': ple_table, 'layer_idx': 3, 'ple_dim': 64}
    _L0_tok_all = _L0_tok_setup()
    _L0_tok_in = {k: v for k, v in _L0_tok_all.items() if k in ('ple_table',)}
    del _L0_tok_all

    def _L0_attn_setup():
        import jax, jax.numpy as jnp
        import numpy as np
        SEQ_LEN = 512
        EMBED_DIM = 64
        BATCH = 8
        LN_EPS = 1e-05

        def _layernorm(x, g, b):
            mu = jnp.mean(x, axis=-1, keepdims=True)
            var = jnp.mean(jnp.square(x - mu), axis=-1, keepdims=True)
            return (x - mu) * jax.lax.rsqrt(var + LN_EPS) * g + b
        key = jax.random.key(seed)
        ks = jax.random.split(key, 8)
        C = EMBED_DIM
        x = jax.random.normal(ks[0], (BATCH, SEQ_LEN, C), dtype=jnp.float32)
        qkv_w = jax.random.normal(ks[1], (C, 3 * C), dtype=jnp.float32) * 0.02
        qkv_b = jnp.zeros((3 * C,), dtype=jnp.float32)
        proj_w = jax.random.normal(ks[2], (C, C), dtype=jnp.float32) * 0.02
        proj_b = jnp.zeros((C,), dtype=jnp.float32)
        ln1_g = jnp.ones((C,), dtype=jnp.float32)
        ln1_b = jnp.zeros((C,), dtype=jnp.float32)
        ln2_g = jnp.ones((C,), dtype=jnp.float32)
        ln2_b = jnp.zeros((C,), dtype=jnp.float32)
        bias_table = jax.random.truncated_normal(ks[3], -2.0, 2.0, (2 * SEQ_LEN - 1,), dtype=jnp.float32) * 0.02
        scale = jnp.asarray(1.0 / np.sqrt(C), dtype=jnp.float32)
        return {'x': x, 'ln1_g': ln1_g, 'ln1_b': ln1_b, 'qkv_w': qkv_w, 'qkv_b': qkv_b, 'bias_table': bias_table, 'scale': scale, 'proj_w': proj_w, 'proj_b': proj_b, 'ln2_g': ln2_g, 'ln2_b': ln2_b}
    _L0_attn_all = _L0_attn_setup()
    _L0_attn_in = {k: v for k, v in _L0_attn_all.items() if k in ('ln1_g', 'ln1_b', 'qkv_w', 'qkv_b', 'bias_table', 'scale', 'proj_w', 'proj_b', 'ln2_g', 'ln2_b')}
    del _L0_attn_all

    def _L0_ffn_setup():
        import math
        import jax, jax.numpy as jnp
        import numpy as np
        CAPACITY_FACTOR = 1.25
        key = jax.random.key(seed)
        ks = jax.random.split(key, 5)
        B, L, D, F, E = (8, 2048, 64, 256, 8)
        h = jax.random.normal(ks[0], (B, L, D), dtype=jnp.float32)
        gate_w = jax.random.normal(ks[1], (D, E), dtype=jnp.float32) * 0.02
        gate_b = jnp.zeros((E,), dtype=jnp.float32)
        w1 = jax.random.normal(ks[2], (E, D, F), dtype=jnp.float32) * (1.0 / math.sqrt(D))
        b1 = jnp.zeros((E, F), dtype=jnp.float32)
        w2 = jax.random.normal(ks[3], (E, F, D), dtype=jnp.float32) * (1.0 / math.sqrt(F))
        b2 = jnp.zeros((E, D), dtype=jnp.float32)
        return {'h': h, 'gate_w': gate_w, 'gate_b': gate_b, 'w1': w1, 'b1': b1, 'w2': w2, 'b2': b2}
    _L0_ffn_all = _L0_ffn_setup()
    _L0_ffn_in = {k: v for k, v in _L0_ffn_all.items() if k in ('gate_w', 'gate_b', 'w1', 'b1', 'w2', 'b2')}
    del _L0_ffn_all

    def _L1_attn_setup():
        import jax, jax.numpy as jnp
        import numpy as np
        B, L, D = (4, 1024, 64)
        key = jax.random.key(seed)
        kx, kq, kk, kv, ko = jax.random.split(key, 5)
        std = 0.02
        return {'x': jax.random.normal(kx, (B, L, D), dtype=jnp.float32), 'Wq': std * jax.random.normal(kq, (D, D), dtype=jnp.float32), 'Wk': std * jax.random.normal(kk, (D, D), dtype=jnp.float32), 'Wv': std * jax.random.normal(kv, (D, D), dtype=jnp.float32), 'Wo': std * jax.random.normal(ko, (D, D), dtype=jnp.float32)}
    _L1_attn_all = _L1_attn_setup()
    _L1_attn_in = {k: v for k, v in _L1_attn_all.items() if k in ('Wq', 'Wk', 'Wv', 'Wo')}
    del _L1_attn_all

    def _L1_ffn_setup():
        import jax, jax.numpy as jnp
        import numpy as np
        DIM = 64
        HEADS = 8
        NUM_KEYS = 64
        NUM_KV = NUM_KEYS ** 2
        PK_TOPK = 16
        FINAL_TOPK = 16
        DIM_KEY = DIM // 2
        P = 2

        def _pk(x, Wq_pk, pk_keys):
            b, n, _ = x.shape
            q = (x @ Wq_pk).reshape(b, n, P, HEADS, DIM_KEY).transpose(2, 0, 1, 3, 4)
            sim = jnp.einsum('pbnhd,pkhd->pbnhk', q, pk_keys)
            scores, idx = jax.lax.top_k(sim, PK_TOPK)
            idx0 = idx[0]
            idx1 = idx[1] * NUM_KEYS
            index = (idx0[..., :, None] + idx1[..., None, :]).reshape(b, n, HEADS, PK_TOPK * PK_TOPK)
            score = (scores[0][..., :, None] + scores[1][..., None, :]).reshape(b, n, HEADS, PK_TOPK * PK_TOPK)
            final_scores, pk_idx = jax.lax.top_k(score, FINAL_TOPK)
            final_indices = jnp.take_along_axis(index, pk_idx, axis=-1)
            final_scores = jax.nn.softmax(final_scores, axis=-1)
            return (final_scores, final_indices)
        key = jax.random.key(seed)
        ks = jax.random.split(key, 7)
        b, n = (2, 256)
        std = 0.02
        x = jax.random.normal(ks[0], (b, n, DIM), dtype=jnp.float32)
        Wq_pk = jax.random.normal(ks[1], (DIM, P * HEADS * DIM_KEY), dtype=jnp.float32) * std
        pk_keys = jax.random.normal(ks[2], (P, NUM_KEYS, HEADS, DIM_KEY), dtype=jnp.float32) * std
        Wq = jax.random.normal(ks[3], (DIM, HEADS * DIM), dtype=jnp.float32) * std
        keys_table = jax.random.normal(ks[4], (NUM_KV * HEADS, DIM), dtype=jnp.float32) * std
        values_table = jax.random.normal(ks[5], (NUM_KV * HEADS, DIM), dtype=jnp.float32) * std
        Wo = jax.random.normal(ks[6], (DIM * HEADS, DIM), dtype=jnp.float32) * std
        return {'x': x, 'Wq_pk': Wq_pk, 'pk_keys': pk_keys, 'Wq': Wq, 'keys_table': keys_table, 'values_table': values_table, 'Wo': Wo}
    _L1_ffn_all = _L1_ffn_setup()
    _L1_ffn_in = {k: v for k, v in _L1_ffn_all.items() if k in ('Wq_pk', 'pk_keys', 'Wq', 'keys_table', 'values_table', 'Wo')}
    del _L1_ffn_all
    return {'x': x, 'L0_tok_ple_table': _L0_tok_in['ple_table'], 'L0_attn_ln1_g': _L0_attn_in['ln1_g'], 'L0_attn_ln1_b': _L0_attn_in['ln1_b'], 'L0_attn_qkv_w': _L0_attn_in['qkv_w'], 'L0_attn_qkv_b': _L0_attn_in['qkv_b'], 'L0_attn_bias_table': _L0_attn_in['bias_table'], 'L0_attn_scale': _L0_attn_in['scale'], 'L0_attn_proj_w': _L0_attn_in['proj_w'], 'L0_attn_proj_b': _L0_attn_in['proj_b'], 'L0_attn_ln2_g': _L0_attn_in['ln2_g'], 'L0_attn_ln2_b': _L0_attn_in['ln2_b'], 'L0_ffn_gate_w': _L0_ffn_in['gate_w'], 'L0_ffn_gate_b': _L0_ffn_in['gate_b'], 'L0_ffn_w1': _L0_ffn_in['w1'], 'L0_ffn_b1': _L0_ffn_in['b1'], 'L0_ffn_w2': _L0_ffn_in['w2'], 'L0_ffn_b2': _L0_ffn_in['b2'], 'L1_attn_Wq': _L1_attn_in['Wq'], 'L1_attn_Wk': _L1_attn_in['Wk'], 'L1_attn_Wv': _L1_attn_in['Wv'], 'L1_attn_Wo': _L1_attn_in['Wo'], 'L1_ffn_Wq_pk': _L1_ffn_in['Wq_pk'], 'L1_ffn_pk_keys': _L1_ffn_in['pk_keys'], 'L1_ffn_Wq': _L1_ffn_in['Wq'], 'L1_ffn_keys_table': _L1_ffn_in['keys_table'], 'L1_ffn_values_table': _L1_ffn_in['values_table'], 'L1_ffn_Wo': _L1_ffn_in['Wo']}

def reference(x, L0_tok_ple_table, L0_attn_ln1_g, L0_attn_ln1_b, L0_attn_qkv_w, L0_attn_qkv_b, L0_attn_bias_table, L0_attn_scale, L0_attn_proj_w, L0_attn_proj_b, L0_attn_ln2_g, L0_attn_ln2_b, L0_ffn_gate_w, L0_ffn_gate_b, L0_ffn_w1, L0_ffn_b1, L0_ffn_w2, L0_ffn_b2, L1_attn_Wq, L1_attn_Wk, L1_attn_Wv, L1_attn_Wo, L1_ffn_Wq_pk, L1_ffn_pk_keys, L1_ffn_Wq, L1_ffn_keys_table, L1_ffn_values_table, L1_ffn_Wo):
    import jax
    import jax.numpy as jnp

    def _L0_tok_ref(input_ids, ple_table, layer_idx, ple_dim):
        import jax, jax.numpy as jnp
        import numpy as np
        VOCAB = 32000
        HIDDEN = 512
        BATCH, SEQ = (4, 1024)
        start = layer_idx * ple_dim
        layer_slice = jax.lax.dynamic_slice_in_dim(ple_table, start, ple_dim, axis=1)
        return layer_slice[input_ids].astype(jnp.float32)

    def _L0_attn_ref(x, ln1_g, ln1_b, qkv_w, qkv_b, bias_table, scale, proj_w, proj_b, ln2_g, ln2_b):
        import jax, jax.numpy as jnp
        import numpy as np
        SEQ_LEN = 512
        EMBED_DIM = 64
        BATCH = 8
        LN_EPS = 1e-05

        def _layernorm(x, g, b):
            mu = jnp.mean(x, axis=-1, keepdims=True)
            var = jnp.mean(jnp.square(x - mu), axis=-1, keepdims=True)
            return (x - mu) * jax.lax.rsqrt(var + LN_EPS) * g + b
        B, N, C = x.shape
        h = _layernorm(x, ln1_g, ln1_b)
        qkv = h @ qkv_w + qkv_b
        q, k, v = jnp.split(qkv, 3, axis=-1)
        coords = jnp.arange(N)
        rel_idx = coords[None, :] - coords[:, None] + (N - 1)
        rel_bias = bias_table[rel_idx]
        attn = jnp.einsum('bnc,bmc->bnm', q, k) + rel_bias
        attn = jax.nn.softmax(attn, axis=-1) * scale
        out = jnp.einsum('bnm,bmc->bnc', attn, v)
        out = out @ proj_w + proj_b
        out = _layernorm(out, ln2_g, ln2_b)
        return out

    def _L0_ffn_ref(h, gate_w, gate_b, w1, b1, w2, b2):
        import math
        import jax, jax.numpy as jnp
        import numpy as np
        CAPACITY_FACTOR = 1.25
        B, L, D = h.shape
        E = gate_w.shape[1]
        T = B * L
        C = max(1, math.ceil(CAPACITY_FACTOR * T / E))
        x = h.reshape(T, D)
        logits = x @ gate_w + gate_b
        probs = jax.nn.softmax(logits, axis=-1)
        idx = jnp.argmax(probs, axis=-1)
        prb = jnp.take_along_axis(probs, idx[:, None], axis=1)[:, 0]
        one_hot = jax.nn.one_hot(idx, E, dtype=jnp.float32)
        pos = (jnp.cumsum(one_hot, axis=0) * one_hot).sum(-1).astype(jnp.int32) - 1
        kept = pos < C
        pos_safe = jnp.where(kept, pos, C)
        buf = jnp.zeros((E, C, D), dtype=h.dtype).at[idx, pos_safe].set(x, mode='drop')
        hmid = jax.nn.relu(jnp.einsum('ecd,edf->ecf', buf, w1) + b1[:, None, :])
        ybuf = jnp.einsum('ecf,efd->ecd', hmid, w2) + b2[:, None, :]
        pos_g = jnp.minimum(pos, C - 1)
        y_tok = ybuf[idx, pos_g] * (prb * kept)[:, None]
        y = y_tok.reshape(B, L, D)
        y = jnp.nan_to_num(y, nan=0.0, posinf=10000.0, neginf=-10000.0)
        return y

    def _L1_attn_ref(x, Wq, Wk, Wv, Wo):
        import jax, jax.numpy as jnp
        import numpy as np
        B, L, D = (4, 1024, 64)
        q = x @ Wq.T
        k = x @ Wk.T
        v = x @ Wv.T
        logits = jnp.einsum('bld,bmd->blm', q, k)
        Lq = x.shape[1]
        causal_mask = jnp.triu(jnp.ones((Lq, Lq), dtype=bool), k=1)
        logits = jnp.where(causal_mask[None], jnp.asarray(0.0, logits.dtype), logits)
        attn = jax.nn.relu(logits)
        row_counts = jnp.maximum(jnp.arange(Lq, dtype=attn.dtype), 1.0)
        attn = attn / row_counts[None, :, None]
        ctx = jnp.einsum('blm,bmd->bld', attn, v)
        return ctx @ Wo.T

    def _L1_ffn_ref(x, Wq_pk, pk_keys, Wq, keys_table, values_table, Wo):
        import jax, jax.numpy as jnp
        import numpy as np
        DIM = 64
        HEADS = 8
        NUM_KEYS = 64
        NUM_KV = NUM_KEYS ** 2
        PK_TOPK = 16
        FINAL_TOPK = 16
        DIM_KEY = DIM // 2
        P = 2

        def _pk(x, Wq_pk, pk_keys):
            b, n, _ = x.shape
            q = (x @ Wq_pk).reshape(b, n, P, HEADS, DIM_KEY).transpose(2, 0, 1, 3, 4)
            sim = jnp.einsum('pbnhd,pkhd->pbnhk', q, pk_keys)
            scores, idx = jax.lax.top_k(sim, PK_TOPK)
            idx0 = idx[0]
            idx1 = idx[1] * NUM_KEYS
            index = (idx0[..., :, None] + idx1[..., None, :]).reshape(b, n, HEADS, PK_TOPK * PK_TOPK)
            score = (scores[0][..., :, None] + scores[1][..., None, :]).reshape(b, n, HEADS, PK_TOPK * PK_TOPK)
            final_scores, pk_idx = jax.lax.top_k(score, FINAL_TOPK)
            final_indices = jnp.take_along_axis(index, pk_idx, axis=-1)
            final_scores = jax.nn.softmax(final_scores, axis=-1)
            return (final_scores, final_indices)
        b, n, d = x.shape
        q = (x @ Wq).reshape(b, n, HEADS, DIM) * DIM ** (-0.5)
        kv_scores, indices = _pk(x, Wq_pk, pk_keys)
        offsets = jnp.arange(HEADS, dtype=indices.dtype) * NUM_KV
        ind = indices + offsets[None, None, :, None]
        k = jnp.einsum('bnhk,bnhkd->bnhd', kv_scores, keys_table[ind])
        v = jnp.einsum('bnhk,bnhkd->bnhd', kv_scores, values_table[ind])
        sim = jnp.einsum('bihd,bjhd->bhij', q, k)
        neg = -jnp.finfo(sim.dtype).max
        causal = jnp.tril(jnp.ones((n, n), dtype=bool))
        sim = jnp.where(causal, sim, neg)
        attn = jax.nn.softmax(sim, axis=-1)
        out = jnp.einsum('bhij,bjhd->bhid', attn, v)
        out = out.transpose(0, 2, 1, 3).reshape(b, n, HEADS * DIM)
        return out @ Wo
    h = _L0_tok_ref(x, L0_tok_ple_table, 3, 64)
    h = h + _L0_attn_ref(_layernorm(h, axis=-1), L0_attn_ln1_g, L0_attn_ln1_b, L0_attn_qkv_w, L0_attn_qkv_b, L0_attn_bias_table, L0_attn_scale, L0_attn_proj_w, L0_attn_proj_b, L0_attn_ln2_g, L0_attn_ln2_b)
    h = h + _L0_ffn_ref(_layernorm(h, axis=-1), L0_ffn_gate_w, L0_ffn_gate_b, L0_ffn_w1, L0_ffn_b1, L0_ffn_w2, L0_ffn_b2)
    h = h + _L1_attn_ref(_layernorm(h, axis=-1), L1_attn_Wq, L1_attn_Wk, L1_attn_Wv, L1_attn_Wo)
    h = h + _L1_ffn_ref(_layernorm(h, axis=-1), L1_ffn_Wq_pk, L1_ffn_pk_keys, L1_ffn_Wq, L1_ffn_keys_table, L1_ffn_values_table, L1_ffn_Wo)
    return h

_drawn_inputs = setup_inputs


def setup_inputs(seed=0):
    import zlib

    import numpy as np

    out = dict(_drawn_inputs(seed))
    spreads = {'L0_attn_ln1_g': (1.0, 0.6),
     'L0_attn_ln1_b': (0.0, 0.8),
     'L0_attn_qkv_b': (0.0, 0.468),
     'L0_attn_proj_b': (0.0, 0.1),
     'L0_attn_ln2_g': (1.0, 0.2),
     'L0_attn_ln2_b': (0.0, 0.1),
     'L0_ffn_gate_b': (0.0, 0.1),
     'L0_ffn_b1': (0.0, 0.8),
     'L0_ffn_b2': (0.0, 0.8)}
    factors = {'L0_attn_qkv_w': 3.136,
     'L0_attn_bias_table': 64.0,
     'L1_attn_Wq': 8.0,
     'L1_attn_Wk': 8.0,
     'L1_attn_Wv': 8.0,
     'L1_attn_Wo': 8.0,
     'L1_ffn_Wq_pk': 8.0,
     'L1_ffn_pk_keys': 8.0,
     'L1_ffn_Wq': 64.0,
     'L1_ffn_keys_table': 64.0,
     'L1_ffn_values_table': 8.0,
     'L1_ffn_Wo': 8.0}
    for name, (base, spread) in spreads.items():
        noise = np.random.default_rng([zlib.crc32(name.encode()), seed]).standard_normal(out[name].shape)
        drawn = base * np.exp(spread * noise) if base else spread * noise
        out[name] = jnp.asarray(drawn.astype(out[name].dtype))
    for name, factor in factors.items():
        out[name] = (out[name] * factor).astype(out[name].dtype)
    return out
```

```python
from contextlib import ExitStack

import concourse.bass as bass
from concourse import mybir

ALU = mybir.AluOpType
ACT = mybir.ActivationFunctionType
AX = mybir.AxisListType
F32 = mybir.dt.float32
BF16 = mybir.dt.bfloat16
I32 = mybir.dt.int32
U32 = mybir.dt.uint32

P = 128
D = 64
B, N = 2, 2048
TILES = B * N // P
BT = N // P
CH = 512
NCH = N // CH
VOCAB, PLE = 32000, 512
PLE_START = 3 * 64
EPS = 1e-5
E, F = 8, 256
CAP = 5 * B * N // (4 * E)
HEADS, NK, TOPK = 8, 64, 16
REACH = N - P
WIDE = REACH + N
FAR = -1e30
LOWEST = -3.0e38

PAIRS = [(0, 1, 16), (1, 1, 8), (2, 2, 5), (4, 4, 3), (8, 8, 1)]
NC = sum(na * nb for _, na, nb in PAIRS)


def bcast(ap, axis, shape):
    return ap.unsqueeze(axis).to_broadcast(shape)


class Link:

    def __init__(self, eng, sem):
        self.eng, self.sem, self.n = eng, sem, 0

    def __call__(self, ins):
        self.mark(ins)
        self.wait()

    def mark(self, ins):
        self.n += 1
        ins.then_inc(self.sem, 1)

    def wait(self):
        self.eng.wait_ge(self.sem, self.n)

    def restart(self):
        self.eng.wait_ge(self.sem, self.n)
        self.eng.sem_clear(self.sem)
        self.n = 0


def hold(eng, started, sem, value):
    value = eng.to_reg(value)
    eng.wait_ge(started, 1)
    eng.wait_ge(sem, value)


def layer_norm(nc, dve, link, src, dst, sq, st, s_var, s_std, n, affine=None):
    full = [P, TILES, D]
    link(nc.vector.tensor_reduce(st[:, 0, :], src, AX.X, ALU.add))
    link(nc.vector.tensor_scalar(st[:, 0, :], st[:, 0, :], 1.0 / D, None, ALU.mult))
    link(nc.vector.tensor_tensor(dst, src, bcast(st[:, 0, :], 2, full), ALU.subtract))
    link(nc.vector.tensor_tensor(sq, dst, dst, ALU.mult))
    link(nc.vector.tensor_reduce(st[:, 1, :], sq, AX.X, ALU.add))
    nc.vector.tensor_scalar(st[:, 1, :], st[:, 1, :], 1.0 / D, EPS, ALU.mult, ALU.add).then_inc(s_var, 1)
    dve.wait_ge(s_std, n)
    link(nc.vector.reciprocal(st[:, 3, :], st[:, 2, :]))
    link(nc.vector.tensor_tensor(dst, dst, bcast(st[:, 3, :], 2, full), ALU.mult))
    if affine:
        gain, shift = affine
        link(nc.vector.tensor_tensor(dst, dst, bcast(gain, 1, full), ALU.mult))
        link(nc.vector.tensor_tensor(dst, dst, bcast(shift, 1, full), ALU.add))


def root(nc, act, st, s_var, s_std, n):
    act.wait_ge(s_var, n)
    nc.scalar.activation(st[:, 2, :], st[:, 1, :], ACT.Sqrt).then_inc(s_std, 1)


def build(nc, A, out):
    with ExitStack() as whole:
        def sb(name, shape, dt=F32, ctx=whole):
            return ctx.enter_context(nc.sbuf_tensor(name, shape, dt))

        def ps(name, shape, dt=F32, ctx=whole):
            return ctx.enter_context(nc.psum_tensor(name, shape, dt))

        def sem(name, ctx=whole):
            return ctx.enter_context(nc.semaphore(name))

        h = sb("h", [P, TILES, D])
        xn = sb("xn", [P, TILES, D])
        xT = sb("xT", [D, TILES * P])
        st = sb("st", [P, 4, TILES])
        ident = sb("ident", [P, P])
        ident16 = sb("ident16", [P, P], BF16)
        causal = sb("causal", [P, WIDE], BF16)
        rc = sb("rc", [P, BT])
        s_started = sem("s_started")

        def transposed(phase, pe, act, tp, s_norm, s_tr, s_cp):
            def on_pe():
                pe.wait_ge(s_norm, 1)
                for g in range(TILES // 4):
                    if g >= 2:
                        pe.wait_ge(s_cp, g - 1)
                    for k in range(4):
                        last = nc.tensor.transpose(tp[g % 2][0:D, k * P:(k + 1) * P], xn[:, 4 * g + k, :], ident[:, :])
                    last.then_inc(s_tr, 1)

            def on_act():
                for g in range(TILES // 4):
                    act.wait_ge(s_tr, g + 1)
                    nc.scalar.activation(xT[:, g * CH:(g + 1) * CH], tp[g % 2][0:D, :], ACT.Copy).then_inc(s_cp, 1)
            return on_pe if phase == "pe" else on_act

        with ExitStack() as c:
            ids = sb("ids", [P, TILES], I32, c)
            idf = sb("idf", [P, TILES], F32, c)
            wrap = sb("wrap", [P, TILES], F32, c)
            rows = sb("rows", [P, TILES], U32, c)
            rci = sb("rci", [P, BT], I32, c)
            s_ids, s_rows, s_link, s_tok, s_iota, s_fill = (sem(n, c) for n in (
                "s_ids", "s_rows", "s_link0", "s_tok", "s_iota", "s_fill"))
            block = c.enter_context(nc.Block())

            @block.sync
            def _(sp):
                sp.dma_start(ids[:, :], A["ids"]).then_inc(s_ids, 16)

            @block.vector
            def _(dve):
                link = Link(dve, s_link)
                dve.wait_ge(s_ids, 16)
                link(nc.vector.tensor_copy(idf[:, :], ids[:, :]))
                link(nc.vector.tensor_scalar(wrap[:, :], idf[:, :], 0.0, float(VOCAB), ALU.is_lt, ALU.mult))
                link(nc.vector.tensor_tensor(idf[:, :], idf[:, :], wrap[:, :], ALU.add))
                link(nc.vector.tensor_scalar(idf[:, :], idf[:, :], 0.0, float(VOCAB - 1), ALU.max, ALU.min))
                nc.vector.tensor_scalar(rows[:, :], idf[:, :], float(PLE // D), float(PLE_START // D),
                                        ALU.mult, ALU.add).then_inc(s_rows, 1)
                dve.wait_ge(s_iota, 1)
                link(nc.vector.tensor_scalar(rc[:, :], rci[:, :], 1.0, None, ALU.max))
                link(nc.vector.reciprocal(rc[:, :], rc[:, :]))

            @block.gpsimd
            def _(pool):
                nc.gpsimd.iota(rci[:, :], [[P, BT]], base=0, channel_multiplier=1).then_inc(s_iota, 1)
                nc.gpsimd.memset(ident[:, :], 0.0).then_inc(s_fill, 1)
                nc.gpsimd.memset(ident16[:, :], 0.0).then_inc(s_fill, 1)
                nc.gpsimd.memset(causal[:, :], 0.0).then_inc(s_fill, 1)
                pool.wait_ge(s_fill, 3)
                nc.gpsimd.affine_select(out=ident[:, :], in_=ident[:, :], compare_op=ALU.not_equal, fill=1.0,
                                        base=0, pattern=[[-1, P]], channel_multiplier=1)
                nc.gpsimd.affine_select(out=ident16[:, :], in_=ident16[:, :], compare_op=ALU.not_equal, fill=1.0,
                                        base=0, pattern=[[-1, P]], channel_multiplier=1)
                nc.gpsimd.affine_select(out=causal[:, :], in_=causal[:, :], compare_op=ALU.is_ge, fill=FAR,
                                        base=REACH, pattern=[[-1, WIDE]], channel_multiplier=1).then_inc(s_started, 1)
                pool.wait_ge(s_rows, 1)
                for t in range(TILES):
                    pool.indirect_dma_start(h[:, t, :], None, A["ple"],
                                            bass.IndirectOffsetOnAxis(ap=rows[:, t:t + 1], axis=0)).then_inc(s_tok, 16)
                pool.wait_ge(s_tok, 16 * TILES)

        def dense_attention(name, biased, c, load, qk_w, v_w, proj_w, qk_bias, v_bias, proj_bias, table, scale,
                            dest, accumulate):
            qT = sb(name + "qT", [D, B * N], F32, c)
            kT = sb(name + "kT", [D, B * N], F32, c)
            v = sb(name + "v", [P, TILES, D], F32, c)
            qs = [sb(f"{name}qs{k}", [D, P], F32, c) for k in range(2)]
            prob = [sb(f"{name}prob{k}", [P, N], F32, c) for k in range(2)]
            probT = sb(name + "probT", [P, N], F32, c)
            biased_s = sb(name + "bs", [P, N], F32, c) if biased else None
            nmax = [sb(f"{name}nmax{k}", [P, 1], F32, c) for k in range(2)]
            rsum = [sb(f"{name}rsum{k}", [P, 1], F32, c) for k in range(2)]
            rinv = [sb(f"{name}rinv{k}", [P, 2], F32, c) for k in range(2)]
            ob = sb(name + "ob", [P, D], F32, c)
            obT = sb(name + "obT", [D, P], F32, c)
            S = ps(name + "S", [P, N], F32, c)
            tp = [ps(f"{name}tp{k}", [P, CH], F32, c) for k in range(2)]
            mix = [ps(f"{name}mix{k}", [P, CH], F32, c) for k in range(2)]
            O, OT, PR = mix[0][:, 0:D], mix[0][0:D, P:2 * P], mix[1][:, 0:D]

            with ExitStack() as cc:
                s_w, s_qk, s_qkc, s_v, s_vc = (sem(name + n, cc) for n in ("s_w", "s_qk", "s_qkc", "s_v", "s_vc"))
                block = cc.enter_context(nc.Block())
                nload = load and len(load)

                @block.sync
                def _(sp):
                    for dst, src in load:
                        sp.dma_start(dst, src).then_inc(s_w, 16)
                    sp.wait_ge(s_w, 16 * nload)

                @block.tensor
                def _(pe):
                    pe.wait_ge(s_w, 16 * nload)
                    for g in range(TILES * P // CH):
                        if g >= 2:
                            pe.wait_ge(s_qkc, 2 * (g - 1))
                        nc.tensor.matmul(tp[g % 2][:, :], qk_w, xT[:, g * CH:(g + 1) * CH],
                                         start=True, stop=True).then_inc(s_qk, 1)
                    for g in range(TILES // 8):
                        for k in range(8):
                            last = nc.tensor.matmul(S[:, g * CH + k * D:g * CH + (k + 1) * D],
                                                    xT[:, (8 * g + k) * P:(8 * g + k + 1) * P], v_w,
                                                    start=True, stop=True)
                        last.then_inc(s_v, 1)

                @block.scalar
                def _(act):
                    for g in range(TILES * P // CH):
                        act.wait_ge(s_qk, g + 1)
                        for k, dst in ((0, qT), (1, kT)):
                            src = tp[g % 2][k * D:(k + 1) * D, :]
                            to = dst[:, g * CH:(g + 1) * CH]
                            if qk_bias is None:
                                nc.scalar.activation(to, src, ACT.Copy).then_inc(s_qkc, 1)
                            else:
                                nc.scalar.activation(to, src, ACT.Identity, bias=qk_bias[:, k:k + 1]).then_inc(s_qkc, 1)

                @block.vector
                def _(dve):
                    for g in range(TILES // 8):
                        dve.wait_ge(s_v, g + 1)
                        src = S[:, g * CH:(g + 1) * CH].rearrange("p (k d) -> p k d", d=D)
                        to = v[:, 8 * g:8 * g + 8, :]
                        if v_bias is None:
                            nc.vector.tensor_copy(to, src).then_inc(s_vc, 1)
                        else:
                            nc.vector.tensor_tensor(to, src, bcast(v_bias, 1, [P, 8, D]), ALU.add).then_inc(s_vc, 1)

            with ExitStack() as cc:
                names = "s_qs s_scores s_read s_max s_prob s_tp s_tpc s_o s_ob s_obt s_obs s_proj s_link s_done"
                (s_qs, s_scores, s_read, s_max, s_prob, s_tp, s_tpc, s_o, s_ob, s_obt, s_obs, s_proj, s_link,
                 s_done) = (sem(name + n, cc) for n in names.split())
                block = cc.enter_context(nc.Block())

                def place(j, k):
                    return (2 * j + k) * P, j // (BT // 2) * N, j % (BT // 2) * 2 + k

                @block.scalar
                def _(act):
                    nc.scalar.preload_act_table(ACT.Exp)

                    def stage(j, k):
                        nc.scalar.activation(qs[k % 2][:, :], qT[:, bass.ds(place(j, k)[0], P)], ACT.Copy).then_inc(s_qs, 1)

                    def weights(j, k):
                        i = 2 * j + k
                        if biased:
                            act.wait_ge(s_max, i + 1)
                            nc.scalar.activation(prob[k % 2][:, :], biased_s[:, :], ACT.Exp, bias=nmax[k % 2][:, :],
                                                 accum_out=rsum[k % 2][:, :]).then_inc(s_prob, 1)
                        else:
                            act.wait_ge(s_scores, i + 1)
                            nc.scalar.activation(prob[k % 2][:, :], S[:, :], ACT.Relu).then_inc(s_prob, 1)

                    def item(j, k, ahead):
                        i = 2 * j + k
                        if ahead:
                            stage(j + (k + 1) // 2, (k + 1) % 2)
                        for q in range(NCH):
                            act.wait_ge(s_tp, NCH * i + q + 1)
                            nc.scalar.activation(probT[:, q * CH:(q + 1) * CH], tp[q % 2][:, :], ACT.Copy).then_inc(s_tpc, 1)
                        act.wait_ge(s_obt, i + 1)
                        nc.scalar.activation(obT[:, :], OT, ACT.Copy).then_inc(s_obs, 1)
                        if ahead:
                            weights(j + (k + 1) // 2, (k + 1) % 2)

                    stage(0, 0)
                    weights(0, 0)
                    with act.Fori(0, TILES // 2 - 1) as j:
                        item(j, 0, True)
                        item(j, 1, True)
                    item(TILES // 2 - 1, 0, True)
                    item(TILES // 2 - 1, 1, False)

                @block.tensor
                def _(pe):
                    def scores(j, k, wait_read):
                        i = 2 * j + k
                        _, first, tb = place(j, k)
                        pe.wait_ge(s_qs, i + 1)
                        if wait_read:
                            pe.wait_ge(s_read if biased else s_prob, i)
                        for q in range(NCH):
                            last = nc.tensor.matmul(S[:, q * CH:(q + 1) * CH], qs[k % 2][:, :],
                                                    kT[:, bass.ds(first + q * CH, CH)], start=True, stop=biased)
                            if not biased:
                                last = nc.tensor.matmul(S[:, q * CH:(q + 1) * CH], ident16[:, :],
                                                        causal[:, bass.ds(REACH - tb * P + q * CH, CH)],
                                                        start=False, stop=True)
                        last.then_inc(s_scores, 1)

                    def item(j, k, ahead):
                        i = 2 * j + k
                        _, first, tb = place(j, k)
                        batch = j // (BT // 2) * BT
                        if ahead:
                            scores(j + (k + 1) // 2, (k + 1) % 2, True)
                        pe.wait_ge(s_prob, i + 1)
                        for q in range(NCH):
                            if q >= 2:
                                pe.wait_ge(s_tpc, NCH * i + q - 1)
                            for m in range(4):
                                last = nc.tensor.transpose(tp[q % 2][:, m * P:(m + 1) * P],
                                                           prob[k % 2][:, (4 * q + m) * P:(4 * q + m + 1) * P], ident[:, :])
                            last.then_inc(s_tp, 1)
                        for m in range(BT):
                            if m % 4 == 0:
                                pe.wait_ge(s_tpc, NCH * i + m // 4 + 1)
                            last = nc.tensor.matmul(O, probT[:, m * P:(m + 1) * P],
                                                    v[:, bass.ds(batch + m, 1), :].rearrange("p a d -> p (a d)"),
                                                    start=(m == 0), stop=(m == BT - 1))
                        last.then_inc(s_o, 1)
                        hold(pe, s_started, s_ob, i + 1)
                        nc.tensor.transpose(OT, ob[:, :], ident[:, :]).then_inc(s_obt, 1)
                        pe.wait_ge(s_obs, i + 1)
                        nc.tensor.matmul(PR, obT[:, :], proj_w, start=True, stop=True).then_inc(s_proj, 1)

                    scores(0, 0, False)
                    with pe.Fori(0, TILES // 2 - 1) as j:
                        item(j, 0, True)
                        item(j, 1, True)
                    item(TILES // 2 - 1, 0, True)
                    item(TILES // 2 - 1, 1, False)

                @block.vector
                def _(dve):
                    link = Link(dve, s_link)

                    def soften(j, k):
                        i = 2 * j + k
                        tb = place(j, k)[2]
                        dve.wait_ge(s_scores, i + 1)
                        nc.vector.tensor_tensor(biased_s[:, :], S[:, :], table[:, bass.ds(REACH - tb * P, N)],
                                                ALU.add).then_inc(s_read, 1)
                        dve.wait_ge(s_read, i + 1)
                        nc.vector.tensor_reduce(nmax[k % 2][:, :], biased_s[:, :], AX.X, ALU.max,
                                                negate=True).then_inc(s_max, 1)

                    def item(j, k, ahead):
                        i = 2 * j + k
                        tb = place(j, k)[2]
                        if biased:
                            dve.wait_ge(s_prob, i + 1)
                            link(nc.vector.reciprocal(rinv[k % 2][:, 0:1], rsum[k % 2][:, :]))
                            link(nc.vector.tensor_tensor(rinv[k % 2][:, 1:2], rinv[k % 2][:, 0:1], scale, ALU.mult))
                            if ahead:
                                soften(j + (k + 1) // 2, (k + 1) % 2)
                        dve.wait_ge(s_o, i + 1)
                        by = rinv[k % 2][:, 1:2] if biased else rc[:, bass.ds(tb, 1)]
                        nc.vector.tensor_scalar(ob[:, :], O, by, None, ALU.mult).then_inc(s_ob, 1)
                        dve.wait_ge(s_proj, i + 1)
                        to = dest[:, bass.ds(i, 1), :].rearrange("p a d -> p (a d)")
                        nc.vector.tensor_tensor(to, PR, to if accumulate else proj_bias, ALU.add).then_inc(s_done, 1)

                    if biased:
                        soften(0, 0)
                    with dve.Fori(0, TILES // 2 - 1) as j:
                        item(j, 0, True)
                        item(j, 1, True)
                        link.restart() if biased else None
                    item(TILES // 2 - 1, 0, True)
                    item(TILES // 2 - 1, 1, False)

        def norm_block(name, c, src, affines, dst=None, add_to=None, load=(), transpose=True):
            sq = sb(name + "sq", [P, TILES, D], F32, c)
            tp = [ps(f"{name}tp{k}", [P, CH], F32, c) for k in range(2)]
            s_w, s_var, s_std, s_norm, s_tr, s_cp, s_link = (sem(name + n, c) for n in (
                "s_w", "s_var", "s_std", "s_norm", "s_tr", "s_cp", "s_link"))
            block = c.enter_context(nc.Block())
            if load:
                @block.sync
                def _(sp):
                    for to, frm in load:
                        sp.dma_start(to, frm).then_inc(s_w, 16)

            @block.vector
            def _(dve):
                link = Link(dve, s_link)
                if load:
                    dve.wait_ge(s_w, 16 * len(load))
                at = src
                for n, affine in enumerate(affines):
                    layer_norm(nc, dve, link, at, xn[:, :, :], sq[:, :, :], st, s_var, s_std, n + 1, affine)
                    at = xn[:, :, :]
                if add_to is not None:
                    link(nc.vector.tensor_tensor(add_to, add_to, xn[:, :, :], ALU.add))
                nc.vector.memset(sq[:, 0, 0:1], 0.0).then_inc(s_norm, 1)

            @block.scalar
            def _(act):
                for n in range(len(affines)):
                    root(nc, act, st, s_var, s_std, n + 1)
                if transpose:
                    transposed("act", None, act, tp, s_norm, s_tr, s_cp)()

            if transpose:
                @block.tensor
                def _(pe):
                    transposed("pe", pe, None, tp, s_norm, s_tr, s_cp)()

        with ExitStack() as l0:
            LX = 1152
            table = sb("table", [P, WIDE], F32, l0)
            vecs = sb("vecs", [P, 6, D], F32, l0)
            scale = sb("scale", [P, 1], F32, l0)
            qkb = sb("qkb", [D, 3], F32, l0)
            w0 = sb("w0", [D, 3 * D], F32, l0)
            wp = sb("wp", [D, D], F32, l0)
            ao = sb("ao", [P, TILES, D], F32, l0)
            shear = nc.dram_tensor("shear", (P * LX,), F32, kind="Internal").ap()
            with ExitStack() as c:
                line = sb("line", [P, LX], F32, c)
                s_line, s_long, s_out, s_back, s_fill = (sem(n, c) for n in (
                    "s_line", "s_long", "s_sheared", "s_back", "s_tabled"))
                block = c.enter_context(nc.Block())
                known = A["L0_attn_bias_table"].shape[0]

                @block.sync
                def _(sp):
                    sp.dma_start(line[:, 0:known], A["L0_attn_bias_table"].partition_broadcast(P)).then_inc(s_line, 16)
                    sp.wait_ge(s_long, 1)
                    sp.dma_start(shear.rearrange("(p n) -> p n", n=LX), line[:, :]).then_inc(s_out, 16)
                    sp.wait_ge(s_out, 16)
                    sp.dma_start(table[:, 0:1024], shear[0:P * (LX - 1)].rearrange("(p n) -> p n", n=LX - 1)[:, P - 1:P - 1 + 1024]
                                 ).then_inc(s_back, 16)

                @block.vector
                def _(dve):
                    dve.wait_ge(s_line, 16)
                    nc.vector.tensor_copy(line[:, known:LX], line[:, known - 1:known].to_broadcast([P, LX - known])).then_inc(s_long, 1)
                    dve.wait_ge(s_back, 16)
                    nc.vector.tensor_copy(table[:, 1024:WIDE], table[:, 1023:1024].to_broadcast([P, WIDE - 1024])).then_inc(s_fill, 1)

            with ExitStack() as c:
                row = lambda n: A[n].partition_broadcast(P)
                norm_block("n0", c, h[:, :, :], [None, (vecs[:, 0, :], vecs[:, 1, :])], load=[
                    (vecs[:, 0, :], row("L0_attn_ln1_g")), (vecs[:, 1, :], row("L0_attn_ln1_b")),
                    (vecs[:, 2, :], A["L0_attn_qkv_b"][2 * D:3 * D].partition_broadcast(P)),
                    (vecs[:, 3, :], row("L0_attn_proj_b")),
                    (vecs[:, 4, :], row("L0_attn_ln2_g")), (vecs[:, 5, :], row("L0_attn_ln2_b")),
                    (scale[:, :], row("scale"))])
            with ExitStack() as c:
                dense_attention("a0", True, c, [(w0[:, :], A["L0_attn_qkv_w"]), (wp[:, :], A["L0_attn_proj_w"]),
                                                (qkb[:, :], A["qkv_b_cols"])],
                                w0[:, 0:2 * D], w0[:, 2 * D:3 * D], wp[:, :], qkb, vecs[:, 2, :], vecs[:, 3, :],
                                table, scale[:, :], ao, False)
            with ExitStack() as c:
                norm_block("n1", c, ao[:, :, :], [(vecs[:, 4, :], vecs[:, 5, :])], add_to=h[:, :, :], transpose=False)

        with ExitStack() as c:
            norm_block("n2", c, h[:, :, :], [None])
        with ExitStack() as moe:
            gw = sb("gw", [D, E], F32, moe)
            gb = sb("gb", [P, E], F32, moe)
            w1 = sb("w1", [D, E * F], F32, moe)
            w2 = sb("w2", [P, E, 2, D], F32, moe)
            b1 = sb("b1", [P, 2 * E], F32, moe)
            b2 = sb("b2", [P, E * D], F32, moe)
            rank = sb("rank", [P, E], F32, moe)
            ranki = sb("ranki", [P, E], I32, moe)
            upto = sb("upto", [P, P], F32, moe)
            ones = sb("ones", [P, P], F32, moe)
            lg = sb("lg", [P, TILES, E], F32, moe)
            pr = sb("pr", [P, TILES, E], F32, moe)
            one = sb("one", [P, TILES, E], F32, moe)
            run = [sb(f"run{k}", [P, TILES, E], F32, moe) for k in range(2)]
            gate = sb("gate", [P, TILES, E], F32, moe)
            t0 = sb("t0", [P, TILES], F32, moe)
            t1 = sb("t1", [P, TILES], F32, moe)
            full = [P, TILES, E]
            with ExitStack() as c:
                pl = ps("pl", [P, TILES * E], F32, c)
                pc = ps("pc", [P, 2, TILES * E], F32, c)
                s_w, s_lg, s_sub, s_exp, s_one, s_cum, s_link, s_tri, s_rank = (sem("m" + n, c) for n in (
                    "s_w", "s_lg", "s_sub", "s_exp", "s_one", "s_cum", "s_link", "s_tri", "s_rank"))
                block = c.enter_context(nc.Block())
                loads = [(gw[:, :], A["L0_ffn_gate_w"]), (gb[:, :], A["L0_ffn_gate_b"].partition_broadcast(P)),
                         (w1[:, :].rearrange("d (e f) -> d e f", e=E), A["L0_ffn_w1"].rearrange("e d f -> d e f")),
                         (w2[:, :, :, :].rearrange("p e a d -> p (e a) d"),
                          A["L0_ffn_w2"].rearrange("e (a p) d -> p (e a) d", p=P)),
                         (b1[:, :], A["b1_cols"]), (b2[:, :], A["L0_ffn_b2"].rearrange("e d -> (e d)").partition_broadcast(P))]

                @block.sync
                def _(sp):
                    for to, frm in loads:
                        sp.dma_start(to, frm).then_inc(s_w, 16)
                    sp.wait_ge(s_w, 16 * len(loads))

                @block.gpsimd
                def _(pool):
                    nc.gpsimd.iota(ranki[:, :], [[-1, E]], base=E, channel_multiplier=0).then_inc(s_rank, 1)
                    nc.gpsimd.memset(upto[:, :], 1.0).then_inc(s_tri, 1)
                    nc.gpsimd.memset(ones[:, :], 1.0).then_inc(s_tri, 1)
                    pool.wait_ge(s_tri, 2)
                    nc.gpsimd.affine_select(out=upto[:, :], in_=upto[:, :], compare_op=ALU.is_ge, fill=0.0,
                                            base=0, pattern=[[1, P]], channel_multiplier=-1).then_inc(s_tri, 1)

                @block.tensor
                def _(pe):
                    pe.wait_ge(s_w, 16 * len(loads))
                    for t in range(TILES):
                        last = nc.tensor.matmul(pl[:, t * E:(t + 1) * E], xT[:, t * P:(t + 1) * P], gw[:, :],
                                                start=True, stop=True)
                    last.then_inc(s_lg, 1)
                    pe.wait_ge(s_tri, 3)
                    pe.wait_ge(s_one, 1)
                    flat = one[:, :, :].rearrange("p t e -> p (t e)")
                    nc.tensor.matmul(pc[:, 0, :], upto[:, :], flat, start=True, stop=True)
                    nc.tensor.matmul(pc[:, 1, :], ones[:, :], flat, start=True, stop=True).then_inc(s_cum, 1)

                @block.scalar
                def _(act):
                    act.wait_ge(s_sub, 1)
                    nc.scalar.activation(pr[:, :, :], lg[:, :, :], ACT.Exp).then_inc(s_exp, 1)

                @block.vector
                def _(dve):
                    link = Link(dve, s_link)
                    dve.wait_ge(s_rank, 1)
                    link(nc.vector.tensor_copy(rank[:, :], ranki[:, :]))
                    dve.wait_ge(s_lg, 1)
                    dve.wait_ge(s_w, 16 * len(loads))
                    link(nc.vector.tensor_tensor(lg[:, :, :], pl[:, :].rearrange("p (t e) -> p t e", e=E),
                                                 bcast(gb[:, :], 1, full), ALU.add))
                    link(nc.vector.tensor_reduce(t0[:, :], lg[:, :, :], AX.X, ALU.max))
                    nc.vector.tensor_tensor(lg[:, :, :], lg[:, :, :], bcast(t0[:, :], 2, full), ALU.subtract).then_inc(s_sub, 1)
                    dve.wait_ge(s_exp, 1)
                    link(nc.vector.tensor_reduce(t1[:, :], pr[:, :, :], AX.X, ALU.add))
                    link(nc.vector.reciprocal(t1[:, :], t1[:, :]))
                    link(nc.vector.tensor_tensor(pr[:, :, :], pr[:, :, :], bcast(t1[:, :], 2, full), ALU.mult))
                    link(nc.vector.tensor_reduce(t0[:, :], pr[:, :, :], AX.X, ALU.max))
                    link(nc.vector.tensor_tensor(lg[:, :, :], pr[:, :, :], bcast(t0[:, :], 2, full), ALU.is_equal))
                    link(nc.vector.tensor_tensor(lg[:, :, :], lg[:, :, :], bcast(rank[:, :], 1, full), ALU.mult))
                    link(nc.vector.tensor_reduce(t1[:, :], lg[:, :, :], AX.X, ALU.max))
                    nc.vector.tensor_tensor(one[:, :, :], lg[:, :, :], bcast(t1[:, :], 2, full), ALU.is_equal).then_inc(s_one, 1)
                    dve.wait_ge(s_cum, 1)
                    link(nc.vector.tensor_copy(run[0][:, :, :], pc[:, 1, :].rearrange("p (t e) -> p t e", e=E)))
                    at, step = 0, 1
                    while step < TILES:
                        nc.vector.tensor_copy(run[1 - at][:, 0:step, :], run[at][:, 0:step, :])
                        link(nc.vector.tensor_tensor(run[1 - at][:, step:, :], run[at][:, step:, :],
                                                     run[at][:, 0:TILES - step, :], ALU.add))
                        at, step = 1 - at, 2 * step
                    link(nc.vector.tensor_tensor(gate[:, :, :], run[at][:, :, :],
                                                 pc[:, 1, :].rearrange("p (t e) -> p t e", e=E), ALU.subtract))
                    link(nc.vector.tensor_tensor(gate[:, :, :], gate[:, :, :],
                                                 pc[:, 0, :].rearrange("p (t e) -> p t e", e=E), ALU.add))
                    link(nc.vector.tensor_scalar(gate[:, :, :], gate[:, :, :], float(CAP), None, ALU.is_le))
                    link(nc.vector.tensor_tensor(gate[:, :, :], gate[:, :, :], one[:, :, :], ALU.mult))
                    link(nc.vector.tensor_tensor(gate[:, :, :], gate[:, :, :], bcast(t0[:, :], 2, full), ALU.mult))

            with ExitStack() as c:
                mid = [[sb(f"mid{k}{a}", [P, CH], F32, c) for a in range(2)] for k in range(2)]
                y = sb("y", [P, TILES, D], F32, c)
                ye = [sb(f"ye{k}", [P, E, D], F32, c) for k in range(4)]
                fine = sb("fine", [P, TILES * D], F32, c)
                fini = sb("fini", [P, TILES * D], I32, c)
                ph = [[ps(f"ph{k}{a}", [P, CH], F32, c) for a in range(2)] for k in range(2)]
                py = ps("py", [P, 4, E * D], F32, c)
                s_h, s_relu, s_y, s_taken, s_link, s_sum = (sem("x" + n, c) for n in (
                    "s_h", "s_relu", "s_y", "s_taken", "s_link", "s_sum"))
                block = c.enter_context(nc.Block())
                GROUPS = TILES // 4

                @block.tensor
                def _(pe):
                    with pe.Fori(0, GROUPS) as g:
                        def widen(e):
                            for a in range(2):
                                last = nc.tensor.matmul(ph[e % 2][a][:, :], w1[:, e * F + a * P:e * F + (a + 1) * P],
                                                        xT[:, bass.ds(g * CH, CH)], start=True, stop=True)
                            last.then_inc(s_h, 1)

                        def narrow(e):
                            pe.wait_ge(s_relu, g * E + e + 1)
                            if e == 0:
                                pe.wait_ge(s_taken, 4 * g + 4)
                            for t in range(4):
                                for a in range(2):
                                    last = nc.tensor.matmul(py[:, t, e * D:(e + 1) * D], mid[e % 2][a][:, t * P:(t + 1) * P],
                                                            w2[:, e, a, :], start=(a == 0), stop=(a == 1))
                            if e == E - 1:
                                last.then_inc(s_y, 1)

                        widen(0)
                        for e in range(E):
                            if e + 1 < E:
                                widen(e + 1)
                            narrow(e)

                @block.scalar
                def _(act):
                    nc.scalar.preload_act_table(ACT.Relu)
                    with act.Fori(0, GROUPS) as g:
                        for e in range(E):
                            act.wait_ge(s_h, g * E + e + 1)
                            for a in range(2):
                                last = nc.scalar.activation(mid[e % 2][a][:, :], ph[e % 2][a][:, :], ACT.Relu,
                                                            bias=b1[:, 2 * e + a:2 * e + a + 1])
                            last.then_inc(s_relu, 1)

                @block.vector
                def _(dve):
                    link = Link(dve, s_link)
                    nc.vector.memset(fine[:, 0:1], 0.0).then_inc(s_taken, 4)
                    with dve.Fori(0, GROUPS) as g:
                        dve.wait_ge(s_y, g + 1)
                        for t in range(4):
                            nc.vector.tensor_tensor(ye[t][:, :, :], py[:, t, :].rearrange("p (e d) -> p e d", e=E),
                                                    b2[:, :].rearrange("p (e d) -> p e d", e=E), ALU.add).then_inc(s_taken, 1)
                        dve.wait_ge(s_taken, 4 * g + 8)
                        for t in range(4):
                            link.mark(nc.vector.tensor_tensor(ye[t][:, :, :], ye[t][:, :, :],
                                                              gate[:, bass.ds(4 * g + t, 1), :].rearrange("p a e -> p (a e)")
                                                              .unsqueeze(2).to_broadcast([P, E, D]), ALU.mult))
                        link.wait()
                        for t in range(4):
                            link.mark(nc.vector.tensor_reduce(y[:, bass.ds(4 * g + t, 1), :].rearrange("p a d -> p (a d)"),
                                                              ye[t][:, :, :].rearrange("p e d -> p d e"), AX.X, ALU.add))
                        link.restart()
                    yf = y[:, :, :].rearrange("p t d -> p (t d)")
                    yc = xn[:, :, :].rearrange("p t d -> p (t d)")
                    link(nc.vector.tensor_scalar(fini[:, :], yf, 0.0, 0.0, ALU.mult, ALU.is_equal))
                    link(nc.vector.tensor_tensor(fine[:, :], yf, yf, ALU.is_equal))
                    link(nc.vector.tensor_scalar(yc, yf, -1e4, 1e4, ALU.max, ALU.min))
                    link(nc.vector.tensor_tensor(yc, yc, fine[:, :], ALU.mult))
                    link(nc.vector.copy_predicated(yc, fini[:, :], yf))
                    nc.vector.tensor_tensor(h[:, :, :], h[:, :, :], xn[:, :, :], ALU.add).then_inc(s_sum, 1)

        with ExitStack() as c:
            norm_block("n3", c, h[:, :, :], [None])
        with ExitStack() as c:
            w3 = sb("w3", [D, 4, D], F32, c)
            dense_attention("a1", False, c, [(w3[:, :, :], A["L1_attn_wT"])],
                            w3[:, 0:2, :].rearrange("c a d -> c (a d)"), w3[:, 2, :], w3[:, 3, :],
                            None, None, None, None, None, h, True)

        with ExitStack() as c:
            norm_block("n4", c, h[:, :, :], [None])
        with ExitStack() as c:
            memory(nc, A, out, c, sb, ps, sem, h, xT, ident, ident16, causal, s_started)


def memory(nc, A, out, c, sb, ps, sem, h, xT, ident, ident16, causal, s_started):
    W = 2 * D
    RING = 4
    CREDIT = RING
    keys = sb("keys", [P, HEADS // 2, N], F32, c)
    vals = sb("vals", [P, BT, HEADS, D], F32, c)
    rowbuf = [sb(f"rowbuf{r}", [P, TOPK, W], F32, c) for r in range(RING)]
    prob = sb("prob", [P, N], F32, c)
    probT = sb("probT", [P, N], F32, c)
    wq = sb("wq", [D, HEADS * D], F32, c)
    wo = sb("wo", [P, 4, D], F32, c)
    msim = sb("msim", [D, HEADS * 2 * NK], F32, c)
    xs = [sb(f"xs{k}", [D, P], F32, c) for k in range(2)]
    qs = sb("qs", [P, P], F32, c)
    acc = sb("acc", [P, W], F32, c)
    nmax = sb("nmax", [P, 1], F32, c)
    rsum = sb("rsum", [P, 1], F32, c)
    rinv = sb("rinv", [P, 1], F32, c)
    ob = sb("ob", [P, HEADS * D], F32, c)
    obT = sb("obT", [P, 4 * P], F32, c)
    top = sb("top", [P, HEADS, 2, TOPK], F32, c)
    topi = sb("topi", [P, HEADS, 2, TOPK], U32, c)
    left = sb("left", [P, 4, NK], F32, c)
    key0 = sb("key0", [P, HEADS, TOPK], F32, c)
    key1 = sb("key1", [P, HEADS, TOPK], F32, c)
    headrow = sb("headrow", [P, HEADS, TOPK], F32, c)
    headi = sb("headi", [P, HEADS, TOPK], I32, c)
    cand = sb("cand", [P, HEADS, NC], F32, c)
    candi = sb("candi", [P, HEADS, NC], F32, c)
    cleft = sb("cleft", [P, 2, NC], F32, c)
    best = sb("best", [P, HEADS, TOPK], F32, c)
    bestd = sb("bestd", [P, HEADS, TOPK], F32, c)
    beste = sb("beste", [P, HEADS, TOPK], F32, c)
    bests = sb("bests", [P, HEADS], F32, c)
    spot = sb("spot", [P, HEADS, TOPK], U32, c)
    spotf = sb("spotf", [P, HEADS, TOPK], F32, c)
    place = sb("place", [P, NC], F32, c)
    placei = sb("placei", [P, NC], I32, c)
    HH = HEADS // 2
    hit = sb("hit", [P, HH, TOPK, NC], F32, c)
    rowf = sb("rowf", [P, HH, TOPK], F32, c)
    row = [sb(f"row{k}", [P, HEADS, TOPK], U32, c) for k in range(2)]
    mixw = [sb(f"mixw{k}", [P, HEADS, TOPK], F32, c) for k in range(2)]

    with ExitStack() as cc:
        kd = sb("kd", [32, HEADS * 2, NK], F32, cc)
        wd = sb("wd", [32, HEADS * 2, D], F32, cc)
        pm = ps("pm", [D, HEADS * 2 * NK], F32, cc)
        s_w, s_m, s_mc, s_zero, s_iota = (sem("p" + n, cc) for n in ("s_w", "s_m", "s_mc", "s_zero", "s_iota"))
        block = cc.enter_context(nc.Block())
        loads = [(kd[:, :, :], A["pk_keysT"]), (wd[:, :, :], A["Wq_pkT"]), (wq[:, :], A["L1_ffn_Wq"]),
                 (wo[:, :, :], A["L1_ffn_Wo"].rearrange("(a p) d -> p a d", p=P))]

        @block.sync
        def _(sp):
            for to, frm in loads:
                sp.dma_start(to, frm).then_inc(s_w, 16)

        @block.tensor
        def _(pe):
            pe.wait_ge(s_w, 16 * len(loads))
            for m in range(HEADS * 2):
                last = nc.tensor.matmul(pm[:, m * NK:(m + 1) * NK], wd[:, m, :], kd[:, m, :], start=True, stop=True)
            last.then_inc(s_m, 1)

        @block.scalar
        def _(act):
            act.wait_ge(s_m, 1)
            for k in range(2):
                nc.scalar.activation(msim[:, k * CH:(k + 1) * CH], pm[:, k * CH:(k + 1) * CH], ACT.Copy).then_inc(s_mc, 1)

        @block.gpsimd
        def _(pool):
            nc.gpsimd.iota(headi[:, :, :], [[NK * NK, HEADS], [0, TOPK]], base=0, channel_multiplier=0).then_inc(s_iota, 1)
            nc.gpsimd.iota(placei[:, :], [[1, NC]], base=0, channel_multiplier=0).then_inc(s_iota, 1)
            nc.gpsimd.memset(vals[:, :, :, :], 0.0).then_inc(s_zero, 1)

        @block.vector
        def _(dve):
            dve.wait_ge(s_iota, 2)
            nc.vector.tensor_copy(headrow[:, :, :], headi[:, :, :])
            nc.vector.tensor_copy(place[:, :], placei[:, :])
            nc.vector.memset(keys[:, :, :], 0.0).then_inc(s_zero, 1)

    S = ps("S", [P, N], F32, c)
    tp = [ps(f"tp{k}", [P, CH], F32, c) for k in range(2)]
    psim = ps("psim", [P, CH], F32, c)
    mix = ps("mix", [P, CH], F32, c)
    Q, KT, O, PR = tp[0][0:D, 0:P], tp[1][0:D, 0:P], mix[:, 0:D], mix[:, P:P + D]
    s_xs, s_sim, s_top, s_q, s_qs, s_acc, s_kt, s_key, s_scores, s_max, s_prob, s_tp, s_tpc, s_o, s_rinv, s_ob = (
        sem("q" + n, c) for n in "s_xs s_sim s_top s_q s_qs s_acc s_kt s_key s_scores s_max s_prob s_tp s_tpc s_o s_rinv s_ob".split())
    s_obt, s_obtc, s_pr, s_res, s_out, s_diff, s_wexp, s_row, s_link = (
        sem("q" + n, c) for n in "s_obt s_obtc s_pr s_res s_out s_diff s_wexp s_row s_link".split())
    s_rows = [sem(f"s_rows{r}", c) for r in range(RING)]
    def side(hd):
        return slice(hd % 2 * D, hd % 2 * D + D)

    PIECES = 4
    LASTJ = TILES // 2 - 1
    block = c.enter_context(nc.Block())

    def turns(eng, tile):
        with eng.Fori(0, LASTJ) as j:
            tile(j, 0, True)
            tile(j, 1, True)
        tile(LASTJ, 0, True)
        tile(LASTJ, 1, False)

    @block.gpsimd
    def _(pool):
        def tile(j, k, more):
            t = 2 * j + k
            hold(pool, s_started, s_row, t + 1)
            for hd in range(HEADS):
                hold(pool, s_started, s_acc, t * HEADS + hd + 1 - RING + CREDIT)
                for m in range(TOPK):
                    pool.indirect_dma_start(rowbuf[hd % RING][:, m, :], None, A["memory"],
                                            bass.IndirectOffsetOnAxis(ap=row[k][:, hd, m:m + 1], axis=0)
                                            ).then_inc(s_rows[hd % RING], 16)
        turns(pool, tile)

    @block.sync
    def _(sp):
        def tile(j, k, more):
            t = 2 * j + k
            sp.wait_ge(s_res, t + 1)
            sp.dma_start(out[bass.ds(t, 1), :, :].rearrange("a p d -> p (a d)"),
                         h[:, bass.ds(t, 1), :].rearrange("p a d -> p (a d)")).then_inc(s_out, 16)
        turns(sp, tile)
        sp.wait_ge(s_out, 16 * TILES)

    @block.scalar
    def _(act):
        nc.scalar.preload_act_table(ACT.Exp)

        def stage(t, k):
            nc.scalar.activation(xs[k][:, :], xT[:, bass.ds(t * P, P)], ACT.Copy).then_inc(s_xs, 1)

        def weights(t):
            act.wait_ge(s_diff, t + 1)
            nc.scalar.activation(beste[:, :, :], bestd[:, :, :], ACT.Exp).then_inc(s_wexp, 1)

        def tile(j, k, more):
            t = 2 * j + k
            tb = j % (BT // 2) * 2 + k
            for hd in range(HEADS):
                n = t * HEADS + hd
                if hd == 0 and more:
                    stage(t + 1, 1 - k)
                act.wait_ge(s_q, n + 1)
                nc.scalar.activation(qs[side(hd), :], Q, ACT.Copy, scale=float(D) ** -0.5).then_inc(s_qs, 1)
                act.wait_ge(s_acc, n + 1 + CREDIT)
                nc.scalar.activation(vals[:, bass.ds(tb, 1), hd, :].rearrange("p a d -> p (a d)"), acc[:, D:W], ACT.Copy)
                act.wait_ge(s_kt, n + 1)
                nc.scalar.activation(keys[side(hd), hd // 2, bass.ds(tb * P, P)], KT, ACT.Copy).then_inc(s_key, 1)
                act.wait_ge(s_max, n + 1)
                nc.scalar.activation(prob[:, :], S[:, :], ACT.Exp, bias=nmax[:, :], accum_out=rsum[:, :]).then_inc(s_prob, 1)
                for q in range(NCH):
                    act.wait_ge(s_tp, NCH * n + q + 1)
                    nc.scalar.activation(probT[:, q * CH:(q + 1) * CH], tp[q % 2][:, :], ACT.Copy).then_inc(s_tpc, 1)
                act.wait_ge(s_rinv, n + 1)
                act.wait_ge(s_o, n + 1)
                nc.scalar.activation(ob[:, hd * D:(hd + 1) * D], O, ACT.Copy, scale=rinv[:, :]).then_inc(s_ob, 1)
                if hd == 5 and more:
                    weights(t + 1)
            act.wait_ge(s_obt, t + 1)
            nc.scalar.activation(obT[:, :], tp[0][:, :], ACT.Copy).then_inc(s_obtc, 1)

        stage(0, 0)
        weights(0)
        turns(act, tile)

    @block.tensor
    def _(pe):
        def similarities(t, k, piece):
            n = t * PIECES + piece
            if piece == 0:
                pe.wait_ge(s_xs, t + 1)
            if isinstance(t, int) and n == 0:
                pass
            else:
                pe.wait_ge(s_top, n)
            nc.tensor.matmul(psim[:, 0:4 * NK], xs[k][:, :], msim[:, piece * 4 * NK:(piece + 1) * 4 * NK],
                             start=True, stop=True).then_inc(s_sim, 1)

        def tile(j, k, more):
            t = 2 * j + k
            tb = j % (BT // 2) * 2 + k
            for hd in range(HEADS):
                n = t * HEADS + hd
                if hd < PIECES and more:
                    similarities(t + 1, 1 - k, hd)
                nc.tensor.matmul(Q, wq[:, hd * D:(hd + 1) * D], xs[k][:, :], start=True, stop=True).then_inc(s_q, 1)
                hold(pe, s_started, s_acc, n + 1 + CREDIT)
                nc.tensor.transpose(KT, acc[:, 0:D], ident[:, :]).then_inc(s_kt, 1)
                pe.wait_ge(s_qs, n + 1)
                pe.wait_ge(s_key, n + 1)
                for q in range(NCH):
                    nc.tensor.matmul(S[:, q * CH:(q + 1) * CH], qs[side(hd), :], keys[side(hd), hd // 2, q * CH:(q + 1) * CH],
                                     start=True, stop=False)
                    last = nc.tensor.matmul(S[:, q * CH:(q + 1) * CH], ident16[:, :],
                                            causal[:, bass.ds(REACH - tb * P + q * CH, CH)], start=False, stop=True)
                last.then_inc(s_scores, 1)
                pe.wait_ge(s_prob, n + 1)
                for q in range(NCH):
                    if q >= 2:
                        pe.wait_ge(s_tpc, NCH * n + q - 1)
                    for m in range(4):
                        last = nc.tensor.transpose(tp[q % 2][:, m * P:(m + 1) * P],
                                                   prob[:, (4 * q + m) * P:(4 * q + m + 1) * P], ident[:, :])
                    last.then_inc(s_tp, 1)
                for m in range(BT):
                    if m % 4 == 0:
                        pe.wait_ge(s_tpc, NCH * n + m // 4 + 1)
                    last = nc.tensor.matmul(O, probT[:, m * P:(m + 1) * P], vals[:, m, hd, :],
                                            start=(m == 0), stop=(m == BT - 1))
                last.then_inc(s_o, 1)
            pe.wait_ge(s_ob, (t + 1) * HEADS)
            for m in range(4):
                last = nc.tensor.transpose(tp[0][:, m * P:(m + 1) * P], ob[:, m * P:(m + 1) * P], ident[:, :])
            last.then_inc(s_obt, 1)
            pe.wait_ge(s_obtc, t + 1)
            for m in range(4):
                last = nc.tensor.matmul(PR, obT[:, m * P:(m + 1) * P], wo[:, m, :], start=(m == 0), stop=(m == 3))
            last.then_inc(s_pr, 1)

        for piece in range(PIECES):
            similarities(0, 0, piece)
        turns(pe, tile)

    @block.vector
    def _(dve):
        link = Link(dve, s_link)
        nc.vector.memset(acc[:, :], 0.0).then_inc(s_acc, CREDIT)
        dve.wait_ge(s_acc, CREDIT)

        def halves(t, piece):
            hold(dve, s_started, s_sim, t * PIECES + piece + 1)
            four = [(2 * piece + m // 2, m % 2, psim[:, m * NK:(m + 1) * NK], left[:, m, :]) for m in range(4)]
            for hd, p, src, rest in four:
                link.mark(nc.vector.max(top[:, hd, p, 0:8], src))
            link.wait()
            for hd, p, src, rest in four:
                link.mark(nc.vector.match_replace(rest, top[:, hd, p, 0:8], src, LOWEST))
                last = nc.vector.max_index(topi[:, hd, p, 0:8], top[:, hd, p, 0:8], src)
            last.then_inc(s_top, 1)
            link.wait()
            for hd, p, src, rest in four:
                link.mark(nc.vector.max(top[:, hd, p, 8:16], rest))
            link.wait()
            for hd, p, src, rest in four:
                link.mark(nc.vector.max_index(topi[:, hd, p, 8:16], top[:, hd, p, 8:16], rest))
            link.wait()

        def candidates():
            link.mark(nc.vector.tensor_copy(key0[:, :, :], topi[:, :, 0, :]))
            link(nc.vector.scalar_tensor_tensor(key1[:, :, :], topi[:, :, 1, :], float(NK), headrow[:, :, :],
                                                ALU.mult, ALU.add))
            at = 0
            for a, na, nb in PAIRS:
                shape = [P, HEADS, na, nb]
                for to, x, y in ((cand, top[:, :, 0, a:a + na], top[:, :, 1, 0:nb]),
                                 (candi, key0[:, :, a:a + na], key1[:, :, 0:nb])):
                    link.mark(nc.vector.tensor_tensor(to[:, :, at:at + na * nb].rearrange("p h (a b) -> p h a b", a=na),
                                                      x.unsqueeze(3).to_broadcast(shape), y.unsqueeze(2).to_broadcast(shape),
                                                      ALU.add))
                at += na * nb
            link.wait()

        def choose(heads):
            for pair in range(heads.start, heads.stop, 2):
                two = [(pair + m, cleft[:, m, :]) for m in range(2)]
                for hd, rest in two:
                    link.mark(nc.vector.max(best[:, hd, 0:8], cand[:, hd, :]))
                link.wait()
                for hd, rest in two:
                    link.mark(nc.vector.match_replace(rest, best[:, hd, 0:8], cand[:, hd, :], LOWEST))
                    link.mark(nc.vector.max_index(spot[:, hd, 0:8], best[:, hd, 0:8], cand[:, hd, :]))
                link.wait()
                for hd, rest in two:
                    link.mark(nc.vector.max(best[:, hd, 8:16], rest))
                link.wait()
                for hd, rest in two:
                    link.mark(nc.vector.max_index(spot[:, hd, 8:16], best[:, hd, 8:16], rest))
                link.wait()

        def less_largest():
            link.mark(nc.vector.tensor_copy(spotf[:, :, :], spot[:, :, :]))
            nc.vector.tensor_tensor(bestd[:, :, :], best[:, :, :], best[:, :, 0:1].to_broadcast([P, HEADS, TOPK]),
                                    ALU.subtract).then_inc(s_diff, 1)
            link.wait()

        def normalise(t, k):
            dve.wait_ge(s_wexp, t + 1)
            link(nc.vector.tensor_reduce(bests[:, :], beste[:, :, :], AX.X, ALU.add))
            link(nc.vector.reciprocal(bests[:, :], bests[:, :]))
            link(nc.vector.tensor_tensor(mixw[k][:, :, :], beste[:, :, :], bcast(bests[:, :], 2, [P, HEADS, TOPK]), ALU.mult))

        def find_rows(k, half):
            hs = slice(half * HH, (half + 1) * HH)
            flat = [P, HH * TOPK, NC]
            hits = hit[:, :, :, :].rearrange("p h k c -> p (h k) c")
            link(nc.vector.tensor_tensor(hits, bcast(spotf[:, hs, :].rearrange("p h k -> p (h k)"), 2, flat),
                                         bcast(place[:, :], 1, flat), ALU.is_equal))
            link(nc.vector.tensor_tensor(hit[:, :, :, :], hit[:, :, :, :], bcast(candi[:, hs, :], 2, [P, HH, TOPK, NC]),
                                         ALU.mult))
            link(nc.vector.tensor_reduce(rowf[:, :, :].rearrange("p h k -> p (h k)"), hits, AX.X, ALU.add))
            last = nc.vector.tensor_copy(row[k][:, hs, :], rowf[:, :, :])
            if half:
                last.then_inc(s_row, 1)
            else:
                link(last)

        def ahead(t, k, slot):
            if slot < PIECES:
                halves(t, slot)
            if slot == 4:
                candidates()
                choose(range(0, 4))
            if slot == 5:
                choose(range(4, 8))
                less_largest()
            if slot == 6:
                normalise(t, k)
                find_rows(k, 0)
            if slot == 7:
                find_rows(k, 1)

        def tile(j, k, more):
            t = 2 * j + k
            for hd in range(HEADS):
                n = t * HEADS + hd
                r = hd % RING
                dve.wait_ge(s_rows[r], 16 * TOPK * (t * (HEADS // RING) + hd // RING + 1))
                link(nc.vector.tensor_scalar(acc[:, :], rowbuf[r][:, 0, :], mixw[k][:, hd, 0:1], None, ALU.mult))
                for m in range(1, TOPK):
                    ins = nc.vector.scalar_tensor_tensor(acc[:, :], rowbuf[r][:, m, :], mixw[k][:, hd, m:m + 1],
                                                         acc[:, :], ALU.mult, ALU.add)
                    if m < TOPK - 1:
                        link(ins)
                    else:
                        ins.then_inc(s_acc, 1)
                if more:
                    ahead(t + 1, 1 - k, hd)
                dve.wait_ge(s_scores, n + 1)
                nc.vector.tensor_reduce(nmax[:, :], S[:, :], AX.X, ALU.max, negate=True).then_inc(s_max, 1)
                dve.wait_ge(s_prob, n + 1)
                nc.vector.reciprocal(rinv[:, :], rsum[:, :]).then_inc(s_rinv, 1)
            dve.wait_ge(s_pr, t + 1)
            at = h[:, bass.ds(t, 1), :].rearrange("p a d -> p (a d)")
            nc.vector.tensor_tensor(at, PR, at, ALU.add).then_inc(s_res, 1)
            link.restart()

        for slot in range(HEADS):
            ahead(0, 0, slot)
        link.restart()
        turns(dve, tile)


def kernel(**inputs):
    import numpy as np
    import concourse.bacc as bacc
    from concourse.bass_utils import run_bass_kernel_spmd as run

    nc = bacc.Bacc("TRN2", target_bir_lowering=False, num_devices=1)
    a = {k: np.asarray(v) for k, v in inputs.items()}
    arrays = {
        "ids": a["x"].reshape(TILES, P).T,
        "ple": a["L0_tok_ple_table"].reshape(VOCAB * PLE // D, D),
        "qkv_b_cols": a["L0_attn_qkv_b"].reshape(3, D).T,
        "scale": a["L0_attn_scale"].reshape(1),
        "b1_cols": a["L0_ffn_b1"].reshape(2 * E, P).T,
        "L1_attn_wT": np.stack([a["L1_attn_W" + n].T for n in "qkvo"], axis=1),
        "pk_keysT": a["L1_ffn_pk_keys"].transpose(3, 2, 0, 1).reshape(32, 2 * HEADS, NK),
        "Wq_pkT": a["L1_ffn_Wq_pk"].reshape(D, 2, HEADS, 32).transpose(3, 2, 1, 0).reshape(32, 2 * HEADS, D),
        "memory": np.concatenate([a["L1_ffn_keys_table"], a["L1_ffn_values_table"]], axis=1),
    }
    for name in ("L0_attn_bias_table L0_attn_ln1_g L0_attn_ln1_b L0_attn_qkv_b L0_attn_qkv_w L0_attn_proj_w L0_attn_proj_b "
                 "L0_attn_ln2_g L0_attn_ln2_b L0_ffn_gate_w L0_ffn_gate_b L0_ffn_w1 L0_ffn_w2 L0_ffn_b2 L1_ffn_Wq "
                 "L1_ffn_Wo").split():
        arrays[name] = a[name]
    arrays = {k: np.ascontiguousarray(v) for k, v in arrays.items()}
    A = {k: nc.dram_tensor("in_" + k, v.shape, mybir.dt.from_np(v.dtype), kind="ExternalInput").ap()
         for k, v in arrays.items()}
    out = nc.dram_tensor("out", (TILES, P, D), F32, kind="ExternalOutput").ap()
    build(nc, A, out)
    r = run(nc, [{"in_" + k: v for k, v in arrays.items()}], core_ids=[0])
    return r.results[0]["out"].reshape(B, N, D)
```

```python
from contextlib import ExitStack

import concourse.bass as bass
from concourse import mybir

ALU = mybir.AluOpType
ACT = mybir.ActivationFunctionType
AX = mybir.AxisListType
F32 = mybir.dt.float32
BF16 = mybir.dt.bfloat16
I32 = mybir.dt.int32
U32 = mybir.dt.uint32
U16 = mybir.dt.uint16

P = 128
D = 64
B, N = 2, 2048
TILES = B * N // P
BT = N // P
CH = 512
NCH = N // CH
VOCAB, PLE = 32000, 512
PLE_START = 3 * 64
EPS = 1e-5
E, F = 8, 256
CAP = 5 * B * N // (4 * E)
HEADS, NK, TOPK = 8, 64, 16
REACH = N - P
WIDE = REACH + N
FAR = -1e30
LOWEST = -3.0e38

PAIRS = [(0, 1, 16), (1, 1, 8), (2, 2, 5), (4, 4, 3), (8, 8, 1)]
NC = sum(na * nb for _, na, nb in PAIRS)
FEW = [(0, 0, 8), (8, 16, 4), (12, 24, 2), (14, 29, 2), (16, 34, 1), (17, 37, 1), (18, 40, 1), (19, 43, 1)]
NFEW = 20


def bcast(ap, axis, shape):
    return ap.unsqueeze(axis).to_broadcast(shape)


class Link:

    def __init__(self, eng, sem):
        self.eng, self.sem, self.n = eng, sem, 0

    def __call__(self, ins):
        self.mark(ins)
        self.wait()

    def mark(self, ins):
        self.n += 1
        ins.then_inc(self.sem, 1)

    def wait(self):
        self.eng.wait_ge(self.sem, self.n)

    def restart(self):
        self.eng.wait_ge(self.sem, self.n)
        self.eng.sem_clear(self.sem)
        self.n = 0


def hold(eng, started, sem, value):
    value = eng.to_reg(value)
    eng.wait_ge(started, 1)
    eng.wait_ge(sem, value)


def layer_norm(nc, dve, link, src, dst, sq, st, s_var, s_std, n, affine=None):
    full = [P, TILES, D]
    link(nc.vector.tensor_reduce(st[:, 0, :], src, AX.X, ALU.add))
    link(nc.vector.tensor_scalar(st[:, 0, :], st[:, 0, :], 1.0 / D, None, ALU.mult))
    link(nc.vector.tensor_tensor(dst, src, bcast(st[:, 0, :], 2, full), ALU.subtract))
    link(nc.vector.tensor_tensor(sq, dst, dst, ALU.mult))
    link(nc.vector.tensor_reduce(st[:, 1, :], sq, AX.X, ALU.add))
    nc.vector.tensor_scalar(st[:, 1, :], st[:, 1, :], 1.0 / D, EPS, ALU.mult, ALU.add).then_inc(s_var, 1)
    dve.wait_ge(s_std, n)
    link(nc.vector.reciprocal(st[:, 3, :], st[:, 2, :]))
    link(nc.vector.tensor_tensor(dst, dst, bcast(st[:, 3, :], 2, full), ALU.mult))
    if affine:
        gain, shift = affine
        link(nc.vector.tensor_tensor(dst, dst, bcast(gain, 1, full), ALU.mult))
        link(nc.vector.tensor_tensor(dst, dst, bcast(shift, 1, full), ALU.add))


def root(nc, act, st, s_var, s_std, n):
    act.wait_ge(s_var, n)
    nc.scalar.activation(st[:, 2, :], st[:, 1, :], ACT.Sqrt).then_inc(s_std, 1)


def build(nc, A, out):
    with ExitStack() as whole:
        def sb(name, shape, dt=F32, ctx=whole):
            return ctx.enter_context(nc.sbuf_tensor(name, shape, dt))

        def ps(name, shape, dt=F32, ctx=whole):
            return ctx.enter_context(nc.psum_tensor(name, shape, dt))

        def sem(name, ctx=whole):
            return ctx.enter_context(nc.semaphore(name))

        h = sb("h", [P, TILES, D])
        xn = sb("xn", [P, TILES, D])
        xT = sb("xT", [P, TILES * P])
        st = sb("st", [P, 4, TILES])
        ident = sb("ident", [P, P])
        ident16 = sb("ident16", [P, P], BF16)
        causal = sb("causal", [P, WIDE], BF16)
        rc = sb("rc", [P, BT])
        s_started = sem("s_started")

        def transposed(phase, pe, act, tp, s_norm, s_tr, s_cp):
            def on_pe():
                pe.wait_ge(s_norm, 1)
                for g in range(TILES // 4):
                    if g >= 2:
                        pe.wait_ge(s_cp, g - 1)
                    for k in range(4):
                        last = nc.tensor.transpose(tp[g % 2][0:D, k * P:(k + 1) * P], xn[:, 4 * g + k, :], ident[:, :])
                    last.then_inc(s_tr, 1)

            def on_act():
                for g in range(TILES // 4):
                    act.wait_ge(s_tr, g + 1)
                    nc.scalar.activation(xT[0:D, g * CH:(g + 1) * CH], tp[g % 2][0:D, :], ACT.Copy).then_inc(s_cp, 1)
            return on_pe if phase == "pe" else on_act

        with ExitStack() as c:
            ids = sb("ids", [P, TILES], I32, c)
            idf = sb("idf", [P, TILES], F32, c)
            wrap = sb("wrap", [P, TILES], F32, c)
            rows = sb("rows", [P, TILES], U32, c)
            rci = sb("rci", [P, BT], I32, c)
            s_ids, s_rows, s_link, s_tok, s_iota, s_fill = (sem(n, c) for n in (
                "s_ids", "s_rows", "s_link0", "s_tok", "s_iota", "s_fill"))
            block = c.enter_context(nc.Block())

            @block.sync
            def _(sp):
                sp.dma_start(ids[:, :], A["ids"]).then_inc(s_ids, 16)

            @block.vector
            def _(dve):
                link = Link(dve, s_link)
                dve.wait_ge(s_ids, 16)
                link(nc.vector.tensor_copy(idf[:, :], ids[:, :]))
                link(nc.vector.tensor_scalar(wrap[:, :], idf[:, :], 0.0, float(VOCAB), ALU.is_lt, ALU.mult))
                link(nc.vector.tensor_tensor(idf[:, :], idf[:, :], wrap[:, :], ALU.add))
                link(nc.vector.tensor_scalar(idf[:, :], idf[:, :], 0.0, float(VOCAB - 1), ALU.max, ALU.min))
                nc.vector.tensor_scalar(rows[:, :], idf[:, :], float(PLE // D), float(PLE_START // D),
                                        ALU.mult, ALU.add).then_inc(s_rows, 1)
                dve.wait_ge(s_iota, 1)
                nc.vector.memset(xT[D:P, :], 0.0)
                link(nc.vector.tensor_scalar(rc[:, :], rci[:, :], 1.0, None, ALU.max))
                link(nc.vector.reciprocal(rc[:, :], rc[:, :]))

            @block.gpsimd
            def _(pool):
                nc.gpsimd.iota(rci[:, :], [[P, BT]], base=0, channel_multiplier=1).then_inc(s_iota, 1)
                nc.gpsimd.memset(ident[:, :], 0.0).then_inc(s_fill, 1)
                nc.gpsimd.memset(ident16[:, :], 0.0).then_inc(s_fill, 1)
                nc.gpsimd.memset(causal[:, :], 0.0).then_inc(s_fill, 1)
                pool.wait_ge(s_fill, 3)
                nc.gpsimd.affine_select(out=ident[:, :], in_=ident[:, :], compare_op=ALU.not_equal, fill=1.0,
                                        base=0, pattern=[[-1, P]], channel_multiplier=1)
                nc.gpsimd.affine_select(out=ident16[:, :], in_=ident16[:, :], compare_op=ALU.not_equal, fill=1.0,
                                        base=0, pattern=[[-1, P]], channel_multiplier=1)
                nc.gpsimd.affine_select(out=causal[:, :], in_=causal[:, :], compare_op=ALU.is_ge, fill=FAR,
                                        base=REACH, pattern=[[-1, WIDE]], channel_multiplier=1).then_inc(s_started, 1)
                pool.wait_ge(s_rows, 1)
                for t in range(TILES):
                    pool.indirect_dma_start(h[:, t, :], None, A["ple"],
                                            bass.IndirectOffsetOnAxis(ap=rows[:, t:t + 1], axis=0)).then_inc(s_tok, 16)
                pool.wait_ge(s_tok, 16 * TILES)

        def dense_attention(name, biased, c, load, pad_w, qk_w, v_w, proj_w, qk_bias, v_bias, proj_bias, table, scale,
                            dest, accumulate):
            qT = sb(name + "qT", [D, B * N], F32, c)
            kT = sb(name + "kT", [P, B * N], F32, c)
            v = sb(name + "v", [P, TILES, D], F32, c)
            qs = [sb(f"{name}qs{k}", [P, P], F32, c) for k in range(2)]
            prob = [sb(f"{name}prob{k}", [P, N], F32, c) for k in range(2)]
            probT = sb(name + "probT", [P, N], F32, c)
            biased_s = sb(name + "bs", [P, N], F32, c) if biased else None
            nmax = [sb(f"{name}nmax{k}", [P, 1], F32, c) for k in range(2)]
            rsum = [sb(f"{name}rsum{k}", [P, 1], F32, c) for k in range(2)]
            rinv = [sb(f"{name}rinv{k}", [P, 2], F32, c) for k in range(2)]
            ob = sb(name + "ob", [P, D], F32, c)
            obT = sb(name + "obT", [D, P], F32, c)
            S = ps(name + "S", [P, N], F32, c)
            tp = [ps(f"{name}tp{k}", [P, CH], F32, c) for k in range(2)]
            mix = [ps(f"{name}mix{k}", [P, CH], F32, c) for k in range(2)]
            O, OT, PR = mix[0][:, 0:D], mix[0][0:D, P:2 * P], mix[1][:, 0:D]

            with ExitStack() as cc:
                s_w, s_qk, s_qkc, s_v, s_vc, s_pad = (sem(name + n, cc) for n in ("s_w", "s_qk", "s_qkc", "s_v", "s_vc", "s_pad"))
                block = cc.enter_context(nc.Block())
                nload = len(load)

                @block.sync
                def _(sp):
                    for dst, src in load:
                        sp.dma_start(dst, src).then_inc(s_w, 16)
                    sp.wait_ge(s_w, 16 * nload)

                @block.tensor
                def _(pe):
                    pe.wait_ge(s_w, 16 * nload)
                    pe.wait_ge(s_pad, 1)
                    for g in range(TILES * P // CH):
                        if g >= 2:
                            pe.wait_ge(s_qkc, 2 * (g - 1))
                        nc.tensor.matmul(tp[g % 2][:, :], qk_w, xT[:, g * CH:(g + 1) * CH],
                                         start=True, stop=True).then_inc(s_qk, 1)
                    for g in range(TILES // 8):
                        for k in range(8):
                            last = nc.tensor.matmul(S[:, g * CH + k * D:g * CH + (k + 1) * D],
                                                    xT[:, (8 * g + k) * P:(8 * g + k + 1) * P], v_w,
                                                    start=True, stop=True)
                        last.then_inc(s_v, 1)

                @block.scalar
                def _(act):
                    for g in range(TILES * P // CH):
                        act.wait_ge(s_qk, g + 1)
                        for k, dst in ((0, qT), (1, kT)):
                            src = tp[g % 2][k * D:(k + 1) * D, :]
                            to = dst[0:D, g * CH:(g + 1) * CH]
                            if qk_bias is None:
                                nc.scalar.activation(to, src, ACT.Copy).then_inc(s_qkc, 1)
                            else:
                                nc.scalar.activation(to, src, ACT.Identity, bias=qk_bias[:, k:k + 1]).then_inc(s_qkc, 1)

                @block.vector
                def _(dve):
                    nc.vector.memset(pad_w, 0.0).then_inc(s_pad, 1)
                    for pad in (kT, qs[0], qs[1]):
                        nc.vector.memset(pad[D:P, :], 0.0)
                    for g in range(TILES // 8):
                        dve.wait_ge(s_v, g + 1)
                        src = S[:, g * CH:(g + 1) * CH].rearrange("p (k d) -> p k d", d=D)
                        to = v[:, 8 * g:8 * g + 8, :]
                        if v_bias is None:
                            nc.vector.tensor_copy(to, src).then_inc(s_vc, 1)
                        else:
                            nc.vector.tensor_tensor(to, src, bcast(v_bias, 1, [P, 8, D]), ALU.add).then_inc(s_vc, 1)

            with ExitStack() as cc:
                names = "s_qs s_scores s_read s_max s_prob s_tp s_tpc s_o s_ob s_obt s_obs s_proj s_link s_done"
                (s_qs, s_scores, s_read, s_max, s_prob, s_tp, s_tpc, s_o, s_ob, s_obt, s_obs, s_proj, s_link,
                 s_done) = (sem(name + n, cc) for n in names.split())
                block = cc.enter_context(nc.Block())

                def place(j, k):
                    return (2 * j + k) * P, j // (BT // 2) * N, j % (BT // 2) * 2 + k

                @block.scalar
                def _(act):
                    nc.scalar.preload_act_table(ACT.Exp)

                    def stage(j, k):
                        nc.scalar.activation(qs[k % 2][0:D, :], qT[:, bass.ds(place(j, k)[0], P)], ACT.Copy).then_inc(s_qs, 1)

                    def weights(j, k):
                        i = 2 * j + k
                        if biased:
                            act.wait_ge(s_max, i + 1)
                            nc.scalar.activation(prob[k % 2][:, :], biased_s[:, :], ACT.Exp, bias=nmax[k % 2][:, :],
                                                 accum_out=rsum[k % 2][:, :]).then_inc(s_prob, 1)
                        else:
                            act.wait_ge(s_scores, i + 1)
                            nc.scalar.activation(prob[k % 2][:, :], S[:, :], ACT.Relu).then_inc(s_prob, 1)

                    def item(j, k, ahead):
                        i = 2 * j + k
                        if ahead:
                            stage(j + (k + 1) // 2, (k + 1) % 2)
                        for q in range(NCH):
                            act.wait_ge(s_tp, NCH * i + q + 1)
                            nc.scalar.activation(probT[:, q * CH:(q + 1) * CH], tp[q % 2][:, :], ACT.Copy).then_inc(s_tpc, 1)
                        act.wait_ge(s_obt, i + 1)
                        nc.scalar.activation(obT[:, :], OT, ACT.Copy).then_inc(s_obs, 1)
                        if ahead:
                            weights(j + (k + 1) // 2, (k + 1) % 2)

                    stage(0, 0)
                    weights(0, 0)
                    with act.Fori(0, TILES // 2 - 1) as j:
                        item(j, 0, True)
                        item(j, 1, True)
                    item(TILES // 2 - 1, 0, True)
                    item(TILES // 2 - 1, 1, False)

                @block.tensor
                def _(pe):
                    def scores(j, k, wait_read):
                        i = 2 * j + k
                        _, first, tb = place(j, k)
                        pe.wait_ge(s_qs, i + 1)
                        if wait_read:
                            pe.wait_ge(s_read if biased else s_prob, i)
                        for q in range(NCH):
                            last = nc.tensor.matmul(S[:, q * CH:(q + 1) * CH], qs[k % 2][:, :],
                                                    kT[:, bass.ds(first + q * CH, CH)], start=True, stop=biased)
                            if not biased:
                                last = nc.tensor.matmul(S[:, q * CH:(q + 1) * CH], ident16[:, :],
                                                        causal[:, bass.ds(REACH - tb * P + q * CH, CH)],
                                                        start=False, stop=True)
                        last.then_inc(s_scores, 1)

                    def item(j, k, ahead):
                        i = 2 * j + k
                        _, first, tb = place(j, k)
                        batch = j // (BT // 2) * BT
                        if ahead:
                            scores(j + (k + 1) // 2, (k + 1) % 2, True)
                        pe.wait_ge(s_prob, i + 1)
                        for q in range(NCH):
                            if q >= 2:
                                pe.wait_ge(s_tpc, NCH * i + q - 1)
                            for m in range(4):
                                last = nc.tensor.transpose(tp[q % 2][:, m * P:(m + 1) * P],
                                                           prob[k % 2][:, (4 * q + m) * P:(4 * q + m + 1) * P], ident[:, :])
                            last.then_inc(s_tp, 1)
                        for m in range(BT):
                            if m % 4 == 0:
                                pe.wait_ge(s_tpc, NCH * i + m // 4 + 1)
                            last = nc.tensor.matmul(O, probT[:, m * P:(m + 1) * P],
                                                    v[:, bass.ds(batch + m, 1), :].rearrange("p a d -> p (a d)"),
                                                    start=(m == 0), stop=(m == BT - 1))
                        last.then_inc(s_o, 1)
                        hold(pe, s_started, s_ob, i + 1)
                        nc.tensor.transpose(OT, ob[:, :], ident[:, :]).then_inc(s_obt, 1)
                        pe.wait_ge(s_obs, i + 1)
                        nc.tensor.matmul(PR, obT[:, :], proj_w, start=True, stop=True).then_inc(s_proj, 1)

                    scores(0, 0, False)
                    with pe.Fori(0, TILES // 2 - 1) as j:
                        item(j, 0, True)
                        item(j, 1, True)
                    item(TILES // 2 - 1, 0, True)
                    item(TILES // 2 - 1, 1, False)

                @block.vector
                def _(dve):
                    link = Link(dve, s_link)

                    def soften(j, k):
                        i = 2 * j + k
                        tb = place(j, k)[2]
                        dve.wait_ge(s_scores, i + 1)
                        nc.vector.tensor_tensor(biased_s[:, :], S[:, :], table[:, bass.ds(REACH - tb * P, N)],
                                                ALU.add).then_inc(s_read, 1)
                        dve.wait_ge(s_read, i + 1)
                        nc.vector.tensor_reduce(nmax[k % 2][:, :], biased_s[:, :], AX.X, ALU.max,
                                                negate=True).then_inc(s_max, 1)

                    def item(j, k, ahead):
                        i = 2 * j + k
                        tb = place(j, k)[2]
                        if biased:
                            dve.wait_ge(s_prob, i + 1)
                            link(nc.vector.reciprocal(rinv[k % 2][:, 0:1], rsum[k % 2][:, :]))
                            link(nc.vector.tensor_tensor(rinv[k % 2][:, 1:2], rinv[k % 2][:, 0:1], scale, ALU.mult))
                            if ahead:
                                soften(j + (k + 1) // 2, (k + 1) % 2)
                        dve.wait_ge(s_o, i + 1)
                        by = rinv[k % 2][:, 1:2] if biased else rc[:, bass.ds(tb, 1)]
                        nc.vector.tensor_scalar(ob[:, :], O, by, None, ALU.mult).then_inc(s_ob, 1)
                        dve.wait_ge(s_proj, i + 1)
                        to = dest[:, bass.ds(i, 1), :].rearrange("p a d -> p (a d)")
                        nc.vector.tensor_tensor(to, PR, to if accumulate else proj_bias, ALU.add).then_inc(s_done, 1)

                    if biased:
                        soften(0, 0)
                    with dve.Fori(0, TILES // 2 - 1) as j:
                        item(j, 0, True)
                        item(j, 1, True)
                        link.restart() if biased else None
                    item(TILES // 2 - 1, 0, True)
                    item(TILES // 2 - 1, 1, False)

        def norm_block(name, c, src, affines, dst=None, add_to=None, load=(), transpose=True):
            sq = sb(name + "sq", [P, TILES, D], F32, c)
            tp = [ps(f"{name}tp{k}", [P, CH], F32, c) for k in range(2)]
            s_w, s_var, s_std, s_norm, s_tr, s_cp, s_link = (sem(name + n, c) for n in (
                "s_w", "s_var", "s_std", "s_norm", "s_tr", "s_cp", "s_link"))
            block = c.enter_context(nc.Block())
            if load:
                @block.sync
                def _(sp):
                    for to, frm in load:
                        sp.dma_start(to, frm).then_inc(s_w, 16)

            @block.vector
            def _(dve):
                link = Link(dve, s_link)
                if load:
                    dve.wait_ge(s_w, 16 * len(load))
                at = src
                for n, affine in enumerate(affines):
                    layer_norm(nc, dve, link, at, xn[:, :, :], sq[:, :, :], st, s_var, s_std, n + 1, affine)
                    at = xn[:, :, :]
                if add_to is not None:
                    link(nc.vector.tensor_tensor(add_to, add_to, xn[:, :, :], ALU.add))
                nc.vector.memset(sq[:, 0, 0:1], 0.0).then_inc(s_norm, 1)

            @block.scalar
            def _(act):
                for n in range(len(affines)):
                    root(nc, act, st, s_var, s_std, n + 1)
                if transpose:
                    transposed("act", None, act, tp, s_norm, s_tr, s_cp)()

            if transpose:
                @block.tensor
                def _(pe):
                    transposed("pe", pe, None, tp, s_norm, s_tr, s_cp)()

        with ExitStack() as l0:
            LX = 1152
            table = sb("table", [P, WIDE], F32, l0)
            vecs = sb("vecs", [P, 6, D], F32, l0)
            scale = sb("scale", [P, 1], F32, l0)
            qkb = sb("qkb", [D, 3], F32, l0)
            w0 = sb("w0", [P, 3 * D], F32, l0)
            wp = sb("wp", [D, D], F32, l0)
            ao = sb("ao", [P, TILES, D], F32, l0)
            shear = nc.dram_tensor("shear", (P * LX,), F32, kind="Internal").ap()
            with ExitStack() as c:
                line = sb("line", [P, LX], F32, c)
                s_line, s_long, s_out, s_back, s_fill = (sem(n, c) for n in (
                    "s_line", "s_long", "s_sheared", "s_back", "s_tabled"))
                block = c.enter_context(nc.Block())
                known = A["L0_attn_bias_table"].shape[0]

                @block.sync
                def _(sp):
                    sp.dma_start(line[:, 0:known], A["L0_attn_bias_table"].partition_broadcast(P)).then_inc(s_line, 16)
                    sp.wait_ge(s_long, 1)
                    sp.dma_start(shear.rearrange("(p n) -> p n", n=LX), line[:, :]).then_inc(s_out, 16)
                    sp.wait_ge(s_out, 16)
                    sp.dma_start(table[:, 0:1024], shear[0:P * (LX - 1)].rearrange("(p n) -> p n", n=LX - 1)[:, P - 1:P - 1 + 1024]
                                 ).then_inc(s_back, 16)

                @block.vector
                def _(dve):
                    dve.wait_ge(s_line, 16)
                    nc.vector.tensor_copy(line[:, known:LX], line[:, known - 1:known].to_broadcast([P, LX - known])).then_inc(s_long, 1)
                    dve.wait_ge(s_back, 16)
                    nc.vector.tensor_copy(table[:, 1024:WIDE], table[:, 1023:1024].to_broadcast([P, WIDE - 1024])).then_inc(s_fill, 1)

            with ExitStack() as c:
                row = lambda n: A[n].partition_broadcast(P)
                norm_block("n0", c, h[:, :, :], [None, (vecs[:, 0, :], vecs[:, 1, :])], load=[
                    (vecs[:, 0, :], row("L0_attn_ln1_g")), (vecs[:, 1, :], row("L0_attn_ln1_b")),
                    (vecs[:, 2, :], A["L0_attn_qkv_b"][2 * D:3 * D].partition_broadcast(P)),
                    (vecs[:, 3, :], row("L0_attn_proj_b")),
                    (vecs[:, 4, :], row("L0_attn_ln2_g")), (vecs[:, 5, :], row("L0_attn_ln2_b")),
                    (scale[:, :], row("scale"))])
            with ExitStack() as c:
                dense_attention("a0", True, c, [(w0[0:D, :], A["L0_attn_qkv_w"]), (wp[:, :], A["L0_attn_proj_w"]),
                                                (qkb[:, :], A["qkv_b_cols"])], w0[D:P, :],
                                w0[:, 0:2 * D], w0[:, 2 * D:3 * D], wp[:, :], qkb, vecs[:, 2, :], vecs[:, 3, :],
                                table, scale[:, :], ao, False)
            with ExitStack() as c:
                norm_block("n1", c, ao[:, :, :], [(vecs[:, 4, :], vecs[:, 5, :])], add_to=h[:, :, :], transpose=False)

        with ExitStack() as c:
            norm_block("n2", c, h[:, :, :], [None])
        with ExitStack() as moe:
            gw = sb("gw", [P, E], F32, moe)
            gb = sb("gb", [P, E], F32, moe)
            w1 = sb("w1", [P, E * F], F32, moe)
            w2 = sb("w2", [P, E, 2, D], F32, moe)
            b1 = sb("b1", [P, 2 * E], F32, moe)
            b2 = sb("b2", [P, E * D], F32, moe)
            rank = sb("rank", [P, E], F32, moe)
            ranki = sb("ranki", [P, E], I32, moe)
            upto = sb("upto", [P, P], F32, moe)
            ones = sb("ones", [P, P], F32, moe)
            lg = sb("lg", [P, TILES, E], F32, moe)
            pr = sb("pr", [P, TILES, E], F32, moe)
            one = sb("one", [P, TILES, E], F32, moe)
            run = [sb(f"run{k}", [P, TILES, E], F32, moe) for k in range(2)]
            gate = sb("gate", [P, TILES, E], F32, moe)
            t0 = sb("t0", [P, TILES], F32, moe)
            t1 = sb("t1", [P, TILES], F32, moe)
            full = [P, TILES, E]
            with ExitStack() as c:
                pl = ps("pl", [P, TILES * E], F32, c)
                pc = ps("pc", [P, 2, TILES * E], F32, c)
                s_w, s_lg, s_sub, s_exp, s_one, s_cum, s_link, s_tri, s_rank, s_pad = (sem("m" + n, c) for n in (
                    "s_w", "s_lg", "s_sub", "s_exp", "s_one", "s_cum", "s_link", "s_tri", "s_rank", "s_pad"))
                block = c.enter_context(nc.Block())
                loads = [(gw[0:D, :], A["L0_ffn_gate_w"]), (gb[:, :], A["L0_ffn_gate_b"].partition_broadcast(P)),
                         (w1[0:D, :].rearrange("d (e f) -> d e f", e=E), A["L0_ffn_w1"].rearrange("e d f -> d e f")),
                         (w2[:, :, :, :].rearrange("p e a d -> p (e a) d"),
                          A["L0_ffn_w2"].rearrange("e (a p) d -> p (e a) d", p=P)),
                         (b1[:, :], A["b1_cols"]), (b2[:, :], A["L0_ffn_b2"].rearrange("e d -> (e d)").partition_broadcast(P))]

                @block.sync
                def _(sp):
                    for to, frm in loads:
                        sp.dma_start(to, frm).then_inc(s_w, 16)
                    sp.wait_ge(s_w, 16 * len(loads))

                @block.gpsimd
                def _(pool):
                    nc.gpsimd.iota(ranki[:, :], [[-1, E]], base=E, channel_multiplier=0).then_inc(s_rank, 1)
                    nc.gpsimd.memset(upto[:, :], 1.0).then_inc(s_tri, 1)
                    nc.gpsimd.memset(ones[:, :], 1.0).then_inc(s_tri, 1)
                    pool.wait_ge(s_tri, 2)
                    nc.gpsimd.affine_select(out=upto[:, :], in_=upto[:, :], compare_op=ALU.is_ge, fill=0.0,
                                            base=0, pattern=[[1, P]], channel_multiplier=-1).then_inc(s_tri, 1)

                @block.tensor
                def _(pe):
                    pe.wait_ge(s_w, 16 * len(loads))
                    pe.wait_ge(s_pad, 1)
                    for t in range(TILES):
                        last = nc.tensor.matmul(pl[:, t * E:(t + 1) * E], xT[:, t * P:(t + 1) * P], gw[:, :],
                                                start=True, stop=True)
                    last.then_inc(s_lg, 1)
                    pe.wait_ge(s_tri, 3)
                    pe.wait_ge(s_one, 1)
                    flat = one[:, :, :].rearrange("p t e -> p (t e)")
                    nc.tensor.matmul(pc[:, 0, :], upto[:, :], flat, start=True, stop=True)
                    nc.tensor.matmul(pc[:, 1, :], ones[:, :], flat, start=True, stop=True).then_inc(s_cum, 1)

                @block.scalar
                def _(act):
                    act.wait_ge(s_sub, 1)
                    nc.scalar.activation(pr[:, :, :], lg[:, :, :], ACT.Exp).then_inc(s_exp, 1)

                @block.vector
                def _(dve):
                    link = Link(dve, s_link)
                    nc.vector.memset(gw[D:P, :], 0.0).then_inc(s_pad, 1)
                    nc.vector.memset(w1[D:P, :], 0.0)
                    dve.wait_ge(s_rank, 1)
                    link(nc.vector.tensor_copy(rank[:, :], ranki[:, :]))
                    dve.wait_ge(s_lg, 1)
                    dve.wait_ge(s_w, 16 * len(loads))
                    link(nc.vector.tensor_tensor(lg[:, :, :], pl[:, :].rearrange("p (t e) -> p t e", e=E),
                                                 bcast(gb[:, :], 1, full), ALU.add))
                    link(nc.vector.tensor_reduce(t0[:, :], lg[:, :, :], AX.X, ALU.max))
                    nc.vector.tensor_tensor(lg[:, :, :], lg[:, :, :], bcast(t0[:, :], 2, full), ALU.subtract).then_inc(s_sub, 1)
                    dve.wait_ge(s_exp, 1)
                    link(nc.vector.tensor_reduce(t1[:, :], pr[:, :, :], AX.X, ALU.add))
                    link(nc.vector.reciprocal(t1[:, :], t1[:, :]))
                    link(nc.vector.tensor_tensor(pr[:, :, :], pr[:, :, :], bcast(t1[:, :], 2, full), ALU.mult))
                    link(nc.vector.tensor_reduce(t0[:, :], pr[:, :, :], AX.X, ALU.max))
                    link(nc.vector.tensor_tensor(lg[:, :, :], pr[:, :, :], bcast(t0[:, :], 2, full), ALU.is_equal))
                    link(nc.vector.tensor_tensor(lg[:, :, :], lg[:, :, :], bcast(rank[:, :], 1, full), ALU.mult))
                    link(nc.vector.tensor_reduce(t1[:, :], lg[:, :, :], AX.X, ALU.max))
                    nc.vector.tensor_tensor(one[:, :, :], lg[:, :, :], bcast(t1[:, :], 2, full), ALU.is_equal).then_inc(s_one, 1)
                    dve.wait_ge(s_cum, 1)
                    link(nc.vector.tensor_copy(run[0][:, :, :], pc[:, 1, :].rearrange("p (t e) -> p t e", e=E)))
                    at, step = 0, 1
                    while step < TILES:
                        nc.vector.tensor_copy(run[1 - at][:, 0:step, :], run[at][:, 0:step, :])
                        link(nc.vector.tensor_tensor(run[1 - at][:, step:, :], run[at][:, step:, :],
                                                     run[at][:, 0:TILES - step, :], ALU.add))
                        at, step = 1 - at, 2 * step
                    link(nc.vector.tensor_tensor(gate[:, :, :], run[at][:, :, :],
                                                 pc[:, 1, :].rearrange("p (t e) -> p t e", e=E), ALU.subtract))
                    link(nc.vector.tensor_tensor(gate[:, :, :], gate[:, :, :],
                                                 pc[:, 0, :].rearrange("p (t e) -> p t e", e=E), ALU.add))
                    link(nc.vector.tensor_scalar(gate[:, :, :], gate[:, :, :], float(CAP), None, ALU.is_le))
                    link(nc.vector.tensor_tensor(gate[:, :, :], gate[:, :, :], one[:, :, :], ALU.mult))
                    link(nc.vector.tensor_tensor(gate[:, :, :], gate[:, :, :], bcast(t0[:, :], 2, full), ALU.mult))

            with ExitStack() as c:
                mid = [[sb(f"mid{k}{a}", [P, CH], F32, c) for a in range(2)] for k in range(2)]
                y = sb("y", [P, TILES, D], F32, c)
                ye = [sb(f"ye{k}", [P, E, D], F32, c) for k in range(4)]
                fine = sb("fine", [P, TILES * D], F32, c)
                fini = sb("fini", [P, TILES * D], I32, c)
                ph = [[ps(f"ph{k}{a}", [P, CH], F32, c) for a in range(2)] for k in range(2)]
                py = ps("py", [P, 4, E * D], F32, c)
                s_h, s_relu, s_y, s_taken, s_link, s_sum = (sem("x" + n, c) for n in (
                    "s_h", "s_relu", "s_y", "s_taken", "s_link", "s_sum"))
                block = c.enter_context(nc.Block())
                GROUPS = TILES // 4

                @block.tensor
                def _(pe):
                    with pe.Fori(0, GROUPS) as g:
                        def widen(e):
                            for a in range(2):
                                last = nc.tensor.matmul(ph[e % 2][a][:, :], w1[:, e * F + a * P:e * F + (a + 1) * P],
                                                        xT[:, bass.ds(g * CH, CH)], start=True, stop=True)
                            last.then_inc(s_h, 1)

                        def narrow(e):
                            pe.wait_ge(s_relu, g * E + e + 1)
                            if e == 0:
                                pe.wait_ge(s_taken, 4 * g + 4)
                            for t in range(4):
                                for a in range(2):
                                    last = nc.tensor.matmul(py[:, t, e * D:(e + 1) * D], mid[e % 2][a][:, t * P:(t + 1) * P],
                                                            w2[:, e, a, :], start=(a == 0), stop=(a == 1))
                            if e == E - 1:
                                last.then_inc(s_y, 1)

                        widen(0)
                        for e in range(E):
                            if e + 1 < E:
                                widen(e + 1)
                            narrow(e)

                @block.scalar
                def _(act):
                    nc.scalar.preload_act_table(ACT.Relu)
                    with act.Fori(0, GROUPS) as g:
                        for e in range(E):
                            act.wait_ge(s_h, g * E + e + 1)
                            for a in range(2):
                                last = nc.scalar.activation(mid[e % 2][a][:, :], ph[e % 2][a][:, :], ACT.Relu,
                                                            bias=b1[:, 2 * e + a:2 * e + a + 1])
                            last.then_inc(s_relu, 1)

                @block.vector
                def _(dve):
                    link = Link(dve, s_link)
                    nc.vector.memset(fine[:, 0:1], 0.0).then_inc(s_taken, 4)
                    with dve.Fori(0, GROUPS) as g:
                        dve.wait_ge(s_y, g + 1)
                        for t in range(4):
                            nc.vector.tensor_tensor(ye[t][:, :, :], py[:, t, :].rearrange("p (e d) -> p e d", e=E),
                                                    b2[:, :].rearrange("p (e d) -> p e d", e=E), ALU.add).then_inc(s_taken, 1)
                        dve.wait_ge(s_taken, 4 * g + 8)
                        for t in range(4):
                            link.mark(nc.vector.tensor_tensor(ye[t][:, :, :], ye[t][:, :, :],
                                                              gate[:, bass.ds(4 * g + t, 1), :].rearrange("p a e -> p (a e)")
                                                              .unsqueeze(2).to_broadcast([P, E, D]), ALU.mult))
                        link.wait()
                        for t in range(4):
                            link.mark(nc.vector.tensor_reduce(y[:, bass.ds(4 * g + t, 1), :].rearrange("p a d -> p (a d)"),
                                                              ye[t][:, :, :].rearrange("p e d -> p d e"), AX.X, ALU.add))
                        link.restart()
                    yf = y[:, :, :].rearrange("p t d -> p (t d)")
                    yc = xn[:, :, :].rearrange("p t d -> p (t d)")
                    link(nc.vector.tensor_scalar(fini[:, :], yf, 0.0, 0.0, ALU.mult, ALU.is_equal))
                    link(nc.vector.tensor_tensor(fine[:, :], yf, yf, ALU.is_equal))
                    link(nc.vector.tensor_scalar(yc, yf, -1e4, 1e4, ALU.max, ALU.min))
                    link(nc.vector.tensor_tensor(yc, yc, fine[:, :], ALU.mult))
                    link(nc.vector.copy_predicated(yc, fini[:, :], yf))
                    nc.vector.tensor_tensor(h[:, :, :], h[:, :, :], xn[:, :, :], ALU.add).then_inc(s_sum, 1)

        with ExitStack() as c:
            norm_block("n3", c, h[:, :, :], [None])
        with ExitStack() as c:
            w3 = sb("w3", [P, 4, D], F32, c)
            dense_attention("a1", False, c, [(w3[0:D, :, :], A["L1_attn_wT"])], w3[D:P, :, :],
                            w3[:, 0:2, :].rearrange("c a d -> c (a d)"), w3[:, 2, :], w3[0:D, 3, :],
                            None, None, None, None, None, h, True)

        with ExitStack() as c:
            norm_block("n4", c, h[:, :, :], [None])
        with ExitStack() as c:
            memory(nc, A, out, c, sb, ps, sem, h, xT, ident, ident16, causal, s_started)


def memory(nc, A, out, c, sb, ps, sem, h, xT, ident, ident16, causal, s_started):
    W = 2 * D
    RING = 4
    CREDIT = RING
    keys = sb("keys", [P, HEADS // 2, N], F32, c)
    vals = sb("vals", [P, BT, HEADS, D], F32, c)
    rowbuf = [sb(f"rowbuf{r}", [P, TOPK, W], F32, c) for r in range(RING)]
    prob = [sb(f"prob{k}", [P, N], F32, c) for k in range(2)]
    probT = sb("probT", [P, N], F32, c)
    wq = sb("wq", [D, HEADS * D], F32, c)
    wo = sb("wo", [P, 4, D], F32, c)
    msim = sb("msim", [D, HEADS * 2 * NK], F32, c)
    xs = [sb(f"xs{k}", [D, P], F32, c) for k in range(2)]
    xsim = sb("xsim", [D, P], F32, c)
    qs = [sb(f"qs{k}", [P, P], F32, c) for k in range(2)]
    acc = sb("acc", [P, W], F32, c)
    nmax = sb("nmax", [P, 1], F32, c)
    rsum = sb("rsum", [P, 1], F32, c)
    rinv = sb("rinv", [P, 1], F32, c)
    ob = sb("ob", [P, HEADS * D], F32, c)
    obT = sb("obT", [P, 4 * P], F32, c)
    top = sb("top", [P, HEADS, 2, TOPK], F32, c)
    topi = sb("topi", [P, HEADS, 2, TOPK], U32, c)
    left = sb("left", [P, HEADS, NK], F32, c)
    key0 = sb("key0", [P, HEADS, TOPK], F32, c)
    key1 = sb("key1", [P, HEADS, TOPK], F32, c)
    headrow = sb("headrow", [P, HEADS, TOPK], F32, c)
    headi = sb("headi", [P, HEADS, TOPK], I32, c)
    cand = sb("cand", [P, HEADS, NC], F32, c)
    candi = sb("candi", [P, HEADS, NC], U16, c)
    cleft = sb("cleft", [P, 2, NC], F32, c)
    best = sb("best", [P, HEADS, TOPK], F32, c)
    bestd = sb("bestd", [P, HEADS, TOPK], F32, c)
    beste = sb("beste", [P, HEADS, TOPK], F32, c)
    bests = sb("bests", [P, HEADS], F32, c)
    spot = sb("spot", [P, HEADS, TOPK], U16, c)
    place = sb("place", [P, NC], U16, c)
    placei = sb("placei", [P, NC], I32, c)
    placefew = sb("placefew", [P, NFEW], U16, c)
    candfew = sb("candfew", [P, HEADS, NFEW], U16, c)
    HH = HEADS // 2
    hitfew = sb("hitfew", [P, HH, TOPK // 2, NFEW], U16, c)
    hit = sb("hit", [P, HH, TOPK // 2, NC], U16, c)
    row = [sb(f"row{k}", [P, HEADS, TOPK], U32, c) for k in range(2)]
    mixw = [sb(f"mixw{k}", [P, HEADS, TOPK], F32, c) for k in range(2)]

    with ExitStack() as cc:
        kd = sb("kd", [32, HEADS * 2, NK], F32, cc)
        wd = sb("wd", [32, HEADS * 2, D], F32, cc)
        pm = ps("pm", [D, HEADS * 2 * NK], F32, cc)
        s_w, s_m, s_mc, s_zero, s_iota = (sem("p" + n, cc) for n in ("s_w", "s_m", "s_mc", "s_zero", "s_iota"))
        block = cc.enter_context(nc.Block())
        loads = [(kd[:, :, :], A["pk_keysT"]), (wd[:, :, :], A["Wq_pkT"]), (wq[:, :], A["L1_ffn_Wq"]),
                 (wo[:, :, :], A["L1_ffn_Wo"].rearrange("(a p) d -> p a d", p=P))]

        @block.sync
        def _(sp):
            for to, frm in loads:
                sp.dma_start(to, frm).then_inc(s_w, 16)

        @block.tensor
        def _(pe):
            pe.wait_ge(s_w, 16 * len(loads))
            for m in range(HEADS * 2):
                last = nc.tensor.matmul(pm[:, m * NK:(m + 1) * NK], wd[:, m, :], kd[:, m, :], start=True, stop=True)
            last.then_inc(s_m, 1)

        @block.scalar
        def _(act):
            act.wait_ge(s_m, 1)
            for k in range(2):
                nc.scalar.activation(msim[:, k * CH:(k + 1) * CH], pm[:, k * CH:(k + 1) * CH], ACT.Copy).then_inc(s_mc, 1)

        @block.gpsimd
        def _(pool):
            nc.gpsimd.iota(headi[:, :, :], [[NK * NK, HEADS], [0, TOPK]], base=0, channel_multiplier=0).then_inc(s_iota, 1)
            nc.gpsimd.iota(placei[:, :], [[1, NC]], base=0, channel_multiplier=0).then_inc(s_iota, 1)
            nc.gpsimd.memset(vals[:, :, :, :], 0.0).then_inc(s_zero, 1)

        @block.vector
        def _(dve):
            dve.wait_ge(s_iota, 2)
            nc.vector.tensor_copy(headrow[:, :, :], headi[:, :, :])
            nc.vector.tensor_copy(place[:, :], placei[:, :])
            for few, at, n in FEW:
                nc.vector.tensor_copy(placefew[:, few:few + n], placei[:, at:at + n])
            nc.vector.memset(keys[:, :, :], 0.0)
            for k in range(2):
                nc.vector.memset(qs[k][(1 - k) * D:(2 - k) * D, :], 0.0)

    S = ps("S", [P, N], F32, c)
    tp = [ps(f"tp{k}", [P, CH], F32, c) for k in range(2)]
    psim = ps("psim", [P, CH], F32, c)
    mix = ps("mix", [P, CH], F32, c)
    Q, KT, O, PR = tp[0][0:D, 0:P], tp[1][0:D, 0:P], mix[:, 0:D], mix[:, P:P + D]
    s_xs, s_xsim, s_sim, s_top, s_q, s_qs, s_acc, s_kt, s_key, s_scores, s_max, s_prob, s_tp, s_tpc, s_o, s_rinv, s_ob = (
        sem("q" + n, c) for n in "s_xs s_xsim s_sim s_top s_q s_qs s_acc s_kt s_key s_scores s_max s_prob s_tp s_tpc s_o s_rinv s_ob".split())
    s_obt, s_obtc, s_pr, s_res, s_out, s_diff, s_wexp, s_row, s_scaled, s_link = (
        sem("q" + n, c) for n in "s_obt s_obtc s_pr s_res s_out s_diff s_wexp s_row s_scaled s_link".split())
    s_rows = [sem(f"s_rows{r}", c) for r in range(RING)]
    def side(hd):
        return slice(hd % 2 * D, hd % 2 * D + D)

    PIECES = 2
    STEPS, LATE = 3, 3
    EARLY = HEADS - STEPS
    LASTJ = TILES // 2 - 1
    block = c.enter_context(nc.Block())

    def turns(eng, tile):
        tile(0, 0, True, 2)
        tile(0, 1, False, 2)
        with eng.Fori(1, LASTJ) as j:
            tile(j, 0, False, 2)
            tile(j, 1, False, 2)
        tile(LASTJ, 0, False, 1)
        tile(LASTJ, 1, False, 0)

    @block.gpsimd
    def _(pool):
        def tile(j, k, first, more):
            t = 2 * j + k
            for hd in range(HEADS):
                if hd % HH == 0:
                    hold(pool, s_started, s_row, 2 * t + hd // HH + 1)
                hold(pool, s_started, s_acc, t * HEADS + hd + 1 - RING + CREDIT)
                for m in range(TOPK):
                    pool.indirect_dma_start(rowbuf[hd % RING][:, m, :], None, A["memory"],
                                            bass.IndirectOffsetOnAxis(ap=row[k][:, hd, m:m + 1], axis=0)
                                            ).then_inc(s_rows[hd % RING], 16)
        turns(pool, tile)

    @block.sync
    def _(sp):
        def tile(j, k, first, more):
            t = 2 * j + k
            sp.wait_ge(s_res, t + 1)
            sp.dma_start(out[bass.ds(t, 1), :, :].rearrange("a p d -> p (a d)"),
                         h[:, bass.ds(t, 1), :].rearrange("p a d -> p (a d)")).then_inc(s_out, 16)
        turns(sp, tile)
        sp.wait_ge(s_out, 16 * TILES)

    @block.scalar
    def _(act):
        nc.scalar.preload_act_table(ACT.Exp)

        def stage(t, k):
            nc.scalar.activation(xs[k][:, :], xT[0:D, bass.ds(t * P, P)], ACT.Copy).then_inc(s_xs, 1)

        def stage_ahead(t):
            nc.scalar.activation(xsim[:, :], xT[0:D, bass.ds(t * P, P)], ACT.Copy).then_inc(s_xsim, 1)

        def weights(t):
            act.wait_ge(s_diff, t + 1)
            nc.scalar.activation(beste[:, :, :], bestd[:, :, :], ACT.Exp).then_inc(s_wexp, 1)

        def scale_rows(t, k, hd):
            act.wait_ge(s_rows[hd % RING], 16 * TOPK * (t * (HEADS // RING) + hd // RING + 1))
            for m in range(TOPK):
                rows = rowbuf[hd % RING][:, m, :]
                last = nc.scalar.activation(rows, rows, ACT.Copy, scale=mixw[k][:, hd, m:m + 1])
            last.then_inc(s_scaled, 1)

        def exponentials(n, hd):
            act.wait_ge(s_max, n + 1)
            nc.scalar.activation(prob[hd % 2][:, :], S[:, :], ACT.Exp, bias=nmax[:, :], accum_out=rsum[:, :]
                                 ).then_inc(s_prob, 1)

        def attend(n, hd):
            for q in range(NCH):
                act.wait_ge(s_tp, NCH * n + q + 1)
                nc.scalar.activation(probT[:, q * CH:(q + 1) * CH], tp[q % 2][:, :], ACT.Copy).then_inc(s_tpc, 1)
            act.wait_ge(s_rinv, n + 1)
            act.wait_ge(s_o, n + 1)
            nc.scalar.activation(ob[:, hd * D:(hd + 1) * D], O, ACT.Copy, scale=rinv[:, :]).then_inc(s_ob, 1)

        def output(t):
            act.wait_ge(s_obt, t + 1)
            nc.scalar.activation(obT[:, :], tp[0][:, :], ACT.Copy).then_inc(s_obtc, 1)

        def tile(j, k, first, more):
            t = 2 * j + k
            tb = j % (BT // 2) * 2 + k
            for hd in range(HEADS):
                n = t * HEADS + hd
                if hd == 0 and more:
                    stage(t + 1, 1 - k)
                if not (first and hd == 0):
                    exponentials(n - 1, (hd - 1) % HEADS)
                if hd == 1 and more:
                    weights(t + 1)
                act.wait_ge(s_q, n + 1)
                nc.scalar.activation(qs[hd % 2][side(hd), :], Q, ACT.Copy, scale=float(D) ** -0.5).then_inc(s_qs, 1)
                act.wait_ge(s_acc, n + 1 + CREDIT)
                nc.scalar.activation(vals[:, bass.ds(tb, 1), hd, :].rearrange("p a d -> p (a d)"), acc[:, D:W], ACT.Copy)
                act.wait_ge(s_kt, n + 1)
                nc.scalar.activation(keys[side(hd), hd // 2, bass.ds(tb * P, P)], KT, ACT.Copy).then_inc(s_key, 1)
                if hd < HEADS - 1:
                    scale_rows(t, k, hd + 1)
                elif more:
                    scale_rows(t + 1, 1 - k, 0)
                if not (first and hd == 0):
                    attend(n - 1, (hd - 1) % HEADS)
                    if hd == 0:
                        output(t - 1)
                if hd == EARLY - 1 and more == 2:
                    stage_ahead(t + 2)

        stage(0, 0)
        stage_ahead(0)
        weights(0)
        act.wait_ge(s_sim, PIECES)
        stage_ahead(1)
        scale_rows(0, 0, 0)
        turns(act, tile)
        exponentials(TILES * HEADS - 1, HEADS - 1)
        attend(TILES * HEADS - 1, HEADS - 1)
        output(TILES - 1)

    @block.tensor
    def _(pe):
        def similarities(t, piece, first):
            n = t * PIECES + piece
            if piece == 0:
                pe.wait_ge(s_xsim, t + 1)
            if not first:
                pe.wait_ge(s_top, n)
            nc.tensor.matmul(psim[:, :], xsim[:, :], msim[:, piece * CH:(piece + 1) * CH],
                             start=True, stop=True).then_inc(s_sim, 1)

        def attend(n, hd):
            for q in range(NCH):
                if q >= 2:
                    pe.wait_ge(s_tpc, NCH * n + q - 1)
                for m in range(4):
                    last = nc.tensor.transpose(tp[q % 2][:, m * P:(m + 1) * P],
                                               prob[hd % 2][:, (4 * q + m) * P:(4 * q + m + 1) * P], ident[:, :])
                last.then_inc(s_tp, 1)
            for m in range(BT):
                if m % 4 == 0:
                    pe.wait_ge(s_tpc, NCH * n + m // 4 + 1)
                last = nc.tensor.matmul(O, probT[:, m * P:(m + 1) * P], vals[:, m, hd, :],
                                        start=(m == 0), stop=(m == BT - 1))
            last.then_inc(s_o, 1)

        def output(t):
            pe.wait_ge(s_ob, (t + 1) * HEADS)
            for m in range(4):
                last = nc.tensor.transpose(tp[0][:, m * P:(m + 1) * P], ob[:, m * P:(m + 1) * P], ident[:, :])
            last.then_inc(s_obt, 1)
            pe.wait_ge(s_obtc, t + 1)
            for m in range(4):
                last = nc.tensor.matmul(PR, obT[:, m * P:(m + 1) * P], wo[:, m, :], start=(m == 0), stop=(m == 3))
            last.then_inc(s_pr, 1)

        def tile(j, k, first, more):
            t = 2 * j + k
            tb = j % (BT // 2) * 2 + k
            for hd in range(HEADS):
                n = t * HEADS + hd
                if hd == 0:
                    hold(pe, s_started, s_xs, t + 1)
                if 0 <= hd - EARLY < PIECES and more == 2:
                    similarities(t + 2, hd - EARLY, False)
                nc.tensor.matmul(Q, wq[:, hd * D:(hd + 1) * D], xs[k][:, :], start=True, stop=True).then_inc(s_q, 1)
                hold(pe, s_started, s_acc, n + 1 + CREDIT)
                nc.tensor.transpose(KT, acc[:, 0:D], ident[:, :]).then_inc(s_kt, 1)
                pe.wait_ge(s_qs, n + 1)
                pe.wait_ge(s_key, n + 1)
                if not (first and hd == 0):
                    pe.wait_ge(s_prob, n)
                for q in range(NCH):
                    nc.tensor.matmul(S[:, q * CH:(q + 1) * CH], qs[hd % 2][:, :], keys[:, hd // 2, q * CH:(q + 1) * CH],
                                     start=True, stop=False)
                    last = nc.tensor.matmul(S[:, q * CH:(q + 1) * CH], ident16[:, :],
                                            causal[:, bass.ds(REACH - tb * P + q * CH, CH)], start=False, stop=True)
                last.then_inc(s_scores, 1)
                if hd == 1 and not first:
                    pe.wait_ge(s_res, t)
                if not (first and hd == 0):
                    attend(n - 1, (hd - 1) % HEADS)
                    if hd == 0:
                        output(t - 1)

        for t in range(2):
            for piece in range(PIECES):
                similarities(t, piece, t + piece == 0)
        turns(pe, tile)
        pe.wait_ge(s_prob, TILES * HEADS)
        attend(TILES * HEADS - 1, HEADS - 1)
        output(TILES - 1)

    @block.vector
    def _(dve):
        link = Link(dve, s_link)
        nc.vector.memset(acc[:, :], 0.0).then_inc(s_acc, CREDIT)
        dve.wait_ge(s_acc, CREDIT)

        def halves(t, piece):
            hold(dve, s_started, s_sim, t * PIECES + piece + 1)
            rows = [(HH * piece + m // 2, m % 2, psim[:, m * NK:(m + 1) * NK], left[:, m, :]) for m in range(HEADS)]
            for hd, p, src, rest in rows:
                link.mark(nc.vector.max(top[:, hd, p, 0:8], src))
            link.wait()
            for hd, p, src, rest in rows:
                link.mark(nc.vector.match_replace(rest, top[:, hd, p, 0:8], src, LOWEST))
            for hd, p, src, rest in rows:
                last = nc.vector.max_index(topi[:, hd, p, 0:8], top[:, hd, p, 0:8], src)
            last.then_inc(s_top, 1)
            link.wait()
            for hd, p, src, rest in rows:
                link.mark(nc.vector.max(top[:, hd, p, 8:16], rest))
            link.wait()
            for hd, p, src, rest in rows:
                link.mark(nc.vector.max_index(topi[:, hd, p, 8:16], top[:, hd, p, 8:16], rest))
            link.wait()

        def candidates():
            link.mark(nc.vector.tensor_copy(key0[:, :, :], topi[:, :, 0, :]))
            link(nc.vector.scalar_tensor_tensor(key1[:, :, :], topi[:, :, 1, :], float(NK), headrow[:, :, :],
                                                ALU.mult, ALU.add))
            at = 0
            for a, na, nb in PAIRS:
                shape = [P, HEADS, na, nb]
                for to, x, y in ((cand, top[:, :, 0, a:a + na], top[:, :, 1, 0:nb]),
                                 (candi, key0[:, :, a:a + na], key1[:, :, 0:nb])):
                    link.mark(nc.vector.tensor_tensor(to[:, :, at:at + na * nb].rearrange("p h (a b) -> p h a b", a=na),
                                                      x.unsqueeze(3).to_broadcast(shape), y.unsqueeze(2).to_broadcast(shape),
                                                      ALU.add))
                at += na * nb
            link.wait()
            for few, at, n in FEW:
                link.mark(nc.vector.tensor_copy(candfew[:, :, few:few + n], candi[:, :, at:at + n]))
            link.wait()

        def choose(heads):
            for pair in range(heads.start, heads.stop, 2):
                two = [(pair + m, cleft[:, m, :]) for m in range(2)]
                for hd, rest in two:
                    link.mark(nc.vector.max(best[:, hd, 0:8], cand[:, hd, :]))
                link.wait()
                for hd, rest in two:
                    link.mark(nc.vector.match_replace(rest, best[:, hd, 0:8], cand[:, hd, :], LOWEST))
                    link.mark(nc.vector.max_index(spot[:, hd, 0:8], best[:, hd, 0:8], cand[:, hd, :]))
                link.wait()
                for hd, rest in two:
                    link.mark(nc.vector.max(best[:, hd, 8:16], rest))
                link.wait()
                for hd, rest in two:
                    link.mark(nc.vector.max_index(spot[:, hd, 8:16], best[:, hd, 8:16], rest))
                link.wait()

        def less_largest():
            nc.vector.tensor_tensor(bestd[:, :, :], best[:, :, :], best[:, :, 0:1].to_broadcast([P, HEADS, TOPK]),
                                    ALU.subtract).then_inc(s_diff, 1)
            link.wait()

        def normalise(t, k):
            dve.wait_ge(s_wexp, t + 1)
            link(nc.vector.tensor_reduce(bests[:, :], beste[:, :, :], AX.X, ALU.add))
            link(nc.vector.reciprocal(bests[:, :], bests[:, :]))
            link(nc.vector.tensor_tensor(mixw[k][:, :, :], beste[:, :, :], bcast(bests[:, :], 2, [P, HEADS, TOPK]), ALU.mult))

        def find_rows(t, k, half):
            hs = slice(half * HH, (half + 1) * HH)
            H8 = TOPK // 2
            parts = ((hitfew, 0, NFEW, placefew, candfew), (hit, H8, NC, place, candi))
            for hits, r, n, places, rows in parts:
                link.mark(nc.vector.tensor_tensor(hits[:, :, :, :], bcast(spot[:, hs, r:r + H8], 3, [P, HH, H8, n]),
                                                  places[:, :].unsqueeze(1).unsqueeze(1).to_broadcast([P, HH, H8, n]),
                                                  ALU.is_equal))
            link.wait()
            for hits, r, n, places, rows in parts:
                link.mark(nc.vector.tensor_tensor(hits[:, :, :, :], hits[:, :, :, :], bcast(rows[:, hs, :], 2, [P, HH, H8, n]),
                                                  ALU.mult))
            link.wait()
            for hits, r, n, places, rows in parts:
                last = nc.vector.tensor_reduce(row[k][:, hs, r:r + H8], hits[:, :, :, :], AX.X, ALU.max)
            last.then_inc(s_row, 1)
            dve.wait_ge(s_row, 2 * t + half + 1)

        def begin(t, step):
            if step < PIECES:
                halves(t, step)
            else:
                candidates()
                choose(range(0, HH))

        def finish(t, k, step):
            if step == 0:
                choose(range(HH, HEADS))
                less_largest()
            elif step == 1:
                normalise(t, k)
                find_rows(t, k, 0)
            else:
                find_rows(t, k, 1)

        def mix(n, hd):
            dve.wait_ge(s_scaled, n + 1)
            nc.vector.tensor_reduce(acc[:, :], rowbuf[hd % RING][:, :, :].rearrange("p m w -> p w m"), AX.X,
                                    ALU.add).then_inc(s_acc, 1)

        def reciprocal(n):
            dve.wait_ge(s_prob, n + 1)
            nc.vector.reciprocal(rinv[:, :], rsum[:, :]).then_inc(s_rinv, 1)

        def output(t):
            dve.wait_ge(s_pr, t + 1)
            at = h[:, bass.ds(t, 1), :].rearrange("p a d -> p (a d)")
            nc.vector.tensor_tensor(at, PR, at, ALU.add).then_inc(s_res, 1)

        def tile(j, k, first, more):
            t = 2 * j + k
            for hd in range(HEADS):
                n = t * HEADS + hd
                if more or hd < HEADS - 1:
                    mix(n + 1, (hd + 1) % HEADS)
                if hd == 1 and not first:
                    output(t - 1)
                dve.wait_ge(s_scores, n + 1)
                nc.vector.tensor_reduce(nmax[:, :], S[:, :], AX.X, ALU.max, negate=True).then_inc(s_max, 1)
                if hd < LATE and more:
                    finish(t + 1, 1 - k, hd)
                if hd >= EARLY and more == 2:
                    begin(t + 2, hd - EARLY)
                reciprocal(n)
            link.restart()

        for step in range(STEPS):
            begin(0, step)
        for step in range(LATE):
            finish(0, 0, step)
        link.restart()
        for step in range(STEPS):
            begin(1, step)
        link.restart()
        mix(0, 0)
        turns(dve, tile)
        output(TILES - 1)


def kernel(**inputs):
    import numpy as np
    import concourse.bacc as bacc
    from concourse.bass_utils import run_bass_kernel_spmd as run

    nc = bacc.Bacc("TRN2", target_bir_lowering=False, num_devices=1)
    a = {k: np.asarray(v) for k, v in inputs.items()}
    arrays = {
        "ids": a["x"].reshape(TILES, P).T,
        "ple": a["L0_tok_ple_table"].reshape(VOCAB * PLE // D, D),
        "qkv_b_cols": a["L0_attn_qkv_b"].reshape(3, D).T,
        "scale": a["L0_attn_scale"].reshape(1),
        "b1_cols": a["L0_ffn_b1"].reshape(2 * E, P).T,
        "L1_attn_wT": np.stack([a["L1_attn_W" + n].T for n in "qkvo"], axis=1),
        "pk_keysT": a["L1_ffn_pk_keys"].transpose(3, 2, 0, 1).reshape(32, 2 * HEADS, NK),
        "Wq_pkT": a["L1_ffn_Wq_pk"].reshape(D, 2, HEADS, 32).transpose(3, 2, 1, 0).reshape(32, 2 * HEADS, D),
        "memory": np.concatenate([a["L1_ffn_keys_table"], a["L1_ffn_values_table"]], axis=1),
    }
    for name in ("L0_attn_bias_table L0_attn_ln1_g L0_attn_ln1_b L0_attn_qkv_b L0_attn_qkv_w L0_attn_proj_w L0_attn_proj_b "
                 "L0_attn_ln2_g L0_attn_ln2_b L0_ffn_gate_w L0_ffn_gate_b L0_ffn_w1 L0_ffn_w2 L0_ffn_b2 L1_ffn_Wq "
                 "L1_ffn_Wo").split():
        arrays[name] = a[name]
    arrays = {k: np.ascontiguousarray(v) for k, v in arrays.items()}
    A = {k: nc.dram_tensor("in_" + k, v.shape, mybir.dt.from_np(v.dtype), kind="ExternalInput").ap()
         for k, v in arrays.items()}
    out = nc.dram_tensor("out", (TILES, P, D), F32, kind="ExternalOutput").ap()
    build(nc, A, out)
    r = run(nc, [{"in_" + k: v for k, v in arrays.items()}], core_ids=[0])
    return r.results[0]["out"].reshape(B, N, D)
```

```python
from contextlib import ExitStack

import concourse.bass as bass
from concourse import mybir

ALU = mybir.AluOpType
ACT = mybir.ActivationFunctionType
AX = mybir.AxisListType
F32 = mybir.dt.float32
BF16 = mybir.dt.bfloat16
I32 = mybir.dt.int32
U32 = mybir.dt.uint32
U16 = mybir.dt.uint16

P = 128
D = 64
B, N = 2, 2048
TILES = B * N // P
BT = N // P
CH = 512
NCH = N // CH
VOCAB, PLE = 32000, 512
PLE_START = 3 * 64
EPS = 1e-5
E, F = 8, 256
CAP = 5 * B * N // (4 * E)
HEADS, NK, TOPK = 8, 64, 16
RING = 4
REACH = N - P
WIDE = REACH + N
FAR = -1e30
LOWEST = -3.0e38

PAIRS = [(0, 1, 16), (1, 1, 8), (2, 2, 5), (4, 4, 3), (8, 8, 1)]
NC = sum(na * nb for _, na, nb in PAIRS)
FEW = [(0, 0, 8), (8, 16, 4), (12, 24, 2), (14, 29, 2), (16, 34, 1), (17, 37, 1), (18, 40, 1), (19, 43, 1)]
NFEW = 20


def bcast(ap, axis, shape):
    return ap.unsqueeze(axis).to_broadcast(shape)


class Link:

    def __init__(self, eng, sem):
        self.eng, self.sem, self.n = eng, sem, 0

    def __call__(self, ins):
        self.mark(ins)
        self.wait()

    def mark(self, ins):
        self.n += 1
        ins.then_inc(self.sem, 1)

    def wait(self):
        self.eng.wait_ge(self.sem, self.n)

    def restart(self):
        self.eng.wait_ge(self.sem, self.n)
        self.eng.sem_clear(self.sem)
        self.n = 0


def hold(eng, started, sem, value):
    value = eng.to_reg(value)
    eng.wait_ge(started, 1)
    eng.wait_ge(sem, value)


def build(nc, A, out):
    with ExitStack() as whole:
        def sb(name, shape, dt=F32, ctx=whole):
            return ctx.enter_context(nc.sbuf_tensor(name, shape, dt))

        def ps(name, shape, dt=F32, ctx=whole):
            return ctx.enter_context(nc.psum_tensor(name, shape, dt))

        def sem(name, ctx=whole):
            return ctx.enter_context(nc.semaphore(name))

        h = sb("h", [P, TILES, D])
        xn = sb("xn", [P, TILES, D])
        xT = sb("xT", [P, TILES * P])
        st = sb("st", [P, 4, TILES])
        ident = sb("ident", [P, P])
        ident16 = sb("ident16", [P, P], BF16)
        causal = sb("causal", [P, WIDE], BF16)
        rc = sb("rc", [P, BT])
        s_started = sem("s_started")
        s_tok = [sem(f"s_tok{n}") for n in range(4)]
        s_put = sem("s_put")
        s_dev, s_sq, s_var, s_std, s_norm, s_tr, s_cp, s_nlink, s_vecs = (sem(n) for n in (
            "s_dev", "s_sq", "s_var", "s_std", "s_norm", "s_tr", "s_cp", "s_nlink", "s_vecs"))
        seen = {"chunks": 0, "pairs": 0, "groups": 0}
        s_take = [sem(f"s_take{n}") for n in range(4)]
        s_gathered = [sem(f"s_gathered{n}") for n in range(RING)]
        slots_in = nc.dram_tensor("slots_in", (E * CAP + B * N, D), F32, kind="Internal").ap()
        slots_out = nc.dram_tensor("slots_out", (E * CAP, D), F32, kind="Internal").ap()

        rows = sb("rows", [P, TILES], U32)
        with ExitStack() as c:
            ids = sb("ids", [P, TILES], I32, c)
            idf = sb("idf", [P, TILES], F32, c)
            wrap = sb("wrap", [P, TILES], F32, c)
            rci = sb("rci", [P, BT], I32, c)
            s_ids, s_rows, s_link, s_iota, s_fill = (sem(n, c) for n in (
                "s_ids", "s_rows", "s_link0", "s_iota", "s_fill"))
            block = c.enter_context(nc.Block())

            @block.sync
            def _(sp):
                sp.dma_start(ids[:, :], A["ids"]).then_inc(s_ids, 16)

            @block.vector
            def _(dve):
                link = Link(dve, s_link)
                dve.wait_ge(s_ids, 16)
                link(nc.vector.tensor_copy(idf[:, :], ids[:, :]))
                link(nc.vector.tensor_scalar(wrap[:, :], idf[:, :], 0.0, float(VOCAB), ALU.is_lt, ALU.mult))
                link(nc.vector.tensor_tensor(idf[:, :], idf[:, :], wrap[:, :], ALU.add))
                link(nc.vector.tensor_scalar(idf[:, :], idf[:, :], 0.0, float(VOCAB - 1), ALU.max, ALU.min))
                nc.vector.tensor_scalar(rows[:, :], idf[:, :], float(PLE // D), float(PLE_START // D),
                                        ALU.mult, ALU.add).then_inc(s_rows, 1)
                dve.wait_ge(s_iota, 1)
                nc.vector.memset(xT[D:P, :], 0.0)
                link(nc.vector.tensor_scalar(rc[:, :], rci[:, :], 1.0, None, ALU.max))
                link(nc.vector.reciprocal(rc[:, :], rc[:, :]))

            @block.gpsimd
            def _(pool):
                nc.gpsimd.iota(rci[:, :], [[P, BT]], base=0, channel_multiplier=1).then_inc(s_iota, 1)
                nc.gpsimd.memset(ident[:, :], 0.0).then_inc(s_fill, 1)
                nc.gpsimd.memset(ident16[:, :], 0.0).then_inc(s_fill, 1)
                nc.gpsimd.memset(causal[:, :], 0.0).then_inc(s_fill, 1)
                pool.wait_ge(s_fill, 3)
                nc.gpsimd.affine_select(out=ident[:, :], in_=ident[:, :], compare_op=ALU.not_equal, fill=1.0,
                                        base=0, pattern=[[-1, P]], channel_multiplier=1)
                nc.gpsimd.affine_select(out=ident16[:, :], in_=ident16[:, :], compare_op=ALU.not_equal, fill=1.0,
                                        base=0, pattern=[[-1, P]], channel_multiplier=1)
                nc.gpsimd.affine_select(out=causal[:, :], in_=causal[:, :], compare_op=ALU.is_ge, fill=FAR,
                                        base=REACH, pattern=[[-1, WIDE]], channel_multiplier=1).then_inc(s_started, 1)

        def biased_attention(c, load, w0, wp, qkb, v_bias, proj_bias, table, scale, dest):
            qT = sb("a0qT", [D, B * N], F32, c)
            kT = sb("a0kT", [P, B * N], F32, c)
            v = sb("a0v", [P, TILES, D], F32, c)
            qs = [sb(f"a0qs{k}", [P, P], F32, c) for k in range(2)]
            prob = [sb(f"a0prob{k}", [P, N], F32, c) for k in range(2)]
            probT = sb("a0probT", [P, N], F32, c)
            biased = sb("a0biased", [P, N], F32, c)
            nmax = [sb(f"a0nmax{k}", [P, 1], F32, c) for k in range(2)]
            rsum = [sb(f"a0rsum{k}", [P, 1], F32, c) for k in range(2)]
            rinv = [sb(f"a0rinv{k}", [P, 2], F32, c) for k in range(2)]
            ob = sb("a0ob", [P, D], F32, c)
            obT = sb("a0obT", [D, P], F32, c)
            S = ps("a0S", [P, N], F32, c)
            tp = [ps(f"a0tp{k}", [P, CH], F32, c) for k in range(2)]
            mix = [ps(f"a0mix{k}", [P, CH], F32, c) for k in range(2)]
            O, OT, PR = mix[0][:, 0:D], mix[1][0:D, P:2 * P], mix[1][:, 0:D]

            with ExitStack() as cc:
                s_w, s_qk, s_qkc, s_v, s_vc, s_pad = (sem("a0" + n, cc) for n in ("s_w", "s_qk", "s_qkc", "s_v", "s_vc", "s_pad"))
                block = cc.enter_context(nc.Block())
                nload = len(load)

                @block.sync
                def _(sp):
                    for dst, src in load:
                        sp.dma_start(dst, src).then_inc(s_w, 16)
                    sp.wait_ge(s_w, 16 * nload)

                @block.tensor
                def _(pe):
                    pe.wait_ge(s_w, 16 * nload)
                    pe.wait_ge(s_pad, 1)
                    for g in range(TILES * P // CH):
                        if g >= 2:
                            pe.wait_ge(s_qkc, 2 * (g - 1))
                        nc.tensor.matmul(tp[g % 2][:, :], w0[:, 0:2 * D], xT[:, g * CH:(g + 1) * CH],
                                         start=True, stop=True).then_inc(s_qk, 1)
                    for g in range(TILES // 8):
                        for k in range(8):
                            last = nc.tensor.matmul(S[:, g * CH + k * D:g * CH + (k + 1) * D],
                                                    xT[:, (8 * g + k) * P:(8 * g + k + 1) * P], w0[:, 2 * D:3 * D],
                                                    start=True, stop=True)
                        last.then_inc(s_v, 1)

                @block.scalar
                def _(act):
                    for g in range(TILES * P // CH):
                        act.wait_ge(s_qk, g + 1)
                        for k, dst in ((0, qT), (1, kT)):
                            nc.scalar.activation(dst[0:D, g * CH:(g + 1) * CH], tp[g % 2][k * D:(k + 1) * D, :],
                                                 ACT.Identity, bias=qkb[:, k:k + 1]).then_inc(s_qkc, 1)

                @block.vector
                def _(dve):
                    nc.vector.memset(w0[D:P, :], 0.0).then_inc(s_pad, 1)
                    for pad in (kT, qs[0], qs[1]):
                        nc.vector.memset(pad[D:P, :], 0.0)
                    for g in range(TILES // 8):
                        dve.wait_ge(s_v, g + 1)
                        nc.vector.tensor_tensor(v[:, 8 * g:8 * g + 8, :], S[:, g * CH:(g + 1) * CH].rearrange("p (k d) -> p k d", d=D),
                                                bcast(v_bias, 1, [P, 8, D]), ALU.add).then_inc(s_vc, 1)

            names = "s_qs s_scores s_read s_max s_prob s_tp s_tpc s_o s_ob s_obt s_obs s_proj s_link s_done"
            (s_qs, s_scores, s_read, s_max, s_prob, s_tp, s_tpc, s_o, s_ob, s_obt, s_obs, s_proj, s_link,
             s_done) = (sem("a0" + n, c) for n in names.split())
            block = c.enter_context(nc.Block())
            LASTJ = TILES // 2 - 1

            def turns(eng, item, turned=lambda: None):
                item(0, 0, True, 2)
                item(0, 1, False, 2)
                turned()
                with eng.Fori(1, LASTJ) as j:
                    item(j, 0, False, 2)
                    item(j, 1, False, 2)
                    turned()
                item(LASTJ, 0, False, 1)
                item(LASTJ, 1, False, 0)

            def after(j, k):
                return j + (k + 1) // 2, (k + 1) % 2

            def start(j):
                return j // (BT // 2) * N

            @block.scalar
            def _(act):
                nc.scalar.preload_act_table(ACT.Exp)

                def stage(j, k):
                    nc.scalar.activation(qs[k][0:D, :], qT[:, bass.ds((2 * j + k) * P, P)], ACT.Copy).then_inc(s_qs, 1)

                def weights(j, k):
                    act.wait_ge(s_max, 2 * j + k + 1)
                    nc.scalar.activation(prob[k][:, :], biased[:, :], ACT.Exp, bias=nmax[k][:, :],
                                         accum_out=rsum[k][:, :]).then_inc(s_prob, 1)

                def turn_over(i):
                    act.wait_ge(s_obt, i + 1)
                    nc.scalar.activation(obT[:, :], OT, ACT.Copy).then_inc(s_obs, 1)

                def item(j, k, first, more):
                    i = 2 * j + k
                    if more == 2:
                        stage(j + 1, k)
                    if not first:
                        turn_over(i - 1)
                    for q in range(NCH):
                        act.wait_ge(s_tp, NCH * i + q + 1)
                        nc.scalar.activation(probT[:, q * CH:(q + 1) * CH], tp[q % 2][:, :], ACT.Copy).then_inc(s_tpc, 1)
                    if more:
                        weights(*after(j, k))

                stage(0, 0)
                stage(0, 1)
                weights(0, 0)
                turns(act, item)
                turn_over(TILES - 1)

            @block.tensor
            def _(pe):
                def scores(j, k, wait_read):
                    pe.wait_ge(s_qs, 2 * j + k + 1)
                    if wait_read:
                        pe.wait_ge(s_read, 2 * j + k)
                    for q in range(NCH):
                        last = nc.tensor.matmul(S[:, q * CH:(q + 1) * CH], qs[k][:, :],
                                                kT[:, bass.ds(start(j) + q * CH, CH)], start=True, stop=True)
                    last.then_inc(s_scores, 1)

                def turn_over(i):
                    hold(pe, s_started, s_ob, i + 1)
                    nc.tensor.transpose(OT, ob[:, :], ident[:, :]).then_inc(s_obt, 1)

                def project(i):
                    pe.wait_ge(s_obs, i + 1)
                    nc.tensor.matmul(PR, obT[:, :], wp[:, :], start=True, stop=True).then_inc(s_proj, 1)

                def item(j, k, first, more):
                    i = 2 * j + k
                    batch = j // (BT // 2) * BT
                    if more:
                        scores(*after(j, k), True)
                    if not first:
                        turn_over(i - 1)
                    pe.wait_ge(s_prob, i + 1)
                    for q in range(NCH):
                        if q >= 2:
                            pe.wait_ge(s_tpc, NCH * i + q - 1)
                        for m in range(4):
                            last = nc.tensor.transpose(tp[q % 2][:, m * P:(m + 1) * P],
                                                       prob[k][:, (4 * q + m) * P:(4 * q + m + 1) * P], ident[:, :])
                        last.then_inc(s_tp, 1)
                    if not first:
                        project(i - 1)
                    for m in range(BT):
                        if m % 4 == 0:
                            pe.wait_ge(s_tpc, NCH * i + m // 4 + 1)
                        last = nc.tensor.matmul(O, probT[:, m * P:(m + 1) * P],
                                                v[:, bass.ds(batch + m, 1), :].rearrange("p a d -> p (a d)"),
                                                start=(m == 0), stop=(m == BT - 1))
                    last.then_inc(s_o, 1)

                scores(0, 0, False)
                turns(pe, item)
                turn_over(TILES - 1)
                project(TILES - 1)

            @block.vector
            def _(dve):
                link = Link(dve, s_link)

                def soften(j, k):
                    i = 2 * j + k
                    tb = j % (BT // 2) * 2 + k
                    dve.wait_ge(s_scores, i + 1)
                    nc.vector.tensor_tensor(biased[:, :], S[:, :], table[:, bass.ds(REACH - tb * P, N)],
                                            ALU.add).then_inc(s_read, 1)
                    dve.wait_ge(s_read, i + 1)
                    nc.vector.tensor_reduce(nmax[k][:, :], biased[:, :], AX.X, ALU.max, negate=True).then_inc(s_max, 1)

                def projected(i):
                    dve.wait_ge(s_proj, i + 1)
                    nc.vector.tensor_tensor(dest[:, bass.ds(i, 1), :].rearrange("p a d -> p (a d)"), PR, proj_bias,
                                            ALU.add).then_inc(s_done, 1)

                def item(j, k, first, more):
                    i = 2 * j + k
                    dve.wait_ge(s_prob, i + 1)
                    link(nc.vector.reciprocal(rinv[k][:, 0:1], rsum[k][:, :]))
                    link(nc.vector.tensor_tensor(rinv[k][:, 1:2], rinv[k][:, 0:1], scale, ALU.mult))
                    if more:
                        soften(*after(j, k))
                    if not first:
                        projected(i - 1)
                    dve.wait_ge(s_o, i + 1)
                    nc.vector.tensor_scalar(ob[:, :], O, rinv[k][:, 1:2], None, ALU.mult).then_inc(s_ob, 1)

                soften(0, 0)
                turns(dve, item, link.restart)
                projected(TILES - 1)

        def relu_attention(c, b, w3, bufs, banks, sems, beside=None):
            TG = CH // P
            GROUPS = BT // TG
            BLOCKS = TG * GROUPS * (GROUPS + 1) // 2
            BELOW = BLOCKS - BT

            def below(g):
                return TG * g * (g - 1) // 2

            (s_w, s_pad, s_fill, s_tri, s_v, s_vc, s_qk, s_qkc, s_scores, s_relu, s_diag, s_o, s_ob, s_obt, s_obs, s_proj,
             s_res) = sems
            qT, kT, v, probT, tri, ob, obT = bufs
            S, O, OT, PR = banks
            block = c.enter_context(nc.Block())

            if b == 0:
                @block.sync
                def _(sp):
                    sp.dma_start(w3[0:D, :, :], A["L1_attn_wT"]).then_inc(s_w, 16)

            @block.gpsimd
            def _(pool):
                if beside:
                    beside(pool)
                if b == 0:
                    nc.gpsimd.memset(tri[:, :], 1.0).then_inc(s_fill, 1)
                    pool.wait_ge(s_fill, 1)
                    nc.gpsimd.affine_select(out=tri[:, :], in_=tri[:, :], compare_op=ALU.is_ge, fill=0.0,
                                            base=0, pattern=[[1, P]], channel_multiplier=-1).then_inc(s_tri, 1)

            @block.tensor
            def _(pe):
                def scores(b, g):
                    for m in range(TG * (g + 1)):
                        first = max(m - TG * g, 0) * P
                        bank = m % NCH * CH
                        if m >= NCH:
                            pe.wait_ge(s_relu, b * BELOW + below(g) + m - NCH + 1)
                        elif g > 0:
                            pe.wait_ge(s_diag, b * BT + TG * (g - 1) + m + 1)
                        nc.tensor.matmul(S[:, bank + first:bank + CH], kT[:, m * P:(m + 1) * P],
                                         qT[:, g * CH + first:(g + 1) * CH], start=True, stop=True).then_inc(s_scores, 1)

                def mixed(b, g):
                    if g > 0:
                        pe.wait_ge(s_relu, b * BELOW + below(g + 1))
                    pe.wait_ge(s_diag, b * BT + TG * (g + 1))
                    for u in range(TG):
                        for m in range(TG * g + u + 1):
                            last = nc.tensor.matmul(O[:, u * D:(u + 1) * D], probT[g % 2][:, m, u * P:(u + 1) * P],
                                                    v[:, m, :],
                                                    start=(m == 0), stop=(m == TG * g + u))
                    last.then_inc(s_o, 1)

                def turn_over(b, g):
                    pe.wait_ge(s_ob, b * GROUPS + g + 1)
                    for u in range(TG):
                        last = nc.tensor.transpose(OT[0:D, u * P:(u + 1) * P], ob[:, u, :], ident[:, :])
                    last.then_inc(s_obt, 1)

                def project(b, g):
                    if g > 0:
                        pe.wait_ge(s_res, b * GROUPS + g)
                    pe.wait_ge(s_obs, b * GROUPS + g + 1)
                    for u in range(TG):
                        last = nc.tensor.matmul(PR[:, u * D:(u + 1) * D], obT[:, u * P:(u + 1) * P], w3[0:D, 3, :],
                                                start=True, stop=True)
                    last.then_inc(s_proj, 1)

                pe.wait_ge(s_w, 16)
                pe.wait_ge(s_pad, 1)
                for g in range(BT // 8):
                    for k in range(8):
                        t = b * BT + 8 * g + k
                        last = nc.tensor.matmul(S[:, g * CH + k * D:g * CH + (k + 1) * D], xT[:, t * P:(t + 1) * P], w3[:, 2, :],
                                                start=True, stop=True)
                    last.then_inc(s_v, 1)
                pe.wait_ge(s_vc, (b + 1) * (BT // 8))
                for g in range(NCH):
                    nc.tensor.matmul(S[:, g * CH:(g + 1) * CH], w3[:, 0:2, :].rearrange("c a d -> c (a d)"),
                                     xT[:, b * N + g * CH:b * N + (g + 1) * CH], start=True, stop=True).then_inc(s_qk, 1)
                pe.wait_ge(s_qkc, 2 * NCH * b + 2 * NCH)
                for g in range(GROUPS):
                    scores(b, g)
                    if g >= 2:
                        turn_over(b, g - 2)
                    if g >= 1:
                        mixed(b, g - 1)
                    if g >= 2:
                        project(b, g - 2)
                turn_over(b, GROUPS - 2)
                mixed(b, GROUPS - 1)
                project(b, GROUPS - 2)
                turn_over(b, GROUPS - 1)
                project(b, GROUPS - 1)

            @block.scalar
            def _(act):
                nc.scalar.preload_act_table(ACT.Relu)

                def turned(b, g):
                    act.wait_ge(s_obt, b * GROUPS + g + 1)
                    nc.scalar.activation(obT[:, :], OT[0:D, :], ACT.Copy).then_inc(s_obs, 1)

                for g in range(NCH):
                    act.wait_ge(s_qk, b * NCH + g + 1)
                    for k, to in enumerate((qT, kT)):
                        nc.scalar.activation(to[0:D, g * CH:(g + 1) * CH], S[k * D:(k + 1) * D, g * CH:(g + 1) * CH],
                                             ACT.Copy).then_inc(s_qkc, 1)
                for g in range(GROUPS):
                    for m in range(TG * g):
                        act.wait_ge(s_scores, b * BLOCKS + below(g) + TG * g + m + 1)
                        nc.scalar.activation(probT[g % 2][:, m, :], S[:, m % NCH * CH:(m % NCH + 1) * CH],
                                             ACT.Relu).then_inc(s_relu, 1)
                    if g >= 2:
                        turned(b, g - 2)
                turned(b, GROUPS - 2)
                turned(b, GROUPS - 1)

            @block.vector
            def _(dve):
                if b == 0:
                    nc.vector.memset(w3[D:P, :, :], 0.0).then_inc(s_pad, 1)
                    nc.vector.memset(kT[D:P, :], 0.0)
                    nc.vector.memset(qT[D:P, :], 0.0)
                for g in range(BT // 8):
                    dve.wait_ge(s_v, b * (BT // 8) + g + 1)
                    nc.vector.tensor_copy(v[:, 8 * g:8 * g + 8, :], S[:, g * CH:(g + 1) * CH].rearrange("p (k d) -> p k d", d=D)
                                          ).then_inc(s_vc, 1)
                dve.wait_ge(s_tri, 1)

                def divided(b, g):
                    dve.wait_ge(s_o, b * GROUPS + g + 1)
                    nc.vector.tensor_tensor(ob[:, :, :], O[:, 0:TG * D].rearrange("p (u d) -> p u d", d=D),
                                            bcast(rc[:, TG * g:TG * (g + 1)], 2, [P, TG, D]), ALU.mult).then_inc(s_ob, 1)

                def residual(b, g):
                    dve.wait_ge(s_proj, b * GROUPS + g + 1)
                    at = h[:, b * BT + TG * g:b * BT + TG * (g + 1), :]
                    nc.vector.tensor_tensor(at, PR[:, 0:TG * D].rearrange("p (u d) -> p u d", d=D), at,
                                            ALU.add).then_inc(s_res, 1)

                for g in range(GROUPS):
                    for r in range(TG):
                        m = TG * g + r
                        src = S[:, r * CH:(r + 1) * CH]
                        dve.wait_ge(s_scores, b * BLOCKS + below(g) + TG * g + m + 1)
                        last = nc.vector.scalar_tensor_tensor(probT[g % 2][:, m, r * P:(r + 1) * P],
                                                              src[:, r * P:(r + 1) * P], 0.0, tri[:, :], ALU.max, ALU.mult)
                        if r < TG - 1:
                            last = nc.vector.tensor_scalar(probT[g % 2][:, m, (r + 1) * P:], src[:, (r + 1) * P:],
                                                           0.0, None, ALU.max)
                        last.then_inc(s_diag, 1)
                    if g >= 1:
                        divided(b, g - 1)
                    if g >= 2:
                        residual(b, g - 2)
                divided(b, GROUPS - 1)
                residual(b, GROUPS - 2)
                residual(b, GROUPS - 1)

        def norm_block(name, c, src, affines, add_to=None, load=(), transpose=True, fetch=None, arrived=None,
                       beside=None, sq=None, tp=None, pairs=range(TILES // 16)):
            CHUNK = 8
            if sq is None:
                sq = sb(name + "sq", [P, TILES, D], F32, c)
            if tp is None:
                tp = [ps(f"{name}tp{k}", [P, CH], F32, c) for k in range(2)]
            mark = sb(name + "mark", [P, 1], F32, c)
            block = c.enter_context(nc.Block())
            chunks0, pairs0, groups0 = seen["chunks"], seen["pairs"], seen["groups"]
            seen["chunks"] += len(affines) * 2 * len(pairs)
            seen["pairs"] += len(pairs)
            seen["groups"] += 4 * len(pairs) if transpose else 0
            rounds = [(chunks0 + 2 * (len(affines) * k + n), n, (2 * pair, 2 * pair + 1))
                      for k, pair in enumerate(pairs) for n in range(len(affines))]
            groups = [4 * pair + k for pair in pairs for k in range(4)]

            def tiles(ch):
                return slice(ch * CHUNK, (ch + 1) * CHUNK)

            if load or beside:
                @block.sync
                def _(sp):
                    for to, frm in load:
                        sp.dma_start(to, frm).then_inc(s_vecs, 16)
                    if beside:
                        beside[0](sp)

            if fetch:
                @block.gpsimd
                def _(pool):
                    fetch(pool)

            @block.vector
            def _(dve):
                link = Link(dve, s_nlink)
                part = [P, CHUNK, D]
                if load:
                    dve.wait_ge(s_vecs, 16 * len(load))
                if beside:
                    beside[1](dve)
                for at, n, chs in rounds:
                    frm = src if n == 0 else xn[:, :, :]
                    for ch in chs:
                        if arrived and n == 0:
                            dve.wait_ge(arrived[ch], 16 * CHUNK)
                        link.mark(nc.vector.tensor_reduce(st[:, 0, tiles(ch)], frm[:, tiles(ch), :], AX.X, ALU.add))
                    link.wait()
                    for ch in chs:
                        link.mark(nc.vector.tensor_scalar(st[:, 0, tiles(ch)], st[:, 0, tiles(ch)], 1.0 / D, None, ALU.mult))
                    link.wait()
                    for ch in chs:
                        nc.vector.tensor_tensor(xn[:, tiles(ch), :], frm[:, tiles(ch), :], bcast(st[:, 0, tiles(ch)], 2, part),
                                                ALU.subtract).then_inc(s_dev, 1)
                    for k, ch in enumerate(chs):
                        dve.wait_ge(s_sq, at + k + 1)
                        link(nc.vector.tensor_reduce(st[:, 1, tiles(ch)], sq[:, tiles(ch), :], AX.X, ALU.add))
                        nc.vector.tensor_scalar(st[:, 1, tiles(ch)], st[:, 1, tiles(ch)], 1.0 / D, EPS,
                                                ALU.mult, ALU.add).then_inc(s_var, 1)
                    for k, ch in enumerate(chs):
                        dve.wait_ge(s_std, at + k + 1)
                        link.mark(nc.vector.reciprocal(st[:, 3, tiles(ch)], st[:, 2, tiles(ch)]))
                    link.wait()
                    steps = [(xn, lambda ch: bcast(st[:, 3, tiles(ch)], 2, part), ALU.mult)]
                    if affines[n]:
                        steps += [(xn, lambda ch: bcast(affines[n][0], 1, part), ALU.mult),
                                  (xn, lambda ch: bcast(affines[n][1], 1, part), ALU.add)]
                    if add_to is not None and n == len(affines) - 1:
                        steps += [(add_to, lambda ch: add_to[:, tiles(ch), :], ALU.add)]
                    for to, other, op in steps:
                        for ch in chs:
                            link.mark(nc.vector.tensor_tensor(to[:, tiles(ch), :], xn[:, tiles(ch), :], other(ch), op))
                        link.wait()
                    if n == len(affines) - 1:
                        nc.vector.memset(mark[:, :], 0.0).then_inc(s_norm, 1)
                if beside:
                    beside[2](dve)
                link.restart()

            @block.scalar
            def _(act):
                for at, n, chs in rounds:
                    for k, ch in enumerate(chs):
                        act.wait_ge(s_dev, at + k + 1)
                        nc.scalar.activation(sq[:, tiles(ch), :], xn[:, tiles(ch), :], ACT.Square).then_inc(s_sq, 1)
                    for k, ch in enumerate(chs):
                        act.wait_ge(s_var, at + k + 1)
                        nc.scalar.activation(st[:, 2, tiles(ch)], st[:, 1, tiles(ch)], ACT.Sqrt).then_inc(s_std, 1)
                if transpose:
                    for k, g in enumerate(groups):
                        act.wait_ge(s_tr, groups0 + k + 1)
                        nc.scalar.activation(xT[0:D, g * CH:(g + 1) * CH], tp[g % 2][0:D, :], ACT.Copy).then_inc(s_cp, 1)

            if transpose:
                @block.tensor
                def _(pe):
                    for n, g in enumerate(groups):
                        pe.wait_ge(s_norm, pairs0 + n // 4 + 1)
                        if n >= 2:
                            pe.wait_ge(s_cp, groups0 + n - 1)
                        for k in range(4):
                            last = nc.tensor.transpose(tp[g % 2][0:D, k * P:(k + 1) * P], xn[:, 4 * g + k, :], ident[:, :])
                        last.then_inc(s_tr, 1)

        with ExitStack() as l0:
            LX = 1152
            table = sb("table", [P, WIDE], F32, l0)
            vecs = sb("vecs", [P, 6, D], F32, l0)
            scale = sb("scale", [P, 1], F32, l0)
            qkb = sb("qkb", [D, 3], F32, l0)
            w0 = sb("w0", [P, 3 * D], F32, l0)
            wp = sb("wp", [D, D], F32, l0)
            ao = sb("ao", [P, TILES, D], F32, l0)
            shear = nc.dram_tensor("shear", (P * LX,), F32, kind="Internal").ap()
            with ExitStack() as c:
                line = sb("line", [P, LX], F32, c)
                s_line, s_long, s_out, s_back, s_fill, s_clear = (sem(n, c) for n in (
                    "s_line", "s_long", "s_sheared", "s_back", "s_tabled", "s_clear"))
                known = A["L0_attn_bias_table"].shape[0]
                row = lambda n: A[n].partition_broadcast(P)

                def gather_tokens(pool):
                    for t in range(TILES):
                        pool.indirect_dma_start(h[:, t, :], None, A["ple"],
                                                bass.IndirectOffsetOnAxis(ap=rows[:, t:t + 1], axis=0)).then_inc(s_tok[t // 8], 16)

                def table_loads(sp):
                    sp.dma_start(line[:, 0:known], row("L0_attn_bias_table")).then_inc(s_line, 16)
                    sp.wait_ge(s_line, 16)
                    part = E * CAP // 2
                    for k in range(2):
                        sp.dma_start(slots_in[k * part:(k + 1) * part, :].rearrange("(p n) d -> p (n d)", p=P - D),
                                     xT[D:P, 0:part * D // (P - D)]).then_inc(s_clear, 16)
                    sp.wait_ge(s_long, 1)
                    sp.dma_start(shear.rearrange("(p n) -> p n", n=LX), line[:, :]).then_inc(s_out, 16)
                    sp.wait_ge(s_out, 16)
                    sp.dma_start(table[:, 0:1024], shear[0:P * (LX - 1)].rearrange("(p n) -> p n", n=LX - 1)[:, P - 1:P - 1 + 1024]
                                 ).then_inc(s_back, 16)
                    sp.wait_ge(s_clear, 32)

                def lengthen(dve):
                    dve.wait_ge(s_line, 16)
                    nc.vector.tensor_copy(line[:, known:LX], line[:, known - 1:known].to_broadcast([P, LX - known])).then_inc(s_long, 1)

                def table_end(dve):
                    dve.wait_ge(s_back, 16)
                    nc.vector.tensor_copy(table[:, 1024:WIDE], table[:, 1023:1024].to_broadcast([P, WIDE - 1024])).then_inc(s_fill, 1)

                norm_block("n0", c, h[:, :, :], [None, (vecs[:, 0, :], vecs[:, 1, :])], load=[
                    (vecs[:, 0, :], row("L0_attn_ln1_g")), (vecs[:, 1, :], row("L0_attn_ln1_b")),
                    (vecs[:, 2, :], A["L0_attn_qkv_b"][2 * D:3 * D].partition_broadcast(P)),
                    (vecs[:, 3, :], row("L0_attn_proj_b")),
                    (vecs[:, 4, :], row("L0_attn_ln2_g")), (vecs[:, 5, :], row("L0_attn_ln2_b")),
                    (scale[:, :], row("scale"))], fetch=gather_tokens, arrived=s_tok,
                    beside=(table_loads, lengthen, table_end))
            with ExitStack() as c:
                biased_attention(c, [(w0[0:D, :], A["L0_attn_qkv_w"]), (wp[:, :], A["L0_attn_proj_w"]),
                                     (qkb[:, :], A["qkv_b_cols"])], w0, wp, qkb, vecs[:, 2, :], vecs[:, 3, :],
                                 table, scale[:, :], ao)
            with ExitStack() as c:
                norm_block("n1", c, ao[:, :, :], [(vecs[:, 4, :], vecs[:, 5, :])], add_to=h[:, :, :], transpose=False)

        with ExitStack() as c:
            norm_block("n2", c, h[:, :, :], [None])
        with ExitStack() as moe:
            gw = sb("gw", [P, E], F32, moe)
            gb = sb("gb", [P, E], F32, moe)
            w1 = sb("w1", [P, E * F], F32, moe)
            w2 = sb("w2", [P, E, 2, D], F32, moe)
            b1 = sb("b1", [P, 2 * E], F32, moe)
            b2 = sb("b2", [P, E * D], F32, moe)
            rank = sb("rank", [P, E], F32, moe)
            ranki = sb("ranki", [P, E], I32, moe)
            upto = sb("upto", [P, P], F32, moe)
            ones = sb("ones", [P, P], F32, moe)
            lg = sb("lg", [P, TILES, E], F32, moe)
            pr = sb("pr", [P, TILES, E], F32, moe)
            one = sb("one", [P, TILES, E], F32, moe)
            run = [sb(f"run{k}", [P, TILES, E], F32, moe) for k in range(2)]
            gate = sb("gate", [P, TILES, E], F32, moe)
            t0 = sb("t0", [P, TILES], F32, moe)
            t1 = sb("t1", [P, TILES], F32, moe)
            keep = sb("keep", [P, TILES], F32, moe)
            slot = sb("slot", [P, TILES], F32, moe)
            put = sb("put", [P, TILES], U32, moe)
            take = sb("take", [P, TILES], U32, moe)
            weight = sb("weight", [P, TILES], F32, moe)
            firsti = sb("firsti", [P, E], I32, moe)
            first = sb("first", [P, E], F32, moe)
            sparei = sb("sparei", [P, TILES], I32, moe)
            spare = sb("spare", [P, TILES], F32, moe)
            full = [P, TILES, E]
            with ExitStack() as c:
                pl = ps("pl", [P, TILES * E], F32, c)
                pc = ps("pc", [P, 2, TILES * E], F32, c)
                s_w, s_lg, s_sub, s_exp, s_one, s_cum, s_link, s_tri, s_rank, s_pad = (sem("m" + n, c) for n in (
                    "s_w", "s_lg", "s_sub", "s_exp", "s_one", "s_cum", "s_link", "s_tri", "s_rank", "s_pad"))
                block = c.enter_context(nc.Block())
                loads = [(gw[0:D, :], A["L0_ffn_gate_w"]), (gb[:, :], A["L0_ffn_gate_b"].partition_broadcast(P)),
                         (w1[0:D, :].rearrange("d (e f) -> d e f", e=E), A["L0_ffn_w1"].rearrange("e d f -> d e f")),
                         (w2[:, :, :, :].rearrange("p e a d -> p (e a) d"),
                          A["L0_ffn_w2"].rearrange("e (a p) d -> p (e a) d", p=P)),
                         (b1[:, :], A["b1_cols"]), (b2[:, :], A["L0_ffn_b2"].rearrange("e d -> (e d)").partition_broadcast(P))]

                @block.sync
                def _(sp):
                    for to, frm in loads:
                        sp.dma_start(to, frm).then_inc(s_w, 16)
                    sp.wait_ge(s_w, 16 * len(loads))

                @block.gpsimd
                def _(pool):
                    nc.gpsimd.iota(ranki[:, :], [[-1, E]], base=E, channel_multiplier=0)
                    nc.gpsimd.iota(firsti[:, :], [[CAP, E]], base=-1, channel_multiplier=0)
                    nc.gpsimd.iota(sparei[:, :], [[P, TILES]], base=E * CAP, channel_multiplier=1).then_inc(s_rank, 1)
                    nc.gpsimd.memset(upto[:, :], 1.0).then_inc(s_tri, 1)
                    nc.gpsimd.memset(ones[:, :], 1.0).then_inc(s_tri, 1)
                    pool.wait_ge(s_tri, 2)
                    nc.gpsimd.affine_select(out=upto[:, :], in_=upto[:, :], compare_op=ALU.is_ge, fill=0.0,
                                            base=0, pattern=[[1, P]], channel_multiplier=-1).then_inc(s_tri, 1)

                @block.tensor
                def _(pe):
                    pe.wait_ge(s_w, 16 * len(loads))
                    pe.wait_ge(s_pad, 1)
                    for t in range(TILES):
                        last = nc.tensor.matmul(pl[:, t * E:(t + 1) * E], xT[:, t * P:(t + 1) * P], gw[:, :],
                                                start=True, stop=True)
                    last.then_inc(s_lg, 1)
                    pe.wait_ge(s_tri, 3)
                    pe.wait_ge(s_one, 1)
                    flat = one[:, :, :].rearrange("p t e -> p (t e)")
                    nc.tensor.matmul(pc[:, 0, :], upto[:, :], flat, start=True, stop=True)
                    nc.tensor.matmul(pc[:, 1, :], ones[:, :], flat, start=True, stop=True).then_inc(s_cum, 1)

                @block.scalar
                def _(act):
                    act.wait_ge(s_sub, 1)
                    nc.scalar.activation(pr[:, :, :], lg[:, :, :], ACT.Exp).then_inc(s_exp, 1)

                @block.vector
                def _(dve):
                    link = Link(dve, s_link)
                    nc.vector.memset(gw[D:P, :], 0.0).then_inc(s_pad, 1)
                    nc.vector.memset(w1[D:P, :], 0.0)
                    dve.wait_ge(s_rank, 1)
                    nc.vector.tensor_copy(first[:, :], firsti[:, :])
                    nc.vector.tensor_copy(spare[:, :], sparei[:, :])
                    link(nc.vector.tensor_copy(rank[:, :], ranki[:, :]))
                    dve.wait_ge(s_lg, 1)
                    dve.wait_ge(s_w, 16 * len(loads))
                    link(nc.vector.tensor_tensor(lg[:, :, :], pl[:, :].rearrange("p (t e) -> p t e", e=E),
                                                 bcast(gb[:, :], 1, full), ALU.add))
                    link(nc.vector.tensor_reduce(t0[:, :], lg[:, :, :], AX.X, ALU.max))
                    nc.vector.tensor_tensor(lg[:, :, :], lg[:, :, :], bcast(t0[:, :], 2, full), ALU.subtract).then_inc(s_sub, 1)
                    dve.wait_ge(s_exp, 1)
                    link(nc.vector.tensor_reduce(t1[:, :], pr[:, :, :], AX.X, ALU.add))
                    link(nc.vector.reciprocal(t1[:, :], t1[:, :]))
                    link(nc.vector.tensor_tensor(pr[:, :, :], pr[:, :, :], bcast(t1[:, :], 2, full), ALU.mult))
                    link(nc.vector.tensor_reduce(t0[:, :], pr[:, :, :], AX.X, ALU.max))
                    link(nc.vector.tensor_tensor(lg[:, :, :], pr[:, :, :], bcast(t0[:, :], 2, full), ALU.is_equal))
                    link(nc.vector.tensor_tensor(lg[:, :, :], lg[:, :, :], bcast(rank[:, :], 1, full), ALU.mult))
                    link(nc.vector.tensor_reduce(t1[:, :], lg[:, :, :], AX.X, ALU.max))
                    nc.vector.tensor_tensor(one[:, :, :], lg[:, :, :], bcast(t1[:, :], 2, full), ALU.is_equal).then_inc(s_one, 1)
                    dve.wait_ge(s_cum, 1)
                    link(nc.vector.tensor_copy(run[0][:, :, :], pc[:, 1, :].rearrange("p (t e) -> p t e", e=E)))
                    at, step = 0, 1
                    while step < TILES:
                        nc.vector.tensor_copy(run[1 - at][:, 0:step, :], run[at][:, 0:step, :])
                        link(nc.vector.tensor_tensor(run[1 - at][:, step:, :], run[at][:, step:, :],
                                                     run[at][:, 0:TILES - step, :], ALU.add))
                        at, step = 1 - at, 2 * step
                    link(nc.vector.tensor_tensor(gate[:, :, :], run[at][:, :, :],
                                                 pc[:, 1, :].rearrange("p (t e) -> p t e", e=E), ALU.subtract))
                    link(nc.vector.tensor_tensor(gate[:, :, :], gate[:, :, :],
                                                 pc[:, 0, :].rearrange("p (t e) -> p t e", e=E), ALU.add))
                    link(nc.vector.tensor_tensor(gate[:, :, :], gate[:, :, :], one[:, :, :], ALU.mult))
                    link.mark(nc.vector.tensor_reduce(t1[:, :], gate[:, :, :], AX.X, ALU.add))
                    link(nc.vector.tensor_tensor(lg[:, :, :], one[:, :, :], bcast(first[:, :], 1, full), ALU.mult))
                    link.mark(nc.vector.tensor_scalar(keep[:, :], t1[:, :], float(CAP), None, ALU.is_le))
                    link(nc.vector.tensor_reduce(slot[:, :], lg[:, :, :], AX.X, ALU.add))
                    link.mark(nc.vector.tensor_tensor(weight[:, :], keep[:, :], t0[:, :], ALU.mult))
                    link(nc.vector.tensor_tensor(slot[:, :], slot[:, :], t1[:, :], ALU.add))
                    link(nc.vector.tensor_scalar(slot[:, :], slot[:, :], 0.0, float(E * CAP - 1), ALU.max, ALU.min))
                    link.mark(nc.vector.tensor_tensor(take[:, :], slot[:, :], keep[:, :], ALU.mult))
                    link(nc.vector.tensor_tensor(slot[:, :], slot[:, :], spare[:, :], ALU.subtract))
                    link(nc.vector.tensor_tensor(slot[:, :], slot[:, :], keep[:, :], ALU.mult))
                    link(nc.vector.tensor_tensor(put[:, :], slot[:, :], spare[:, :], ALU.add))

            with ExitStack() as c:
                RUN = CAP // P
                REST = CAP - CH
                xe = sb("xe", [P, E, RUN, D], F32, c)
                xeT = sb("xeT", [P, E * CAP], F32, c)
                mid = [sb(f"mid{k}", [P, 2, CAP], F32, c) for k in range(2)]
                ye = sb("ye", [P, E, RUN, D], F32, c)
                y = sb("y", [P, TILES, D], F32, c)
                CHUNK = 8
                fine = sb("fine", [P, CHUNK * D], F32, c)
                fini = sb("fini", [P, CHUNK * D], I32, c)
                ph = [ps(f"ph{k}", [P, 3, CH], F32, c) for k in range(2)]
                py = [ps(f"py{k}", [P, CH], F32, c) for k in range(2)]
                s_pad, s_turned, s_turnc, s_h, s_relu, s_y, s_ye, s_back, s_link = (
                    sem("x" + n, c) for n in "s_pad s_turned s_turnc s_h s_relu s_y s_ye s_back s_link".split())
                s_xe = [sem(f"xs_xe{n}", c) for n in range(2)]
                block = c.enter_context(nc.Block())

                def part(k, a):
                    return ph[k][:, a, :], ph[k][:, 2, a * REST:(a + 1) * REST]

                @block.gpsimd
                def _(pool):
                    for t in range(TILES):
                        pool.indirect_dma_start(slots_in, bass.IndirectOffsetOnAxis(ap=put[:, t:t + 1], axis=0),
                                                xn[:, t, :], None).then_inc(s_put, 16)
                    pool.wait_ge(s_back, 16 * E)
                    for t in range(TILES):
                        pool.indirect_dma_start(y[:, t, :], None, slots_out,
                                                bass.IndirectOffsetOnAxis(ap=take[:, t:t + 1], axis=0)).then_inc(s_take[t // CHUNK], 16)

                @block.sync
                def _(sp):
                    sp.wait_ge(s_put, 16 * TILES)
                    for n in range(2):
                        es = slice(n * E // 2, (n + 1) * E // 2)
                        sp.dma_start(xe[:, es, :, :].rearrange("p e k d -> p e (k d)"),
                                     slots_in[es.start * CAP:es.stop * CAP, :].rearrange("(e p k) d -> p e (k d)", p=P, k=RUN)
                                     ).then_inc(s_xe[n], 16)
                    for e in range(E):
                        sp.wait_ge(s_ye, e + 1)
                        sp.dma_start(slots_out[e * CAP:(e + 1) * CAP, :].rearrange("(p k) d -> p (k d)", p=P),
                                     ye[:, e, :, :].rearrange("p k d -> p (k d)")).then_inc(s_back, 16)
                    sp.wait_ge(s_back, 16 * E)

                @block.tensor
                def _(pe):
                    def turn(g):
                        pe.wait_ge(s_xe[(4 * g + 3) // (E // 2 * RUN)], 16)
                        if g >= 2:
                            pe.wait_ge(s_turnc, g - 1)
                        for i in range(4 * g, 4 * g + 4):
                            last = nc.tensor.transpose(py[g % 2][0:D, i % 4 * P:(i % 4 + 1) * P], xe[:, i // RUN, i % RUN, :],
                                                       ident[:, :])
                        last.then_inc(s_turned, 1)

                    def widen(e):
                        for a in range(2):
                            for to, at, n in zip(part(e % 2, a), (0, CH), (CH, REST)):
                                last = nc.tensor.matmul(to, w1[:, e * F + a * P:e * F + (a + 1) * P],
                                                        xeT[:, e * CAP + at:e * CAP + at + n], start=True, stop=True)
                        last.then_inc(s_h, 1)

                    def narrow(e):
                        pe.wait_ge(s_relu, e + 1)
                        if e >= 2:
                            pe.wait_ge(s_ye, e - 1)
                        for k in range(RUN):
                            for a in range(2):
                                last = nc.tensor.matmul(py[e % 2][:, k * D:(k + 1) * D], mid[e % 2][:, a, k * P:(k + 1) * P],
                                                        w2[:, e, a, :], start=(a == 0), stop=(a == 1))
                        last.then_inc(s_y, 1)

                    for g in range(E * RUN // 4):
                        turn(g)
                    pe.wait_ge(s_turnc, E * RUN // 4)
                    pe.wait_ge(s_pad, 1)
                    widen(0)
                    for e in range(E):
                        if e + 1 < E:
                            widen(e + 1)
                        narrow(e)

                @block.scalar
                def _(act):
                    nc.scalar.preload_act_table(ACT.Relu)
                    for g in range(E * RUN // 4):
                        act.wait_ge(s_turned, g + 1)
                        nc.scalar.activation(xeT[0:D, g * CH:(g + 1) * CH], py[g % 2][0:D, :], ACT.Copy).then_inc(s_turnc, 1)
                    for e in range(E):
                        act.wait_ge(s_h, e + 1)
                        for a in range(2):
                            for frm, at, n in zip(part(e % 2, a), (0, CH), (CH, REST)):
                                last = nc.scalar.activation(mid[e % 2][:, a, at:at + n], frm, ACT.Relu,
                                                            bias=b1[:, 2 * e + a:2 * e + a + 1])
                        last.then_inc(s_relu, 1)

                @block.vector
                def _(dve):
                    link = Link(dve, s_link)
                    nc.vector.memset(xeT[D:P, :], 0.0).then_inc(s_pad, 1)
                    for e in range(E):
                        dve.wait_ge(s_y, e + 1)
                        nc.vector.tensor_tensor(ye[:, e, :, :], py[e % 2][:, 0:RUN * D].rearrange("p (k d) -> p k d", d=D),
                                                bcast(b2[:, e * D:(e + 1) * D], 1, [P, RUN, D]), ALU.add).then_inc(s_ye, 1)
                    for n in range(TILES // CHUNK):
                        ts = slice(n * CHUNK, (n + 1) * CHUNK)
                        yf = y[:, ts, :].rearrange("p t d -> p (t d)")
                        yc = xn[:, ts, :].rearrange("p t d -> p (t d)")
                        hf = h[:, ts, :].rearrange("p t d -> p (t d)")
                        if n == 0:
                            dve.wait_ge(s_put, 16 * TILES)
                        dve.wait_ge(s_take[n], 16 * CHUNK)
                        link(nc.vector.tensor_tensor(y[:, ts, :], y[:, ts, :], bcast(weight[:, ts], 2, [P, CHUNK, D]), ALU.mult))
                        link.mark(nc.vector.tensor_scalar(fini[:, :], yf, 0.0, 0.0, ALU.mult, ALU.is_equal))
                        link.mark(nc.vector.tensor_tensor(fine[:, :], yf, yf, ALU.is_equal))
                        link(nc.vector.tensor_scalar(yc, yf, -1e4, 1e4, ALU.max, ALU.min))
                        link(nc.vector.tensor_tensor(yc, yc, fine[:, :], ALU.mult))
                        link(nc.vector.copy_predicated(yc, fini[:, :], yf))
                        link(nc.vector.tensor_tensor(hf, hf, yc, ALU.add))

        with ExitStack() as c:
            norm_block("n3", c, h[:, :, :], [None])
        with ExitStack() as c:
            memory(nc, A, out, c, sb, ps, sem, h, xT, ident, ident16, causal, s_started, s_gathered, norm_block,
                   relu_attention)


def memory(nc, A, out, c, sb, ps, sem, h, xT, ident, ident16, causal, s_started, s_gathered, norm_block,
           relu_attention):
    W = 2 * D
    CREDIT = RING
    keys = sb("keys", [P, HEADS // 2, N], F32, c)
    vals = sb("vals", [P, BT, HEADS, D], F32, c)
    rowbuf = [sb(f"rowbuf{r}", [P, TOPK, W], F32, c) for r in range(RING)]
    prob = [sb(f"prob{k}", [P, N], F32, c) for k in range(2)]
    probT = sb("probT", [P, N], F32, c)
    wq = sb("wq", [D, HEADS * D], F32, c)
    wo = sb("wo", [P, 4, D], F32, c)
    msim = sb("msim", [D, HEADS * 2 * NK], F32, c)
    xs = [sb(f"xs{k}", [D, P], F32, c) for k in range(2)]
    xsim = sb("xsim", [D, P], F32, c)
    qs = [sb(f"qs{k}", [P, P], F32, c) for k in range(2)]
    acc = sb("acc", [P, W], F32, c)
    nmax = sb("nmax", [P, 1], F32, c)
    rsum = sb("rsum", [P, 1], F32, c)
    rinv = sb("rinv", [P, 1], F32, c)
    ob = sb("ob", [P, HEADS * D], F32, c)
    obT = sb("obT", [P, 4 * P], F32, c)
    top = sb("top", [P, HEADS, 2, TOPK], F32, c)
    topi = sb("topi", [P, HEADS, 2, TOPK], U32, c)
    left = sb("left", [P, HEADS, NK], F32, c)
    key0 = sb("key0", [P, HEADS, TOPK], F32, c)
    key1 = sb("key1", [P, HEADS, TOPK], F32, c)
    headrow = sb("headrow", [P, HEADS, TOPK], F32, c)
    headi = sb("headi", [P, HEADS, TOPK], I32, c)
    cand = sb("cand", [P, HEADS, NC], F32, c)
    candi = sb("candi", [P, HEADS, NC], U16, c)
    cleft = sb("cleft", [P, 2, NC], F32, c)
    best = sb("best", [P, HEADS, TOPK], F32, c)
    bestd = sb("bestd", [P, HEADS, TOPK], F32, c)
    beste = sb("beste", [P, HEADS, TOPK], F32, c)
    bests = sb("bests", [P, HEADS], F32, c)
    spot = sb("spot", [P, HEADS, TOPK], U16, c)
    place = sb("place", [P, NC], U16, c)
    placei = sb("placei", [P, NC], I32, c)
    placefew = sb("placefew", [P, NFEW], U16, c)
    candfew = sb("candfew", [P, HEADS, NFEW], U16, c)
    HH = HEADS // 2
    hitfew = sb("hitfew", [P, HH, TOPK // 2, NFEW], U16, c)
    hit = sb("hit", [P, HH, TOPK // 2, NC], U16, c)
    row = [sb(f"row{k}", [P, HEADS, TOPK], U32, c) for k in range(2)]
    mixw = [sb(f"mixw{k}", [P, HEADS, TOPK], F32, c) for k in range(2)]

    kd = sb("kd", [32, HEADS * 2, NK], F32, c)
    wd = sb("wd", [32, HEADS * 2, D], F32, c)
    S = ps("S", [P, N], F32, c)
    tp = [ps(f"tp{k}", [P, CH], F32, c) for k in range(2)]
    psim = ps("psim", [P, CH], F32, c)
    mix = ps("mix", [P, CH], F32, c)
    Q, KT, O, PR = tp[0][0:D, 0:P], tp[1][0:D, 0:P], mix[:, 0:D], mix[:, P:P + D]
    s_xs, s_xsim, s_sim, s_top, s_q, s_qs, s_acc, s_kt, s_key, s_scores, s_max, s_prob, s_tp, s_tpc, s_o, s_rinv, s_ob = (
        sem("q" + n, c) for n in "s_xs s_xsim s_sim s_top s_q s_qs s_acc s_kt s_key s_scores s_max s_prob s_tp s_tpc s_o s_rinv s_ob".split())
    s_obt, s_obtc, s_pr, s_res, s_out, s_diff, s_wexp, s_row, s_scaled, s_link = (
        sem("q" + n, c) for n in "s_obt s_obtc s_pr s_res s_out s_diff s_wexp s_row s_scaled s_link".split())
    STEPS, LATE = 3, 3
    EARLY = HEADS - STEPS
    PIECES = 2
    s_w, s_m, s_mc, s_iota, s_fill = (sem("p" + n, c) for n in ("s_w", "s_m", "s_mc", "s_iota", "s_fill"))

    w3 = sb("w3", [P, 4, D], F32, c)
    relu = [w3, [prob[0], prob[1], probT[:, 0:BT * D].rearrange("p (t d) -> p t d", d=D),
                 [keys[:, :, :].rearrange("p a n -> p (a n)").rearrange("p (t n) -> p t n", n=CH),
                  vals[:, :, :, :].rearrange("p t a d -> p t (a d)")],
                 sb("a1tri", [P, P], F32, c), sb("a1ob", [P, CH // P, D], F32, c), sb("a1obT", [D, CH], F32, c)],
            (S, tp[0], tp[1], mix),
            [sem("a1" + n, c) for n in ("s_w s_pad s_fill s_tri s_v s_vc s_qk s_qkc s_scores s_relu s_diag "
                                        "s_o s_ob s_obt s_obs s_proj s_res").split()]]
    with ExitStack() as cc:
        relu_attention(cc, 0, *relu)

    loads = [(kd[:, :, :], A["pk_keysT"]), (wd[:, :, :], A["Wq_pkT"]), (wq[:, :], A["L1_ffn_Wq"]),
             (wo[:, :, :], A["L1_ffn_Wo"].rearrange("(a p) d -> p a d", p=P))]
    sqs = rowbuf[0][:, :, :].rearrange("p m w -> p (m w)").rearrange("p (t d) -> p t d", d=D)

    def numbers(pool):
        nc.gpsimd.iota(headi[:, :, :], [[NK * NK, HEADS], [0, TOPK]], base=0, channel_multiplier=0).then_inc(s_iota, 1)
        nc.gpsimd.iota(placei[:, :], [[1, NC]], base=0, channel_multiplier=0).then_inc(s_iota, 1)
        for buf in (acc[:, :], qs[0][:, :], qs[1][:, :]):
            nc.gpsimd.memset(buf, 0.0).then_inc(s_fill, 1)

    def load_all(sp):
        for to, frm in loads:
            sp.dma_start(to, frm).then_inc(s_w, 16)
        sp.wait_ge(s_w, 16 * len(loads))

    def places(dve):
        dve.wait_ge(s_iota, 2)
        nc.vector.tensor_copy(headrow[:, :, :], headi[:, :, :])
        nc.vector.tensor_copy(place[:, :], placei[:, :])
        for few, at, n in FEW:
            nc.vector.tensor_copy(placefew[:, few:few + n], placei[:, at:at + n])

    with ExitStack() as cc:
        norm_block("n4", cc, h[:, :, :], [None], fetch=numbers, beside=(load_all, places, lambda dve: None),
                   sq=sqs, tp=tp, pairs=(0,))

    def gather(pool, k, hd):
        for m in range(TOPK):
            pool.indirect_dma_start(rowbuf[hd % RING][:, m, :], None, A["memory"],
                                    bass.IndirectOffsetOnAxis(ap=row[k][:, hd, m:m + 1], axis=0)
                                    ).then_inc(s_gathered[hd % RING], 16)

    def stage_on(act, t, k):
        nc.scalar.activation(xs[k][:, :], xT[0:D, bass.ds(t * P, P)], ACT.Copy).then_inc(s_xs, 1)

    def stage_ahead_on(act, t):
        nc.scalar.activation(xsim[:, :], xT[0:D, bass.ds(t * P, P)], ACT.Copy).then_inc(s_xsim, 1)

    def weights_on(act, t):
        act.wait_ge(s_diff, t + 1)
        nc.scalar.activation(beste[:, :, :], bestd[:, :, :], ACT.Exp).then_inc(s_wexp, 1)

    def similarities(pe, t, piece, first):
        n = t * PIECES + piece
        if piece == 0:
            pe.wait_ge(s_xsim, t + 1)
        if not first:
            pe.wait_ge(s_top, n)
        nc.tensor.matmul(psim[:, :], xsim[:, :], msim[:, piece * CH:(piece + 1) * CH],
                         start=True, stop=True).then_inc(s_sim, 1)

    def choosing(dve, link):
        def halves(t, piece):
            hold(dve, s_started, s_sim, t * PIECES + piece + 1)
            rows = [(HH * piece + m // 2, m % 2, psim[:, m * NK:(m + 1) * NK], left[:, m, :]) for m in range(HEADS)]
            for hd, p, src, rest in rows:
                link.mark(nc.vector.max(top[:, hd, p, 0:8], src))
            link.wait()
            for hd, p, src, rest in rows:
                link.mark(nc.vector.match_replace(rest, top[:, hd, p, 0:8], src, LOWEST))
            for hd, p, src, rest in rows:
                last = nc.vector.max_index(topi[:, hd, p, 0:8], top[:, hd, p, 0:8], src)
            last.then_inc(s_top, 1)
            link.wait()
            for hd, p, src, rest in rows:
                link.mark(nc.vector.max(top[:, hd, p, 8:16], rest))
            link.wait()
            for hd, p, src, rest in rows:
                link.mark(nc.vector.max_index(topi[:, hd, p, 8:16], top[:, hd, p, 8:16], rest))
            link.wait()

        def candidates(hs):
            link.mark(nc.vector.tensor_copy(key0[:, hs, :], topi[:, hs, 0, :]))
            link(nc.vector.scalar_tensor_tensor(key1[:, hs, :], topi[:, hs, 1, :], float(NK), headrow[:, hs, :],
                                                ALU.mult, ALU.add))
            at = 0
            for a, na, nb in PAIRS:
                shape = [P, hs.stop - hs.start, na, nb]
                for to, x, y in ((cand, top[:, hs, 0, a:a + na], top[:, hs, 1, 0:nb]),
                                 (candi, key0[:, hs, a:a + na], key1[:, hs, 0:nb])):
                    link.mark(nc.vector.tensor_tensor(to[:, hs, at:at + na * nb].rearrange("p h (a b) -> p h a b", a=na),
                                                      x.unsqueeze(3).to_broadcast(shape), y.unsqueeze(2).to_broadcast(shape),
                                                      ALU.add))
                at += na * nb
            link.wait()
            for few, at, n in FEW:
                link.mark(nc.vector.tensor_copy(candfew[:, hs, few:few + n], candi[:, hs, at:at + n]))
            link.wait()

        def choose(heads):
            for pair in range(heads.start, heads.stop, 2):
                two = [(pair + m, cleft[:, m, :]) for m in range(2)]
                for hd, rest in two:
                    link.mark(nc.vector.max(best[:, hd, 0:8], cand[:, hd, :]))
                link.wait()
                for hd, rest in two:
                    link.mark(nc.vector.match_replace(rest, best[:, hd, 0:8], cand[:, hd, :], LOWEST))
                    link.mark(nc.vector.max_index(spot[:, hd, 0:8], best[:, hd, 0:8], cand[:, hd, :]))
                link.wait()
                for hd, rest in two:
                    link.mark(nc.vector.max(best[:, hd, 8:16], rest))
                link.wait()
                for hd, rest in two:
                    link.mark(nc.vector.max_index(spot[:, hd, 8:16], best[:, hd, 8:16], rest))
                link.wait()

        def less_largest():
            nc.vector.tensor_tensor(bestd[:, :, :], best[:, :, :], best[:, :, 0:1].to_broadcast([P, HEADS, TOPK]),
                                    ALU.subtract).then_inc(s_diff, 1)
            link.wait()

        def normalise(t, k):
            dve.wait_ge(s_wexp, t + 1)
            link(nc.vector.tensor_reduce(bests[:, :], beste[:, :, :], AX.X, ALU.add))
            link(nc.vector.reciprocal(bests[:, :], bests[:, :]))
            link(nc.vector.tensor_tensor(mixw[k][:, :, :], beste[:, :, :], bcast(bests[:, :], 2, [P, HEADS, TOPK]), ALU.mult))

        def find_rows(t, k, half):
            hs = slice(half * HH, (half + 1) * HH)
            H8 = TOPK // 2
            parts = ((hitfew, 0, NFEW, placefew, candfew), (hit, H8, NC, place, candi))
            for hits, r, n, places, rows in parts:
                link.mark(nc.vector.tensor_tensor(hits[:, :, :, :], bcast(spot[:, hs, r:r + H8], 3, [P, HH, H8, n]),
                                                  places[:, :].unsqueeze(1).unsqueeze(1).to_broadcast([P, HH, H8, n]),
                                                  ALU.is_equal))
            link.wait()
            for hits, r, n, places, rows in parts:
                link.mark(nc.vector.tensor_tensor(hits[:, :, :, :], hits[:, :, :, :], bcast(rows[:, hs, :], 2, [P, HH, H8, n]),
                                                  ALU.mult))
            link.wait()
            for hits, r, n, places, rows in parts:
                last = nc.vector.tensor_reduce(row[k][:, hs, r:r + H8], hits[:, :, :, :], AX.X, ALU.max)
            last.then_inc(s_row, 1)
            dve.wait_ge(s_row, 2 * t + half + 1)

        def begin(t, step):
            if step < PIECES:
                halves(t, step)
            else:
                candidates(slice(0, HEADS))
                choose(range(0, HH))

        def finish(t, k, step):
            if step == 0:
                choose(range(HH, HEADS))
                less_largest()
            elif step == 1:
                normalise(t, k)
                find_rows(t, k, 0)
            else:
                find_rows(t, k, 1)

        def first():
            for half in range(2):
                halves(0, half)
                candidates(slice(half * HH, (half + 1) * HH))
                choose(range(half * HH, (half + 1) * HH))
                if half == 1:
                    less_largest()
                    normalise(0, 0)
                find_rows(0, 0, half)

        return begin, finish, first

    with ExitStack() as cc:
        block = cc.enter_context(nc.Block())

        @block.tensor
        def _(pe):
            for m in range(HEADS * 2):
                last = nc.tensor.matmul(S[0:D, m * NK:(m + 1) * NK], wd[:, m, :], kd[:, m, :], start=True, stop=True)
            last.then_inc(s_m, 1)
            pe.wait_ge(s_mc, 2)
            for piece in range(PIECES):
                similarities(pe, 0, piece, piece == 0)

        @block.scalar
        def _(act):
            nc.scalar.preload_act_table(ACT.Exp)
            stage_on(act, 0, 0)
            stage_ahead_on(act, 0)
            act.wait_ge(s_m, 1)
            nc.scalar.activation(msim[:, 0:CH], S[0:D, 0:CH], ACT.Copy).then_inc(s_mc, 1)
            weights_on(act, 0)

        @block.vector
        def _(dve):
            link = Link(dve, s_link)
            dve.wait_ge(s_m, 1)
            nc.vector.tensor_copy(msim[:, CH:2 * CH], S[0:D, CH:2 * CH]).then_inc(s_mc, 1)
            choosing(dve, link)[2]()
            link.restart()

    with ExitStack() as cc:
        relu_attention(cc, 1, *relu, beside=lambda pool: [gather(pool, 0, hd) for hd in range(RING)])

    def zeros(pool):
        for buf in (keys[:, :, :], vals[:, :, :, :]):
            nc.gpsimd.memset(buf, 0.0).then_inc(s_fill, 1)

    with ExitStack() as cc:
        norm_block("n5", cc, h[:, :, :], [None], fetch=zeros, sq=prob[0][:, :].rearrange("p (t d) -> p t d", d=D),
                   tp=tp, pairs=(1,))

    def side(hd):
        return slice(hd % 2 * D, hd % 2 * D + D)

    LASTJ = TILES // 2 - 1
    block = c.enter_context(nc.Block())

    def turns(eng, tile):
        tile(0, 0, True, 2)
        tile(0, 1, False, 2)
        with eng.Fori(1, LASTJ) as j:
            tile(j, 0, False, 2)
            tile(j, 1, False, 2)
        tile(LASTJ, 0, False, 1)
        tile(LASTJ, 1, False, 0)

    @block.gpsimd
    def _(pool):
        def tile(j, k, first, more):
            t = 2 * j + k
            for hd in range(RING if first else 0, HEADS):
                if hd % HH == 0:
                    hold(pool, s_started, s_row, 2 * t + hd // HH + 1)
                hold(pool, s_started, s_acc, t * HEADS + hd + 1 - RING + CREDIT)
                gather(pool, k, hd)
        turns(pool, tile)

    @block.sync
    def _(sp):
        def tile(j, k, first, more):
            t = 2 * j + k
            sp.wait_ge(s_res, t + 1)
            sp.dma_start(out[bass.ds(t, 1), :, :].rearrange("a p d -> p (a d)"),
                         h[:, bass.ds(t, 1), :].rearrange("p a d -> p (a d)")).then_inc(s_out, 16)
        turns(sp, tile)
        sp.wait_ge(s_out, 16 * TILES)

    @block.scalar
    def _(act):
        nc.scalar.preload_act_table(ACT.Exp)

        def stage(t, k):
            stage_on(act, t, k)

        def stage_ahead(t):
            stage_ahead_on(act, t)

        def weights(t):
            weights_on(act, t)

        def scale_rows(t, k, hd):
            act.wait_ge(s_gathered[hd % RING], 16 * TOPK * (t * (HEADS // RING) + hd // RING + 1))
            for m in range(TOPK):
                rows = rowbuf[hd % RING][:, m, :]
                last = nc.scalar.activation(rows, rows, ACT.Copy, scale=mixw[k][:, hd, m:m + 1])
            last.then_inc(s_scaled, 1)

        def exponentials(n, hd):
            act.wait_ge(s_max, n + 1)
            nc.scalar.activation(prob[hd % 2][:, :], S[:, :], ACT.Exp, bias=nmax[:, :], accum_out=rsum[:, :]
                                 ).then_inc(s_prob, 1)

        def attend(n, hd):
            for q in range(NCH):
                act.wait_ge(s_tp, NCH * n + q + 1)
                nc.scalar.activation(probT[:, q * CH:(q + 1) * CH], tp[q % 2][:, :], ACT.Copy).then_inc(s_tpc, 1)
            act.wait_ge(s_rinv, n + 1)
            act.wait_ge(s_o, n + 1)
            nc.scalar.activation(ob[:, hd * D:(hd + 1) * D], O, ACT.Copy, scale=rinv[:, :]).then_inc(s_ob, 1)

        def output(t):
            act.wait_ge(s_obt, t + 1)
            nc.scalar.activation(obT[:, :], tp[0][:, :], ACT.Copy).then_inc(s_obtc, 1)

        def tile(j, k, first, more):
            t = 2 * j + k
            tb = j % (BT // 2) * 2 + k
            for hd in range(HEADS):
                n = t * HEADS + hd
                if hd == 0 and more:
                    stage(t + 1, 1 - k)
                if not (first and hd == 0):
                    exponentials(n - 1, (hd - 1) % HEADS)
                if hd == 1 and more:
                    weights(t + 1)
                act.wait_ge(s_q, n + 1)
                nc.scalar.activation(qs[hd % 2][side(hd), :], Q, ACT.Copy, scale=float(D) ** -0.5).then_inc(s_qs, 1)
                act.wait_ge(s_acc, n + 1 + CREDIT)
                nc.scalar.activation(vals[:, bass.ds(tb, 1), hd, :].rearrange("p a d -> p (a d)"), acc[:, D:W], ACT.Copy)
                act.wait_ge(s_kt, n + 1)
                nc.scalar.activation(keys[side(hd), hd // 2, bass.ds(tb * P, P)], KT, ACT.Copy).then_inc(s_key, 1)
                if hd < HEADS - 1:
                    scale_rows(t, k, hd + 1)
                elif more:
                    scale_rows(t + 1, 1 - k, 0)
                if not (first and hd == 0):
                    attend(n - 1, (hd - 1) % HEADS)
                    if hd == 0:
                        output(t - 1)
                if hd == EARLY - 1 and more == 2:
                    stage_ahead(t + 2)

        stage_ahead(1)
        scale_rows(0, 0, 0)
        turns(act, tile)
        exponentials(TILES * HEADS - 1, HEADS - 1)
        attend(TILES * HEADS - 1, HEADS - 1)
        output(TILES - 1)

    @block.tensor
    def _(pe):
        def attend(n, hd):
            for q in range(NCH):
                if q >= 2:
                    pe.wait_ge(s_tpc, NCH * n + q - 1)
                for m in range(4):
                    last = nc.tensor.transpose(tp[q % 2][:, m * P:(m + 1) * P],
                                               prob[hd % 2][:, (4 * q + m) * P:(4 * q + m + 1) * P], ident[:, :])
                last.then_inc(s_tp, 1)
            for m in range(BT):
                if m % 4 == 0:
                    pe.wait_ge(s_tpc, NCH * n + m // 4 + 1)
                last = nc.tensor.matmul(O, probT[:, m * P:(m + 1) * P], vals[:, m, hd, :],
                                        start=(m == 0), stop=(m == BT - 1))
            last.then_inc(s_o, 1)

        def output(t):
            pe.wait_ge(s_ob, (t + 1) * HEADS)
            for m in range(4):
                last = nc.tensor.transpose(tp[0][:, m * P:(m + 1) * P], ob[:, m * P:(m + 1) * P], ident[:, :])
            last.then_inc(s_obt, 1)
            pe.wait_ge(s_obtc, t + 1)
            for m in range(4):
                last = nc.tensor.matmul(PR, obT[:, m * P:(m + 1) * P], wo[:, m, :], start=(m == 0), stop=(m == 3))
            last.then_inc(s_pr, 1)

        def tile(j, k, first, more):
            t = 2 * j + k
            tb = j % (BT // 2) * 2 + k
            for hd in range(HEADS):
                n = t * HEADS + hd
                if hd == 0:
                    hold(pe, s_started, s_xs, t + 1)
                if 0 <= hd - EARLY < PIECES and more == 2:
                    similarities(pe, t + 2, hd - EARLY, False)
                nc.tensor.matmul(Q, wq[:, hd * D:(hd + 1) * D], xs[k][:, :], start=True, stop=True).then_inc(s_q, 1)
                hold(pe, s_started, s_acc, n + 1 + CREDIT)
                nc.tensor.transpose(KT, acc[:, 0:D], ident[:, :]).then_inc(s_kt, 1)
                pe.wait_ge(s_qs, n + 1)
                pe.wait_ge(s_key, n + 1)
                if not (first and hd == 0):
                    pe.wait_ge(s_prob, n)
                for q in range(NCH):
                    nc.tensor.matmul(S[:, q * CH:(q + 1) * CH], qs[hd % 2][:, :], keys[:, hd // 2, q * CH:(q + 1) * CH],
                                     start=True, stop=False)
                    last = nc.tensor.matmul(S[:, q * CH:(q + 1) * CH], ident16[:, :],
                                            causal[:, bass.ds(REACH - tb * P + q * CH, CH)], start=False, stop=True)
                last.then_inc(s_scores, 1)
                if hd == 1 and not first:
                    pe.wait_ge(s_res, t)
                if not (first and hd == 0):
                    attend(n - 1, (hd - 1) % HEADS)
                    if hd == 0:
                        output(t - 1)

        for piece in range(PIECES):
            similarities(pe, 1, piece, False)
        turns(pe, tile)
        pe.wait_ge(s_prob, TILES * HEADS)
        attend(TILES * HEADS - 1, HEADS - 1)
        output(TILES - 1)

    @block.vector
    def _(dve):
        link = Link(dve, s_link)
        begin, finish, _ = choosing(dve, link)
        nc.vector.memset(rsum[:, :], 0.0).then_inc(s_acc, CREDIT)
        dve.wait_ge(s_acc, CREDIT)

        def mix(n, hd):
            dve.wait_ge(s_scaled, n + 1)
            nc.vector.tensor_reduce(acc[:, :], rowbuf[hd % RING][:, :, :].rearrange("p m w -> p w m"), AX.X,
                                    ALU.add).then_inc(s_acc, 1)

        def reciprocal(n):
            dve.wait_ge(s_prob, n + 1)
            nc.vector.reciprocal(rinv[:, :], rsum[:, :]).then_inc(s_rinv, 1)

        def output(t):
            dve.wait_ge(s_pr, t + 1)
            at = h[:, bass.ds(t, 1), :].rearrange("p a d -> p (a d)")
            nc.vector.tensor_tensor(at, PR, at, ALU.add).then_inc(s_res, 1)

        def tile(j, k, first, more):
            t = 2 * j + k
            for hd in range(HEADS):
                n = t * HEADS + hd
                if more or hd < HEADS - 1:
                    mix(n + 1, (hd + 1) % HEADS)
                if hd == 1 and not first:
                    output(t - 1)
                dve.wait_ge(s_scores, n + 1)
                nc.vector.tensor_reduce(nmax[:, :], S[:, :], AX.X, ALU.max, negate=True).then_inc(s_max, 1)
                if hd < LATE and more:
                    finish(t + 1, 1 - k, hd)
                if hd >= EARLY and more == 2:
                    begin(t + 2, hd - EARLY)
                reciprocal(n)
            link.restart()

        mix(0, 0)
        for step in range(STEPS):
            begin(1, step)
        link.restart()
        turns(dve, tile)
        output(TILES - 1)


def kernel(**inputs):
    import numpy as np
    import concourse.bacc as bacc
    from concourse.bass_utils import run_bass_kernel_spmd as run

    nc = bacc.Bacc("TRN2", target_bir_lowering=False, num_devices=1)
    a = {k: np.asarray(v) for k, v in inputs.items()}
    arrays = {
        "ids": a["x"].reshape(TILES, P).T,
        "ple": a["L0_tok_ple_table"].reshape(VOCAB * PLE // D, D),
        "qkv_b_cols": a["L0_attn_qkv_b"].reshape(3, D).T,
        "scale": a["L0_attn_scale"].reshape(1),
        "b1_cols": a["L0_ffn_b1"].reshape(2 * E, P).T,
        "L1_attn_wT": np.stack([a["L1_attn_W" + n].T for n in "qkvo"], axis=1),
        "pk_keysT": a["L1_ffn_pk_keys"].transpose(3, 2, 0, 1).reshape(32, 2 * HEADS, NK),
        "Wq_pkT": a["L1_ffn_Wq_pk"].reshape(D, 2, HEADS, 32).transpose(3, 2, 1, 0).reshape(32, 2 * HEADS, D),
        "memory": np.concatenate([a["L1_ffn_keys_table"], a["L1_ffn_values_table"]], axis=1),
    }
    for name in ("L0_attn_bias_table L0_attn_ln1_g L0_attn_ln1_b L0_attn_qkv_b L0_attn_qkv_w L0_attn_proj_w L0_attn_proj_b "
                 "L0_attn_ln2_g L0_attn_ln2_b L0_ffn_gate_w L0_ffn_gate_b L0_ffn_w1 L0_ffn_w2 L0_ffn_b2 L1_ffn_Wq "
                 "L1_ffn_Wo").split():
        arrays[name] = a[name]
    arrays = {k: np.ascontiguousarray(v) for k, v in arrays.items()}
    A = {k: nc.dram_tensor("in_" + k, v.shape, mybir.dt.from_np(v.dtype), kind="ExternalInput").ap()
         for k, v in arrays.items()}
    out = nc.dram_tensor("out", (TILES, P, D), F32, kind="ExternalOutput").ap()
    build(nc, A, out)
    r = run(nc, [{"in_" + k: v for k, v in arrays.items()}], core_ids=[0])
    return r.results[0]["out"].reshape(B, N, D)
```
